# Optimizing a Trainium2 kernel written in Bass

```python
import numpy as np
import jax
import jax.numpy as jnp

def _softmax(x, axis=-1):
    return jax.nn.softmax(x, axis=axis)

def _gelu(x):
    return jax.nn.gelu(x, approximate=True)

def _silu(x):
    return jax.nn.silu(x)

def _sigmoid(x):
    return jax.nn.sigmoid(x)

def _layernorm(x, axis=-1, eps=1e-05):
    m = jnp.mean(x, axis=axis, keepdims=True)
    v = jnp.var(x, axis=axis, keepdims=True)
    return (x - m) / jnp.sqrt(v + eps)

def _scatter_add(tgt, idx, src, axis=0):
    return tgt.at[idx].add(src)

def _segment_sum(src, seg, n):
    return jax.ops.segment_sum(src, seg, n)
kernel_name = 'mk_seq_preln_d2_jaxref_r8_110f9f'

def setup_inputs(seed: int=0):
    np.random.seed(seed)
    _w = jnp.asarray

    def _L0_attn_setup():
        import jax, jax.numpy as jnp
        import numpy as np
        import math
        B, S, D = (1, 256, 512)
        H, KV, HD = (32, 8, 128)
        GROUPS = H // KV
        SYS_LEN, IMG_LEN = (35, 72)
        ENH, SUP = (1.5, 0.5)
        ROPE_BASE = 10000.0

        def _rope_cos_sin(seq_len, dtype):
            inv_freq = 1.0 / ROPE_BASE ** (jnp.arange(0, HD, 2, dtype=jnp.float32) / HD)
            pos = jnp.arange(seq_len, dtype=jnp.float32)
            freqs = pos[:, None] * inv_freq[None, :]
            emb = jnp.concatenate([freqs, freqs], axis=-1)
            return (jnp.cos(emb).astype(dtype), jnp.sin(emb).astype(dtype))

        def _rotate_half(x):
            x1, x2 = (x[..., :HD // 2], x[..., HD // 2:])
            return jnp.concatenate([-x2, x1], axis=-1)
        key = jax.random.key(seed)
        ks = jax.random.split(key, 5)
        scale = 0.02
        return {'hidden_states': jax.random.normal(ks[0], (B, S, D), dtype=jnp.float32), 'wq': jax.random.normal(ks[1], (H * HD, D), dtype=jnp.float32) * scale, 'wk': jax.random.normal(ks[2], (KV * HD, D), dtype=jnp.float32) * scale, 'wv': jax.random.normal(ks[3], (KV * HD, D), dtype=jnp.float32) * scale, 'wo': jax.random.normal(ks[4], (D, H * HD), dtype=jnp.float32) * scale}
    _L0_attn_in = _L0_attn_setup()

    def _L0_ffn_setup():
        import jax, jax.numpy as jnp
        import numpy as np
        H, FF = (512, 1792)
        B, S = (4, 256)
        key = jax.random.key(seed)
        ks = jax.random.split(key, 7)
        x = jax.random.normal(ks[0], (B, S, H), dtype=jnp.float32)
        gate_t = jax.random.randint(ks[1], (FF, H), -1, 2, dtype=jnp.int32)
        up_t = jax.random.randint(ks[2], (FF, H), -1, 2, dtype=jnp.int32)
        down_t = jax.random.randint(ks[3], (H, FF), -1, 2, dtype=jnp.int32)
        gate_s = jax.random.uniform(ks[4], (FF,), jnp.float32, 0.01, 0.1)
        up_s = jax.random.uniform(ks[5], (FF,), jnp.float32, 0.01, 0.1)
        down_s = jax.random.uniform(ks[6], (H,), jnp.float32, 0.01, 0.1)
        return {'x': x, 'gate_t': gate_t, 'up_t': up_t, 'down_t': down_t, 'gate_s': gate_s, 'up_s': up_s, 'down_s': down_s}
    _L0_ffn_in = _L0_ffn_setup()

    def _L1_attn_setup():
        import math
        import jax, jax.numpy as jnp
        import numpy as np
        N_HEADS = 32
        ALIBI_BIAS_MAX = 8

        def _alibi_slopes(n_heads, alibi_bias_max=8):
            _n = 2 ** math.ceil(math.log2(n_heads))
            m = jnp.arange(1, _n + 1, dtype=jnp.float32) * (alibi_bias_max / _n)
            slopes = 1.0 / jnp.power(2.0, m)
            if _n != n_heads:
                slopes = jnp.concatenate([slopes[1::2], slopes[::2]])[:n_heads]
            return slopes
        key = jax.random.key(seed)
        k1, k2, k3 = jax.random.split(key, 3)
        B, S, D = (1, 256, 512)
        x = jax.random.normal(k1, (B, S, D), dtype=jnp.float32)
        w_qkv = jax.random.normal(k2, (3 * D, D), dtype=jnp.float32) * 0.02
        b_qkv = jnp.zeros((3 * D,), dtype=jnp.float32)
        w_out = jax.random.normal(k3, (D, D), dtype=jnp.float32) * 0.02
        b_out = jnp.zeros((D,), dtype=jnp.float32)
        return {'x': x, 'w_qkv': w_qkv, 'b_qkv': b_qkv, 'w_out': w_out, 'b_out': b_out}
    _L1_attn_in = _L1_attn_setup()

    def _L1_ffn_setup():
        import jax, jax.numpy as jnp
        import numpy as np
        BATCH, SEQ, D = (2, 256, 512)
        K, TOPK, RANK = (64, 16, 16)
        ALPHA = 32.0
        SCALING = ALPHA / RANK
        key = jax.random.key(seed)
        k1, k2, k3, k4 = jax.random.split(key, 4)
        x = jax.random.normal(k1, (BATCH, SEQ, D), dtype=jnp.float32)
        A = jax.random.normal(k2, (K, RANK, D), dtype=jnp.float32) * 0.02
        B = jax.random.normal(k3, (K, D, RANK), dtype=jnp.float32) * 0.02
        Wr = jax.random.normal(k4, (K, D), dtype=jnp.float32) * 0.02
        return {'x': x, 'A': A, 'B': B, 'Wr': Wr}
    _L1_ffn_in = _L1_ffn_setup()
    _d = {'L0_attn_hidden_states': _L0_attn_in['hidden_states'], 'L0_attn_wq': _L0_attn_in['wq'], 'L0_attn_wk': _L0_attn_in['wk'], 'L0_attn_wv': _L0_attn_in['wv'], 'L0_attn_wo': _L0_attn_in['wo'], 'L0_ffn_gate_t': _L0_ffn_in['gate_t'], 'L0_ffn_up_t': _L0_ffn_in['up_t'], 'L0_ffn_down_t': _L0_ffn_in['down_t'], 'L0_ffn_gate_s': _L0_ffn_in['gate_s'], 'L0_ffn_up_s': _L0_ffn_in['up_s'], 'L0_ffn_down_s': _L0_ffn_in['down_s'], 'L1_attn_w_qkv': _L1_attn_in['w_qkv'], 'L1_attn_b_qkv': _L1_attn_in['b_qkv'], 'L1_attn_w_out': _L1_attn_in['w_out'], 'L1_attn_b_out': _L1_attn_in['b_out'], 'L1_ffn_A': _L1_ffn_in['A'], 'L1_ffn_B': _L1_ffn_in['B'], 'L1_ffn_Wr': _L1_ffn_in['Wr']}
    _x0 = _d['L0_attn_hidden_states']
    _d['L0_attn_hidden_states'] = jax.random.normal(jax.random.fold_in(jax.random.key(seed), 1), (2, 512, 512), dtype=_x0.dtype)
    del _x0
    return _d

def reference(L0_attn_hidden_states, L0_attn_wq, L0_attn_wk, L0_attn_wv, L0_attn_wo, L0_ffn_gate_t, L0_ffn_up_t, L0_ffn_down_t, L0_ffn_gate_s, L0_ffn_up_s, L0_ffn_down_s, L1_attn_w_qkv, L1_attn_b_qkv, L1_attn_w_out, L1_attn_b_out, L1_ffn_A, L1_ffn_B, L1_ffn_Wr):

    def _L0_attn_ref(hidden_states, wq, wk, wv, wo):
        import jax, jax.numpy as jnp
        import numpy as np
        import math
        B, S, D = (1, 256, 512)
        H, KV, HD = (32, 8, 128)
        GROUPS = H // KV
        SYS_LEN, IMG_LEN = (35, 72)
        ENH, SUP = (1.5, 0.5)
        ROPE_BASE = 10000.0

        def _rope_cos_sin(seq_len, dtype):
            inv_freq = 1.0 / ROPE_BASE ** (jnp.arange(0, HD, 2, dtype=jnp.float32) / HD)
            pos = jnp.arange(seq_len, dtype=jnp.float32)
            freqs = pos[:, None] * inv_freq[None, :]
            emb = jnp.concatenate([freqs, freqs], axis=-1)
            return (jnp.cos(emb).astype(dtype), jnp.sin(emb).astype(dtype))

        def _rotate_half(x):
            x1, x2 = (x[..., :HD // 2], x[..., HD // 2:])
            return jnp.concatenate([-x2, x1], axis=-1)
        bsz, q_len, _ = hidden_states.shape
        dt = hidden_states.dtype
        q = (hidden_states @ wq.T).reshape(bsz, q_len, H, HD).transpose(0, 2, 1, 3)
        k = (hidden_states @ wk.T).reshape(bsz, q_len, KV, HD).transpose(0, 2, 1, 3)
        v = (hidden_states @ wv.T).reshape(bsz, q_len, KV, HD).transpose(0, 2, 1, 3)
        cos, sin = _rope_cos_sin(q_len, dt)
        q = q * cos + _rotate_half(q) * sin
        k = k * cos + _rotate_half(k) * sin
        k = jnp.repeat(k, GROUPS, axis=1)
        v = jnp.repeat(v, GROUPS, axis=1)
        scores = jnp.einsum('bhqd,bhkd->bhqk', q, k) / math.sqrt(HD)
        kpos = jnp.arange(q_len)
        key_scale = jnp.where(kpos < SYS_LEN, SUP, jnp.where(kpos < SYS_LEN + IMG_LEN, ENH, 1.0)).astype(dt)
        qpos = jnp.arange(q_len)
        row_sel = (qpos >= SYS_LEN + IMG_LEN)[:, None]
        scale = jnp.where(row_sel, key_scale[None, :], jnp.ones((), dt))
        scores = scores * scale
        causal = jnp.where(qpos[:, None] >= kpos[None, :], 0.0, jnp.finfo(jnp.float32).min)
        scores = scores + causal.astype(dt)
        probs = jax.nn.softmax(scores.astype(jnp.float32), axis=-1).astype(dt)
        attn = jnp.einsum('bhqk,bhkd->bhqd', probs, v)
        attn = attn.transpose(0, 2, 1, 3).reshape(bsz, q_len, H * HD)
        return attn @ wo.T

    def _L0_ffn_ref(x, gate_t, up_t, down_t, gate_s, up_s, down_s):
        import jax, jax.numpy as jnp
        import numpy as np
        H, FF = (512, 1792)
        B, S = (4, 256)
        Bb, Ss, Hh = x.shape
        x_flat = x.reshape(Bb * Ss, Hh)
        gate_w = gate_t.astype(jnp.float32) * gate_s[:, None]
        up_w = up_t.astype(jnp.float32) * up_s[:, None]
        down_w = down_t.astype(jnp.float32) * down_s[:, None]
        gate_out = x_flat @ gate_w.T
        up_out = x_flat @ up_w.T
        hidden = jax.nn.silu(gate_out) * up_out
        out_flat = hidden @ down_w.T
        return out_flat.reshape(Bb, Ss, -1)

    def _L1_attn_ref(x, w_qkv, b_qkv, w_out, b_out):
        import math
        import jax, jax.numpy as jnp
        import numpy as np
        N_HEADS = 32
        ALIBI_BIAS_MAX = 8

        def _alibi_slopes(n_heads, alibi_bias_max=8):
            _n = 2 ** math.ceil(math.log2(n_heads))
            m = jnp.arange(1, _n + 1, dtype=jnp.float32) * (alibi_bias_max / _n)
            slopes = 1.0 / jnp.power(2.0, m)
            if _n != n_heads:
                slopes = jnp.concatenate([slopes[1::2], slopes[::2]])[:n_heads]
            return slopes
        B, S, D = x.shape
        H = N_HEADS
        hd = D // H
        qkv = jnp.einsum('bsd,od->bso', x, w_qkv) + b_qkv
        q, k, v = jnp.split(qkv, 3, axis=-1)
        q = q.reshape(B, S, H, hd)
        k = k.reshape(B, S, H, hd)
        v = v.reshape(B, S, H, hd)
        scale = 1.0 / math.sqrt(hd)
        scores = jnp.einsum('bqhd,bkhd->bhqk', q, k) * scale
        slopes = _alibi_slopes(H, ALIBI_BIAS_MAX)
        positions = jnp.arange(1 - S, 1, dtype=jnp.float32)
        alibi = slopes[:, None] * positions[None, :]
        scores = scores + alibi[None, :, None, :]
        causal = jnp.arange(S)[:, None] >= jnp.arange(S)[None, :]
        scores = jnp.where(causal[None, None, :, :], scores, jnp.float32(-1000000000.0))
        attn = jax.nn.softmax(scores, axis=-1)
        out = jnp.einsum('bhqk,bkhd->bqhd', attn, v).reshape(B, S, D)
        return jnp.einsum('bsd,od->bso', out, w_out) + b_out

    def _L1_ffn_ref(x, A, B, Wr):
        import jax, jax.numpy as jnp
        import numpy as np
        BATCH, SEQ, D = (2, 256, 512)
        K, TOPK, RANK = (64, 16, 16)
        ALPHA = 32.0
        SCALING = ALPHA / RANK
        prefix = x.shape[:-1]
        xf = x.reshape(-1, x.shape[-1])
        N = xf.shape[0]
        scores = xf @ Wr.T
        top_vals, top_idx = jax.lax.top_k(scores, TOPK)
        gates = jax.nn.softmax(top_vals, axis=-1)
        G = jnp.zeros((N, K), xf.dtype).at[jnp.arange(N)[:, None], top_idx].set(gates)
        h = jnp.einsum('nd,krd->nkr', xf, A)
        out = jnp.einsum('nkr,kdr->nd', h * G[:, :, None], B)
        return (out * SCALING).reshape(*prefix, -1)
    x = L0_attn_hidden_states
    x = x + _L0_attn_ref(_layernorm(x, axis=-1), L0_attn_wq, L0_attn_wk, L0_attn_wv, L0_attn_wo)
    x = x + _L0_ffn_ref(_layernorm(x, axis=-1), L0_ffn_gate_t, L0_ffn_up_t, L0_ffn_down_t, L0_ffn_gate_s, L0_ffn_up_s, L0_ffn_down_s)
    x = x + _L1_attn_ref(_layernorm(x, axis=-1), L1_attn_w_qkv, L1_attn_b_qkv, L1_attn_w_out, L1_attn_b_out)
    x = x + _L1_ffn_ref(_layernorm(x, axis=-1), L1_ffn_A, L1_ffn_B, L1_ffn_Wr)
    return x

_drawn_inputs = setup_inputs


def setup_inputs(seed=0):
    import zlib

    import numpy as np

    out = dict(_drawn_inputs(seed))
    spreads = {'L1_attn_b_qkv': (0.0, 0.338), 'L1_attn_b_out': (0.0, 0.1)}
    factors = {'L0_attn_wq': 3.108,
     'L0_attn_wk': 3.041,
     'L1_ffn_A': 5.788,
     'L1_ffn_B': 5.621,
     'L1_ffn_Wr': 6.425}
    for name, (base, spread) in spreads.items():
        noise = np.random.default_rng([zlib.crc32(name.encode()), seed]).standard_normal(out[name].shape)
        drawn = base * np.exp(spread * noise) if base else spread * noise
        out[name] = jnp.asarray(drawn.astype(out[name].dtype))
    for name, factor in factors.items():
        out[name] = (out[name] * factor).astype(out[name].dtype)
    return out
```

```python
from contextlib import ExitStack

import numpy as np

import concourse.bass as bass
from concourse import mybir

P = 128
F32 = mybir.dt.float32
F32R = mybir.dt.float32r
I32 = mybir.dt.int32
ALU = mybir.AluOpType
ACT = mybir.ActivationFunctionType

BATCH, SEQ, D = 2, 512, 512
TOK = BATCH * SEQ
NT = TOK // P
DC = D // P
QT = SEQ // P
HEADS0, KV0, HD0 = 32, 8, 128
PER_KV = HEADS0 // KV0
FF = 1792
FC = FF // P
HEADS1, HD1 = 32, 16
EXPERTS, TOPK, RANK = 64, 16, 16
KR = EXPERTS * RANK
EPS = 1e-5
SYS_LEN, IMG_LEN = 35, 72
MASKED = -1.0e30
LOWEST = -3.0e38

SCORE_AT = [P * i * (i + 1) // 2 for i in range(QT + 1)]


class Model:

    def __init__(self, dram, x, ident, xT_hi, xT_lo, ln_loaded, ln_semaphores):
        self.dram, self.x, self.ident = dram, x, ident
        self.xT_hi, self.xT_lo = xT_hi, xT_lo
        self.ln_loaded, self.ln_semaphores = ln_loaded, ln_semaphores


def wait(engine, semaphore, value):
    if isinstance(value, int) and value <= 0:
        return
    engine.wait_ge(semaphore, value)


def product(nc, out, left, right, start, stop):
    nc.tensor.matmul(out, left[0], right[0], start=start, stop=False)
    nc.tensor.matmul(out, left[0], right[1], start=False, stop=False)
    return nc.tensor.matmul(out, left[1], right[0], start=False, stop=stop)


LN_SEMAPHORES = ("consts_in", "stats_done", "moments_done", "var_done", "root_done", "inverse_done", "normal_done",
                 "turned_done", "hi_done", "lo_done")


def layernorm_phase(nc, m, number, load=None):
    name, before, tiles_before = f"ln{number}", number, number * NT
    loaded, sems = m.ln_loaded, m.ln_semaphores
    with ExitStack() as ctx:
        stats = ctx.enter_context(nc.sbuf_tensor(f"{name}_stats", [P, NT, 6], F32))
        moments = ctx.enter_context(nc.sbuf_tensor(f"{name}_moments", [P, NT, 2], F32))
        shifted = ctx.enter_context(nc.sbuf_tensor(f"{name}_shifted", [P, NT], F32))
        deviation = ctx.enter_context(nc.sbuf_tensor(f"{name}_deviation", [P, NT], F32))
        inverse = ctx.enter_context(nc.sbuf_tensor(f"{name}_inverse", [P, NT], F32))
        normal = ctx.enter_context(nc.sbuf_tensor(f"{name}_normal", [P, 2, D], F32))
        turned = ctx.enter_context(nc.psum_tensor(f"{name}_turned", [P, 2, DC, P], F32))

        consts_in, stats_done, moments_done, var_done, root_done, inverse_done, normal_done, turned_done, hi_done, lo_done = sems
        block = ctx.enter_context(nc.Block())

        if load is not None:
            @block.sync
            def _(sp):
                for t in range(NT):
                    sp.dma_start(m.x[:, t, :], load[t * P:(t + 1) * P, :]).then_inc(loaded[t], 16)
                sp.dma_start(m.ident[:], m.dram["ident"]).then_inc(consts_in, 16)

        @block.vector
        def _(dve):
            for t in range(NT):
                if load is not None:
                    dve.wait_ge(loaded[t], 16)
                nc.vector.bn_stats(stats[:, t, :], m.x[:, t, :]).then_inc(stats_done, 1)
            for t in range(NT):
                dve.wait_ge(stats_done, tiles_before + t + 1)
                nc.vector.bn_aggr(moments[:, t, :], stats[:, t, :]).then_inc(moments_done, 1)
            dve.wait_ge(moments_done, tiles_before + NT)
            nc.vector.tensor_scalar(shifted[:], moments[:, :, 1], EPS, None, ALU.add).then_inc(var_done, 1)
            dve.wait_ge(root_done, before + 1)
            nc.vector.reciprocal(inverse[:], deviation[:]).then_inc(inverse_done, 1)
            dve.wait_ge(inverse_done, before + 1)

            def normalise(t):
                if t >= 2:
                    dve.wait_ge(turned_done, tiles_before + t - 1)
                nc.vector.tensor_scalar(normal[:, t % 2, :], m.x[:, t, :], moments[:, t, 0:1], inverse[:, t:t + 1],
                                        ALU.subtract, ALU.mult).then_inc(normal_done, 1)

            normalise(0)
            for t in range(NT):
                if t + 1 < NT:
                    normalise(t + 1)
                dve.wait_ge(hi_done, tiles_before + t + 1)
                nc.vector.tensor_tensor(m.xT_lo[:, :, t * P:(t + 1) * P], turned[:, t % 2],
                                        m.xT_hi[:, :, t * P:(t + 1) * P].bitcast(F32), ALU.subtract).then_inc(lo_done, 1)

        @block.scalar
        def _(act):
            act.wait_ge(var_done, before + 1)
            nc.scalar.activation(deviation[:], shifted[:], ACT.Sqrt).then_inc(root_done, 1)
            for t in range(NT):
                act.wait_ge(turned_done, tiles_before + t + 1)
                nc.scalar.copy(m.xT_hi[:, :, t * P:(t + 1) * P], turned[:, t % 2]).then_inc(hi_done, 1)

        @block.tensor
        def _(pe):
            if load is not None:
                pe.wait_ge(consts_in, 16)
            for t in range(NT):
                pe.wait_ge(normal_done, tiles_before + t + 1)
                if t >= 2:
                    pe.wait_ge(lo_done, tiles_before + t - 1)
                for c in range(DC):
                    last = nc.tensor.transpose(turned[:, t % 2, c], normal[:, t % 2, c * P:(c + 1) * P], m.ident[:])
                last.then_inc(turned_done, 1)


GROUP = 2 * PER_KV
UNITS = KV0 * GROUP
SIDE = {0: "out", 1: "out", 2: "keys", 3: "values", 4: "out", 5: "out", 6: "keys", 7: "values"}

PIECES = [("wo", 0, 2), ("wo", 1, 2), ("wq", 0, 2), ("wo", 2, 3), ("wo", 3, 3), ("wk", 0, 3),
          ("wq", 1, 4), ("wv", 0, 4), ("wq", 2, 5), ("wq", 3, 6)]
FIRST_PIECES = [("wq", 0), ("wk", 0), ("wq", 1), ("wv", 0), ("wq", 2), ("wq", 3)]
SLOTS = 5
PROJECTIONS = [(s, what) for s in range(GROUP) for what in
               ([SIDE[s]] if SIDE[s] != "out" else []) + ["query"]]
ROTATIONS = [x for x in PROJECTIONS if x[1] != "values"]
OUTPUTS = [x for s in range(GROUP) for x in
           ([(s, "out", 0), (s, "out", 1)] if SIDE[s] == "out" else []) + [(s, "attend", 0)]]


def attention0_phase(nc, m):
    dram = m.dram
    with ExitStack() as ctx:
        def sb(what, shape, dt=F32):
            return ctx.enter_context(nc.sbuf_tensor(f"a0_{what}", shape, dt))

        def pair(what, shape):
            return sb(f"{what}_hi", shape, F32R), sb(f"{what}_lo", shape, F32R)

        def sem(what):
            return ctx.enter_context(nc.semaphore(f"a0_{what}"))

        raw = sb("raw", [P, SLOTS, 512])
        zeros = sb("zeros", [P, 512])
        wq = pair("wq", [P, PER_KV, DC, HD0])
        wk = pair("wk", [P, DC, HD0])
        wv = pair("wv", [P, DC, HD0])
        wo = pair("wo", [P, PER_KV, D])
        keys = pair("keys", [P, BATCH, SEQ])
        values = pair("values", [P, BATCH, QT, HD0])
        query = pair("query", [P, 4, SEQ])
        cos_q, sin_q = sb("cos_q", [P, SEQ]), sb("sin_q", [P, SEQ])
        cos_k, sin_k = sb("cos_k", [P, SEQ]), sb("sin_k", [P, SEQ])
        causal = sb("causal", [P, SEQ])
        unscale = sb("unscale", [P, P])
        by_cos, by_sin, rotated = sb("by_cos", [P, SEQ]), sb("by_sin", [P, SEQ]), sb("rotated", [P, SEQ])
        first_tile = sb("first_tile", [P, P])
        probs = sb("probs", [P, 2, SCORE_AT[QT]])
        least = sb("least", [P, 2, QT])
        total = sb("total", [P, 2, QT])
        inverse = sb("inverse", [P, 2, QT])
        probsT = pair("probsT", [P, 2, SEQ])
        attended = pair("attended", [P, BATCH, PER_KV, SEQ])

        ps_proj = ctx.enter_context(nc.psum_tensor("a0_ps_proj", [P, 2, 512], F32))
        ps_score = ctx.enter_context(nc.psum_tensor("a0_ps_score", [P, 2, 512], F32))
        ps_turn = ctx.enter_context(nc.psum_tensor("a0_ps_turn", [P, 2, 512], F32))
        ps_out = ctx.enter_context(nc.psum_tensor("a0_ps_out", [P, 2, 512], F32))

        raw_in = [sem(f"raw_in{s}") for s in range(SLOTS)]
        consts_in, zeros_set, wait_passed = sem("consts_in"), sem("zeros_set"), sem("wait_passed")
        piece_hi, piece_split = sem("piece_hi"), sem("piece_split")
        query_made, keys_made, values_made = sem("query_made"), sem("keys_made"), sem("values_made")
        rotation_scaled, rotation_added = sem("rotation_scaled"), sem("rotation_added")
        rotation_hi, rotation_split = sem("rotation_hi"), sem("rotation_split")
        values_hi, values_split = sem("values_hi"), sem("values_split")
        score_made, first_scaled, score_masked = sem("score_made"), sem("first_scaled"), sem("score_masked")
        exp_done, total_inverted, probs_ready = sem("exp_done"), sem("total_inverted"), sem("probs_ready")
        turned, turned_hi, turned_split = sem("turned"), sem("turned_hi"), sem("turned_split")
        attend_made, attended_hi, attended_split = sem("attend_made"), sem("attended_hi"), sem("attended_split")
        out_made, out_added = sem("out_made"), sem("out_added")

        def rotation(g, s, what):
            return 10 * g + 4 + ROTATIONS.index((s, what)) + 1

        def query_rotation(g, u):
            return rotation(g, u - 3, "query") if u >= 3 else rotation(g - 1, u + 5, "query")

        def values_count(g, s):
            return 2 * g + (2 if s == 3 else 3)

        def out_count(g, s, half):
            return 8 * g + (2 * s - 4 if s < 2 else 2 * (s - 4)) + half + 1

        def piece_count(g, what, which):
            names = [x[:2] for x in PIECES]
            return len(FIRST_PIECES) + len(PIECES) * g + names.index((what, which)) + 1

        def present(g, s, what):
            if not isinstance(g, int):
                return True
            if what == "query":
                return 0 <= GROUP * g + s + 3 < UNITS
            if what in ("keys", "values"):
                return (g >= 0 if s < 4 else g < KV0 - 1) and g < KV0
            if what == "score":
                return 0 <= GROUP * g + s + 1 < UNITS
            if what == "attend":
                return 0 <= g < KV0
            return (1 <= g if s < 2 else 0 <= g < KV0)

        def projection_bank(g, s, what):
            return PROJECTIONS.index((s, what)) % 2

        def wait_projection_bank(pe, g, s, what):
            at = PROJECTIONS.index((s, what)) - 2
            gb = g if at >= 0 else g - 1
            sb_, before = PROJECTIONS[at]
            if isinstance(gb, int) and (gb < -1 or (gb == -1 and sb_ < 5)):
                return
            if before == "values":
                wait(pe, values_split, values_count(gb, sb_))
            else:
                wait(pe, rotation_scaled, rotation(gb, sb_, before))

        def wait_output_bank(pe, g, s, what, half):
            at = OUTPUTS.index((s, what, half)) - 2
            gb = g
            while True:
                if at < 0:
                    at, gb = at + len(OUTPUTS), gb - 1
                sb_, before, hb = OUTPUTS[at]
                if isinstance(gb, int) and gb < 0:
                    return
                if present(gb, sb_, before):
                    break
                at -= 2
            if before == "out":
                wait(pe, out_added, out_count(gb, sb_, hb))
            else:
                wait(pe, attended_split, GROUP * gb + sb_ + 1)

        block = ctx.enter_context(nc.Block())

        @block.sync
        def _(sp):
            for table, what in ((cos_q, "cos_q"), (sin_q, "sin_q"), (cos_k, "cos_k"), (sin_k, "sin_k"),
                                (causal, "causal"), (unscale, "unscale")):
                sp.dma_start(table[:], dram[what]).then_inc(consts_in, 16)

            def fetch(number, what, which, g):
                slot = number % SLOTS
                src = dram[what][g, which] if what in ("wq", "wo") else dram[what][g]
                sp.dma_start(raw[:, slot, :], src).then_inc(raw_in[slot], 16)

            for c, (what, which) in enumerate(FIRST_PIECES):
                wait(sp, piece_split, c - SLOTS + 1)
                fetch(c, what, which, 0)

            def group(g, last):
                for c, (what, which, _) in enumerate(PIECES):
                    if last and what != "wo":
                        continue
                    number = len(FIRST_PIECES) + c
                    done = len([x for x in PIECES[:c] if x[0] == "wo"]) if last else c
                    if last:
                        wait(sp, piece_split, len(FIRST_PIECES) + len(PIECES) * g + done)
                    else:
                        wait(sp, piece_split, len(PIECES) * g + number - SLOTS + 1)
                    fetch(number, what, which, g if what == "wo" else g + 1)

            with sp.Fori(0, KV0 - 1) as g:
                group(g, False)
            group(KV0 - 1, True)

        @block.gpsimd
        def _(pool):
            nc.gpsimd.memset(zeros[:], 0.0).then_inc(zeros_set, 1)
            pool.wait_ge(zeros_set, 1)
            targets = {"wq": wq, "wk": wk, "wv": wv, "wo": wo}

            def split(number, count, landed, what, which):
                slot = number % SLOTS
                hi, lo = targets[what]
                if what in ("wq", "wo"):
                    hi, lo = hi[:, which], lo[:, which]
                if what == "wo":
                    src = raw[:, slot, :]
                else:
                    src = raw[:, slot, :].rearrange("p (c n) -> p c n", c=DC)
                    if what in ("wk", "wv"):
                        hi, lo = hi[:], lo[:]
                pool.wait_ge(raw_in[slot], 16 * landed)
                zero = zeros[:] if what == "wo" else zeros[:].rearrange("p (c n) -> p c n", c=DC)
                nc.gpsimd.tensor_tensor(hi, src, zero, ALU.add).then_inc(piece_hi, 1)
                pool.wait_ge(piece_hi, count + 1)
                nc.gpsimd.tensor_tensor(lo, src, hi.bitcast(F32), ALU.subtract).then_inc(piece_split, 1)

            def add_rotation(count):
                pool.wait_ge(rotation_scaled, count)
                wait(pool, rotation_split, count - 1)
                nc.gpsimd.tensor_tensor(rotated[:], by_cos[:], by_sin[:], ALU.add).then_inc(rotation_added, 1)

            def free_for(g, what, which):
                if what == "wo":
                    wait(pool, out_made, out_count(g, 1, 1))
                elif what == "wk":
                    wait(pool, keys_made, 2 * g + 2)
                elif what == "wv":
                    wait(pool, values_made, 2 * g + 2)
                else:
                    wait(pool, query_made, GROUP * g + PER_KV + which + 1)

            for c, (what, which) in enumerate(FIRST_PIECES[:3]):
                split(c, c, 1, what, which)
            add_rotation(rotation(-1, 5, "query"))
            for c in (3, 4):
                split(c, c, 1, *FIRST_PIECES[c])
            add_rotation(rotation(-1, 6, "keys"))
            add_rotation(rotation(-1, 6, "query"))
            split(5, 5, 2, *FIRST_PIECES[5])
            add_rotation(rotation(-1, 7, "query"))

            def group(g, last):
                for s in range(GROUP):
                    for what in ("keys", "query"):
                        if (s, what) in ROTATIONS and present(g, s, what):
                            add_rotation(rotation(g, s, what))
                    for c, (what, which, step) in enumerate(PIECES):
                        if step != s or (last and what != "wo"):
                            continue
                        number = len(FIRST_PIECES) + c
                        slot = number % SLOTS
                        before = (2 if slot == 0 else 1) + len([x for x in range(c) if (len(FIRST_PIECES) + x) % SLOTS == slot])
                        if last:
                            done = len([x for x in PIECES[:c] if x[0] == "wo"])
                            before = (2 if slot == 0 else 1) + len(
                                [x for x in range(c) if (len(FIRST_PIECES) + x) % SLOTS == slot and PIECES[x][0] == "wo"])
                        else:
                            done = c
                        free_for(g, what, which)
                        split(number, len(FIRST_PIECES) + len(PIECES) * g + done, 2 * g + before + 1, what, which)

            group(0, False)
            with pool.Fori(1, KV0 - 1) as g:
                group(g, False)
            group(KV0 - 1, True)

        @block.tensor
        def _(pe):
            def xT(part, c, at, size):
                return part[:, c, at:at + size]

            def make_query(g, s, chunks):
                u = (s + 3) % GROUP
                b, j = u // PER_KV, u % PER_KV
                bank = projection_bank(g, s, "query")
                gq = g if s + 3 < GROUP else g + 1
                if chunks[0] == 0:
                    wait_projection_bank(pe, g, s, "query")
                    wait(pe, piece_split, weights_ready("wq", j, gq))
                for c in chunks:
                    last = product(nc, ps_proj[:, bank, :], (wq[0][:, j, c, :], wq[1][:, j, c, :]),
                                   (xT(m.xT_hi, c, b * SEQ, SEQ), xT(m.xT_lo, c, b * SEQ, SEQ)), c == 0, c == DC - 1)
                if chunks[-1] == DC - 1:
                    last.then_inc(query_made, 1)

            def weights_ready(what, which, g):
                if isinstance(g, int) and g == 0 and what != "wo":
                    return FIRST_PIECES.index((what, which)) + 1
                if what == "wo":
                    if isinstance(g, int) and g == KV0 - 1:
                        return len(FIRST_PIECES) + len(PIECES) * g + which + 1
                    return piece_count(g, what, which)
                return piece_count(g - 1, what, which)

            def make_keys(g, s):
                b = 1 if s < 4 else 0
                bank = projection_bank(g, s, "keys")
                wait_projection_bank(pe, g, s, "keys")
                wait(pe, piece_split, weights_ready("wk", 0, g if b else g + 1))
                for c in range(DC):
                    last = product(nc, ps_proj[:, bank, :], (wk[0][:, c, :], wk[1][:, c, :]),
                                   (xT(m.xT_hi, c, b * SEQ, SEQ), xT(m.xT_lo, c, b * SEQ, SEQ)), c == 0, c == DC - 1)
                last.then_inc(keys_made, 1)

            def make_values(g, s):
                b = 1 if s < 4 else 0
                bank = projection_bank(g, s, "values")
                wait_projection_bank(pe, g, s, "values")
                wait(pe, piece_split, weights_ready("wv", 0, g if b else g + 1))
                for t in range(QT):
                    for c in range(DC):
                        at = b * SEQ + t * P
                        last = product(nc, ps_proj[:, bank, t * P:(t + 1) * P],
                                       (xT(m.xT_hi, c, at, P), xT(m.xT_lo, c, at, P)),
                                       (wv[0][:, c, :], wv[1][:, c, :]), c == 0, c == DC - 1)
                last.then_inc(values_made, 1)

            def score(g, s, i):
                u = (s + 1) % GROUP
                gu = g if s + 1 < GROUP else g + 1
                n = GROUP * gu + u
                b = u // PER_KV
                if i == 0:
                    wait(pe, rotation_split, query_rotation(gu, u))
                    if u == 0:
                        wait(pe, rotation_split, rotation(gu - 1, 6, "keys"))
                    elif u == PER_KV:
                        wait(pe, rotation_split, rotation(gu, 2, "keys"))
                wait(pe, score_masked, 4 * n + i - 1)
                q = (query[0][:, u % 4, i * P:(i + 1) * P], query[1][:, u % 4, i * P:(i + 1) * P])
                k = (keys[0][:, b, 0:P * (i + 1)], keys[1][:, b, 0:P * (i + 1)])
                product(nc, ps_score[:, i % 2, 0:P * (i + 1)], q, k, True, True).then_inc(score_made, 1)

            def turn(n, u, t):
                if t == 0:
                    wait(pe, probs_ready, 4 * n + 4)
                wait(pe, turned_split, 4 * n + t - 1)
                for i in range(t, QT):
                    at = SCORE_AT[i] + t * P
                    last = nc.tensor.transpose(ps_turn[:, t % 2, (i - t) * P:(i - t + 1) * P],
                                               probs[:, u % 2, at:at + P], m.ident[:])
                last.then_inc(turned, 1)

            def attend(g, u, t):
                n = GROUP * g + u
                b = u // PER_KV
                bank = OUTPUTS.index((u, "attend", 0)) % 2
                if t == 0:
                    wait_output_bank(pe, g, u, "attend", 0)
                    if u % PER_KV == 0:
                        wait(pe, values_split, 2 * g + b + 1)
                wait(pe, turned_split, 4 * n + t + 1)
                w = SEQ - t * P
                product(nc, ps_out[:, bank, t * P:SEQ], (values[0][:, b, t, :], values[1][:, b, t, :]),
                        (probsT[0][:, t % 2, 0:w], probsT[1][:, t % 2, 0:w]), t == 0, t == QT - 1).then_inc(attend_made, 1)

            def make_out(g, s, half):
                b = 1 if s < 2 else 0
                t = 2 * (s % 4) + half
                bank = OUTPUTS.index((s, "out", half)) % 2
                gw = g - 1 if b else g
                wait_output_bank(pe, g, s, "out", half)
                if half == 0 and s in (0, 4):
                    wait(pe, attended_split, GROUP * gw + PER_KV * (b + 1))
                    wait(pe, piece_split, weights_ready("wo", PER_KV - 1, gw))
                for j in range(PER_KV):
                    at = slice(t * P, (t + 1) * P)
                    last = product(nc, ps_out[:, bank, :], (attended[0][:, b, j, at], attended[1][:, b, j, at]),
                                   (wo[0][:, j, :], wo[1][:, j, :]), j == 0, j == PER_KV - 1)
                last.then_inc(out_made, 1)

            def step(g, s):
                n = GROUP * g + s
                if present(g, s, "score"):
                    score(g, s, 0)
                    score(g, s, 1)
                if present(g, s, "attend"):
                    turn(n, s, 0)
                    turn(n, s, 1)
                if present(g, s, SIDE[s]):
                    if SIDE[s] == "out":
                        make_out(g, s, 0)
                        make_out(g, s, 1)
                    elif SIDE[s] == "keys":
                        make_keys(g, s)
                    else:
                        make_values(g, s)
                if present(g, s, "score"):
                    score(g, s, 2)
                    score(g, s, 3)
                if present(g, s, "query"):
                    make_query(g, s, [0, 1])
                if present(g, s, "attend"):
                    attend(g, s, 0)
                    turn(n, s, 2)
                    attend(g, s, 1)
                    turn(n, s, 3)
                if present(g, s, "query"):
                    make_query(g, s, [2, 3])
                if present(g, s, "attend"):
                    attend(g, s, 2)
                    attend(g, s, 3)

            for s in (5, 6, 7):
                step(-1, s)
            for s in range(GROUP):
                step(0, s)
            with pe.Fori(1, KV0 - 1) as g:
                for s in range(GROUP):
                    step(g, s)
            for s in range(GROUP):
                step(KV0 - 1, s)
            for s in (0, 1):
                step(KV0, s)

        @block.vector
        def _(dve):
            half = P // 2
            dve.wait_ge(consts_in, 16 * 6)

            def mask(g, s, i):
                n = GROUP * g + s + 1
                slot = (s + 1) % 2
                at, w = SCORE_AT[i], P * (i + 1)
                dve.wait_ge(score_made, 4 * n + i + 1)
                if i > 0:
                    dve.sem_inc(wait_passed, 1)
                src = ps_score[:, i % 2, 0:w]
                if i == 0:
                    wait(dve, turned, 4 * (n - 1))
                    nc.vector.tensor_tensor(first_tile[:], src, unscale[:], ALU.mult).then_inc(first_scaled, 1)
                    dve.wait_ge(first_scaled, n + 1)
                    dve.sem_inc(wait_passed, 1)
                    src = first_tile[:]
                nc.vector.tensor_tensor_reduce(
                    out=probs[:, slot, at:at + w], in0=src, in1=causal[:, SEQ - w:SEQ], scale=-float(HD0) ** -0.5,
                    scalar=-LOWEST, op0=ALU.add, op1=ALU.min, accum_out=least[:, slot, i:i + 1]).then_inc(score_masked, 1)

            def split_turned(g, s, t):
                n = GROUP * g + s
                w = SEQ - t * P
                dve.wait_ge(turned_hi, 4 * n + t + 1)
                nc.vector.tensor_tensor(probsT[1][:, t % 2, 0:w], ps_turn[:, t % 2, 0:w],
                                        probsT[0][:, t % 2, 0:w].bitcast(F32), ALU.subtract).then_inc(turned_split, 1)

            def rotate(g, s, what):
                bank = projection_bank(g, s, what)
                src = ps_proj[:, bank, :]
                cos, sin = (cos_q, sin_q) if what == "query" else (cos_k, sin_k)
                if what == "query":
                    dve.wait_ge(query_made, GROUP * g + s + 4)
                else:
                    dve.wait_ge(keys_made, 2 * g + (2 if s == 2 else 3))
                wait(dve, rotation_added, rotation(g, s, what) - 1)
                nc.vector.tensor_tensor(by_cos[:], src, cos[:], ALU.mult)
                nc.vector.tensor_tensor(by_sin[0:half], src[half:P], sin[half:P], ALU.mult)
                nc.vector.tensor_tensor(by_sin[half:P], src[0:half], sin[0:half], ALU.mult).then_inc(rotation_scaled, 1)

            def split_rotated(g, s, what):
                dve.wait_ge(rotation_hi, rotation(g, s, what))
                if what == "query":
                    hi, lo = query[0][:, (s + 3) % 4, :], query[1][:, (s + 3) % 4, :]
                else:
                    b = 1 if s < 4 else 0
                    hi, lo = keys[0][:, b, :], keys[1][:, b, :]
                nc.vector.tensor_tensor(lo, rotated[:], hi.bitcast(F32), ALU.subtract).then_inc(rotation_split, 1)

            def step(g, s):
                n = GROUP * g + s
                if present(g, s, "score"):
                    mask(g, s, 0)
                    mask(g, s, 1)
                if present(g, s, "attend"):
                    split_turned(g, s, 0)
                    split_turned(g, s, 1)
                side = SIDE[s] if present(g, s, SIDE[s]) else None
                if side == "out":
                    b = 1 if s < 2 else 0
                    for h in range(2):
                        t = b * QT + 2 * (s % 4) + h
                        count = out_count(g, s, h)
                        dve.wait_ge(out_made, count)
                        wait(dve, out_added, count - QT)
                        nc.vector.tensor_tensor(m.x[:, t, :], ps_out[:, OUTPUTS.index((s, "out", h)) % 2, :],
                                                m.x[:, t, :], ALU.add).then_inc(out_added, 1)
                elif side == "keys":
                    rotate(g, s, "keys")
                elif side == "values":
                    b = 1 if s < 4 else 0
                    dve.wait_ge(values_hi, values_count(g, s))
                    nc.vector.tensor_tensor(values[1][:, b], ps_proj[:, projection_bank(g, s, "values"), :].rearrange(
                        "p (t d) -> p t d", t=QT), values[0][:, b].bitcast(F32), ALU.subtract).then_inc(values_split, 1)
                if present(g, s, "score"):
                    mask(g, s, 2)
                    mask(g, s, 3)
                if side == "keys":
                    split_rotated(g, s, "keys")
                if present(g, s, "attend"):
                    split_turned(g, s, 2)
                if present(g, s, "score"):
                    dve.wait_ge(exp_done, 4 * (n + 1) + 4)
                    nc.vector.reciprocal(inverse[:, (s + 1) % 2, :], total[:, (s + 1) % 2, :]).then_inc(total_inverted, 1)
                if present(g, s, "attend"):
                    split_turned(g, s, 3)
                if present(g, s, "query"):
                    rotate(g, s, "query")
                if present(g, s, "attend"):
                    b, j = s // PER_KV, s % PER_KV
                    dve.wait_ge(attended_hi, n + 1)
                    nc.vector.tensor_tensor(attended[1][:, b, j, :], ps_out[:, OUTPUTS.index((s, "attend", 0)) % 2, :],
                                            attended[0][:, b, j, :].bitcast(F32), ALU.subtract).then_inc(attended_split, 1)
                if present(g, s, "query"):
                    split_rotated(g, s, "query")

            for s in (5, 6, 7):
                step(-1, s)
            for s in range(GROUP):
                step(0, s)
            with dve.Fori(1, KV0 - 1) as g:
                for s in range(GROUP):
                    step(g, s)
            for s in range(GROUP):
                step(KV0 - 1, s)
            for s in (0, 1):
                step(KV0, s)

        @block.scalar
        def _(act):
            def exponent(g, s, i):
                n = GROUP * g + s + 1
                slot = (s + 1) % 2
                tile = probs[:, slot, SCORE_AT[i]:SCORE_AT[i + 1]]
                act.wait_ge(score_masked, 4 * n + i + 1)
                nc.scalar.activation(tile, tile, ACT.Exp, bias=least[:, slot, i:i + 1], scale=-1.0,
                                     accum_out=total[:, slot, i:i + 1]).then_inc(exp_done, 1)

            def round_turned(g, s, t):
                n = GROUP * g + s
                w = SEQ - t * P
                act.wait_ge(turned, 4 * n + t + 1)
                wait(act, attend_made, 4 * n + t - 1)
                nc.scalar.copy(probsT[0][:, t % 2, 0:w], ps_turn[:, t % 2, 0:w]).then_inc(turned_hi, 1)

            def round_rotated(g, s, what):
                act.wait_ge(rotation_added, rotation(g, s, what))
                if what == "query":
                    hi = query[0][:, (s + 3) % 4, :]
                    wait(act, score_made, 4 * (GROUP * g + s + 3 - 4) + 4)
                else:
                    b = 1 if s < 4 else 0
                    hi = keys[0][:, b, :]
                    wait(act, score_made, 4 * GROUP * g if b else 4 * (GROUP * g + PER_KV))
                nc.scalar.copy(hi, rotated[:]).then_inc(rotation_hi, 1)

            def step(g, s):
                n = GROUP * g + s
                if present(g, s, "score"):
                    exponent(g, s, 0)
                    exponent(g, s, 1)
                if present(g, s, "attend"):
                    round_turned(g, s, 0)
                    round_turned(g, s, 1)
                side = SIDE[s] if present(g, s, SIDE[s]) else None
                if side == "values":
                    b = 1 if s < 4 else 0
                    act.wait_ge(values_made, values_count(g, s))
                    wait(act, attend_made, 4 * GROUP * g if b else 4 * (GROUP * g + PER_KV))
                    nc.scalar.copy(values[0][:, b], ps_proj[:, projection_bank(g, s, "values"), :].rearrange(
                        "p (t d) -> p t d", t=QT)).then_inc(values_hi, 1)
                if present(g, s, "score"):
                    exponent(g, s, 2)
                    exponent(g, s, 3)
                if side == "keys":
                    round_rotated(g, s, "keys")
                if present(g, s, "attend"):
                    round_turned(g, s, 2)
                    round_turned(g, s, 3)
                if present(g, s, "score"):
                    slot = (s + 1) % 2
                    act.wait_ge(total_inverted, n + 2)
                    for i in range(QT):
                        tile = probs[:, slot, SCORE_AT[i]:SCORE_AT[i + 1]]
                        nc.scalar.activation(tile, tile, ACT.Copy, scale=inverse[:, slot, i:i + 1]).then_inc(probs_ready, 1)
                if present(g, s, "attend"):
                    b, j = s // PER_KV, s % PER_KV
                    act.wait_ge(attend_made, 4 * n + 4)
                    wait(act, out_made, NT * g if b else NT * g - PER_KV)
                    nc.scalar.copy(attended[0][:, b, j, :],
                                   ps_out[:, OUTPUTS.index((s, "attend", 0)) % 2, :]).then_inc(attended_hi, 1)
                if present(g, s, "query"):
                    round_rotated(g, s, "query")

            for s in (5, 6, 7):
                step(-1, s)
            for s in range(GROUP):
                step(0, s)
            with act.Fori(1, KV0 - 1) as g:
                for s in range(GROUP):
                    step(g, s)
            for s in range(GROUP):
                step(KV0 - 1, s)



def ffn0_phase(nc, m):
    dram = m.dram
    with ExitStack() as ctx:
        def sb(what, shape, dt=F32):
            return ctx.enter_context(nc.sbuf_tensor(f"f0_{what}", shape, dt))

        def pair(what, shape):
            return sb(f"{what}_hi", shape, F32R), sb(f"{what}_lo", shape, F32R)

        def sem(what):
            return ctx.enter_context(nc.semaphore(f"f0_{what}"))

        raw = sb("raw", [P, 2, 3, 512], I32)
        gate = pair("gate", [P, 2, DC, P])
        up = pair("up", [P, 2, DC, P])
        down = pair("down", [P, FC, D])
        gate_s, up_s = sb("gate_s", [P, FC]), sb("up_s", [P, FC])
        down_s = sb("down_s", [P, D])
        gate_col, up_col = sb("gate_col", [P, 2]), sb("up_col", [P, 2])
        silu = sb("silu", [P, 2, SEQ])
        hidden = sb("hidden", [P, 2, SEQ])
        hidden0 = pair("hidden0", [P, 2, SEQ])
        hidden1 = pair("hidden1", [P, FC, SEQ])
        ps_gate = ctx.enter_context(nc.psum_tensor("f0_ps_gate", [P, 2, 512], F32))
        ps_up = ctx.enter_context(nc.psum_tensor("f0_ps_up", [P, 2, 512], F32))
        ps_out = ctx.enter_context(nc.psum_tensor("f0_ps_out", [P, QT, 512], F32))

        raw_in = [[sem(f"{w}_in{s}") for w in ("gate", "up", "down")] for s in range(2)]
        scales_in = sem("scales_in")
        weights_hi, weights_split = sem("weights_hi"), sem("weights_split")
        columns_copied = sem("columns_copied")
        made, silu_done, hidden_made = sem("made"), sem("silu_done"), sem("hidden_made")
        hidden_hi, hidden_split = sem("hidden_hi"), sem("hidden_split")
        summed, out_done, out_scaled, out_added = sem("summed"), sem("out_done"), sem("out_scaled"), sem("out_added")
        block = ctx.enter_context(nc.Block())

        @block.sync
        def _(sp):
            sp.dma_start(gate_s[:], dram["gate_s"]).then_inc(scales_in, 16)
            sp.dma_start(up_s[:], dram["up_s"]).then_inc(scales_in, 16)
            sp.dma_start(down_s[:], dram["down_s"].to_broadcast((P, D))).then_inc(scales_in, 16)

            def fetch(f, k):
                wait(sp, weights_split, 3 * f - 3)
                for w, name in enumerate(("gate", "up", "down")):
                    sp.dma_start(raw[:, k, w, :], dram[name][f]).then_inc(raw_in[k][w], 16)

            fetch(0, 0)
            fetch(1, 1)
            with sp.Fori(1, FC // 2) as i:
                for k in range(2):
                    fetch(2 * i + k, k)

        def split_hi(act, f, k, use):
            for w, hi in enumerate((gate[0][:, k], up[0][:, k], down[0][:, f, :])):
                act.wait_ge(raw_in[k][w], 16 * use)
                if w == 0:
                    wait(act, made, 2 * f - 2)
                src = raw[:, k, w, :]
                if w < 2:
                    src = src.rearrange("p (c n) -> p c n", c=DC)
                nc.scalar.copy(hi, src).then_inc(weights_hi, 1)

        def split_lo(dve, f, k):
            for w, (hi, lo) in enumerate(((gate[0][:, k], gate[1][:, k]), (up[0][:, k], up[1][:, k]),
                                          (down[0][:, f, :], down[1][:, f, :]))):
                src = raw[:, k, w, :]
                if w < 2:
                    src = src.rearrange("p (c n) -> p c n", c=DC)
                dve.wait_ge(weights_hi, 3 * f + w + 1)
                nc.vector.tensor_tensor(lo, src, hi.bitcast(F32), ALU.subtract).then_inc(weights_split, 1)

        @block.scalar
        def _(act):
            split_hi(act, 0, 0, 1)

            def chunk(f, k, use, last=False):
                if not last:
                    split_hi(act, f + 1, 1 - k, use + k)
                for b in range(BATCH):
                    q = 2 * f + b
                    act.wait_ge(columns_copied, f + 1)
                    act.wait_ge(made, q + 1)
                    wait(act, hidden_made, q - 1)
                    nc.scalar.activation(silu[:, b, :], ps_gate[:, b, :], ACT.Silu,
                                         scale=gate_col[:, k:k + 1]).then_inc(silu_done, 1)
                    act.wait_ge(hidden_made, q + 1)
                    if b == 0:
                        wait(act, summed, f - 1)
                        hi = hidden0[0][:, k, :]
                    else:
                        hi = hidden1[0][:, f, :]
                    nc.scalar.copy(hi, hidden[:, b, :]).then_inc(hidden_hi, 1)

            chunk(0, 0, 1)
            chunk(1, 1, 1)
            with act.Fori(1, FC // 2 - 1) as i:
                for k in range(2):
                    chunk(2 * i + k, k, i + 1)
            chunk(FC - 2, 0, FC // 2)
            chunk(FC - 1, 1, FC // 2, last=True)

        @block.vector
        def _(dve):
            dve.wait_ge(scales_in, 48)

            def copy_columns(f, k):
                wait(dve, hidden_made, 2 * f - 2)
                nc.vector.tensor_copy(gate_col[:, k:k + 1], gate_s[:, bass.ds(f, 1)])
                nc.vector.tensor_copy(up_col[:, k:k + 1], up_s[:, bass.ds(f, 1)]).then_inc(columns_copied, 1)

            copy_columns(0, 0)
            split_lo(dve, 0, 0)

            def chunk(f, k, last=False):
                if not last:
                    copy_columns(f + 1, 1 - k)
                    split_lo(dve, f + 1, 1 - k)
                for b in range(BATCH):
                    q = 2 * f + b
                    dve.wait_ge(columns_copied, f + 1)
                    dve.wait_ge(silu_done, q + 1)
                    wait(dve, hidden_split, q - 1)
                    nc.vector.scalar_tensor_tensor(hidden[:, b, :], ps_up[:, b, :], up_col[:, k:k + 1], silu[:, b, :],
                                                   ALU.mult, ALU.mult).then_inc(hidden_made, 1)
                    hi, lo = (hidden0[0][:, k, :], hidden0[1][:, k, :]) if b == 0 else \
                             (hidden1[0][:, f, :], hidden1[1][:, f, :])
                    dve.wait_ge(hidden_hi, q + 1)
                    nc.vector.tensor_tensor(lo, hidden[:, b, :], hi.bitcast(F32), ALU.subtract).then_inc(hidden_split, 1)

            for f in range(2):
                chunk(f, f)
            with dve.Fori(1, FC // 2 - 1) as i:
                for k in range(2):
                    chunk(2 * i + k, k)
            chunk(FC - 2, 0)
            chunk(FC - 1, 1, last=True)
            for t in range(NT):
                dve.wait_ge(out_done, t + 1)
                nc.vector.tensor_tensor(hidden[:, t % 2, :], ps_out[:, t % QT, :], down_s[:], ALU.mult).then_inc(out_scaled, 1)
                dve.wait_ge(out_scaled, t + 1)
                nc.vector.tensor_tensor(m.x[:, t, :], m.x[:, t, :], hidden[:, t % 2, :], ALU.add).then_inc(out_added, 1)
            dve.wait_ge(out_added, NT)

        @block.tensor
        def _(pe):
            def make(f, k, b):
                q = 2 * f + b
                if b == 0:
                    pe.wait_ge(weights_split, 3 * f + 3)
                wait(pe, hidden_made, q - 1)
                for out, w in ((ps_gate, gate), (ps_up, up)):
                    for c in range(DC):
                        at = slice(b * SEQ, (b + 1) * SEQ)
                        last = product(nc, out[:, b, :], (w[0][:, k, c, :], w[1][:, k, c, :]),
                                       (m.xT_hi[:, c, at], m.xT_lo[:, c, at]), c == 0, c == DC - 1)
                last.then_inc(made, 1)

            def add_to_sums(f, k, first=False, last=False):
                pe.wait_ge(hidden_split, 2 * f + 1)
                for t in range(QT):
                    at = slice(t * P, (t + 1) * P)
                    mm = product(nc, ps_out[:, t, :], (hidden0[0][:, k, at], hidden0[1][:, k, at]),
                                 (down[0][:, f, :], down[1][:, f, :]), first, last)
                    if last:
                        mm.then_inc(out_done, 1)
                    elif t == QT - 1:
                        mm.then_inc(summed, 1)

            make(0, 0, 0)
            make(0, 0, 1)
            make(1, 1, 0)
            add_to_sums(0, 0, first=True)
            make(1, 1, 1)
            with pe.Fori(1, FC // 2) as i:
                for k in range(2):
                    make(2 * i + k, k, 0)
                    add_to_sums(2 * i + k - 1, 1 - k)
                    make(2 * i + k, k, 1)
            add_to_sums(FC - 1, 1, last=True)
            pe.wait_ge(hidden_split, 2 * FC)
            for t in range(QT):
                at = slice(t * P, (t + 1) * P)
                pe.wait_ge(out_scaled, t + 1)
                for f in range(FC):
                    mm = product(nc, ps_out[:, t, :], (hidden1[0][:, f, at], hidden1[1][:, f, at]),
                                 (down[0][:, f, :], down[1][:, f, :]), f == 0, f == FC - 1)
                mm.then_inc(out_done, 1)


HPC = P // HD1
CHUNKS1 = HEADS1 // HPC
STEPS1 = 2 * HPC
WINDOW = P + HD1
SIDE1 = {0: "out", 1: "out", 2: "out", 3: "out", 4: "query", 5: "keys", 6: "values",
         8: "out", 9: "out", 10: "out", 11: "out", 12: "query", 13: "keys", 14: "values"}
PIECES1 = [("wo", 4), ("wq", 5), ("wk", 6), ("wv", 7)]
MADE1 = [(12, "query"), (13, "keys"), (14, "values"), (4, "query"), (5, "keys"), (6, "values")]


def attention1_phase(nc, m):
    dram = m.dram
    with ExitStack() as ctx:
        def sb(what, shape, dt=F32):
            return ctx.enter_context(nc.sbuf_tensor(f"a1_{what}", shape, dt))

        def pair(what, shape):
            return sb(f"{what}_hi", shape, F32R), sb(f"{what}_lo", shape, F32R)

        def sem(what):
            return ctx.enter_context(nc.semaphore(f"a1_{what}"))

        raw = sb("raw", [P, 4, 512])
        zeros = sb("zeros", [P, 512])
        wq, wk, wv = pair("wq", [P, DC, P]), pair("wk", [P, DC, P]), pair("wv", [P, DC, P])
        wo = pair("wo", [P, D])
        bias = sb("bias", [P, 3, CHUNKS1])
        value_bias = sb("value_bias", [P, 1])
        out_bias = sb("out_bias", [P, D])
        parity = sb("parity", [P, 2])
        keep = sb("keep", [P, 2, SEQ])
        query = pair("query", [P, 2, BATCH, SEQ])
        keys = pair("keys", [P, BATCH, SEQ])
        values = pair("values", [P, BATCH, QT, HPC * P])
        causal = sb("causal", [P, SEQ])
        slope = sb("slope", [P, 2, SEQ])
        table = sb("table", [P, 2, SEQ])
        probs = sb("probs", [P, 2, SCORE_AT[QT]])
        least, total, inverse = sb("least", [P, 2, QT]), sb("total", [P, 2, QT]), sb("inverse", [P, 2, QT])
        probsT = pair("probsT", [P, 2, SEQ])
        attended = pair("attended", [P, BATCH, SEQ])

        ps_proj = ctx.enter_context(nc.psum_tensor("a1_ps_proj", [P, 2, 512], F32))
        ps_score = ctx.enter_context(nc.psum_tensor("a1_ps_score", [P, 2, 512], F32))
        ps_turn = ctx.enter_context(nc.psum_tensor("a1_ps_turn", [P, 2, 512], F32))
        ps_attend = ctx.enter_context(nc.psum_tensor("a1_ps_attend", [P, 512], F32))
        ps_out = ctx.enter_context(nc.psum_tensor("a1_ps_out", [P, 512], F32))

        raw_in = [sem(f"{w}_in") for w in ("wo", "wq", "wk", "wv")]
        slope_in = [sem("slope_in0"), sem("slope_in1")]
        consts_in, zeros_set, values_zero, wait_passed = sem("consts_in"), sem("zeros_set"), sem("values_zero"), sem("wait_passed")
        wait_passed_sp, value_bias_set = sem("wait_passed_sp"), sem("value_bias_set")
        piece_hi, piece_split, table_made = sem("piece_hi"), sem("piece_split"), sem("table_made")
        projected, biased, operand_hi, operand_split = sem("projected"), sem("biased"), sem("operand_hi"), sem("operand_split")
        score_made, score_masked = sem("score_made"), sem("score_masked")
        exp_done, total_inverted, probs_ready = sem("exp_done"), sem("total_inverted"), sem("probs_ready")
        turned, turned_hi, turned_split = sem("turned"), sem("turned_hi"), sem("turned_split")
        attend_made, attended_hi, attended_split = sem("attend_made"), sem("attended_hi"), sem("attended_split")
        out_made, out_added, bias_added = sem("out_made"), sem("out_added"), sem("bias_added")

        def operand(c, s):
            return 6 * c + (s - 4 + 4 if s < 8 else s - 12 + 7)

        def out_count(c, s):
            return 8 * c + (s - 3 if s < 4 else s - 8 + 1)

        def piece_count(c, what):
            if what == "wo":
                return 3 + 4 * c + 1
            at = ("wq", "wk", "wv").index(what)
            if isinstance(c, int) and c == 0:
                return at + 1
            return 3 + 4 * (c - 1) + 2 + at

        def present(c, s, what):
            if not isinstance(c, int):
                return True
            if what == "score":
                return 0 <= STEPS1 * c + s + 1 < STEPS1 * CHUNKS1
            if what == "attend":
                return 0 <= c < CHUNKS1
            if what == "out":
                return 1 <= c if s < 8 else 0 <= c < CHUNKS1
            if what is None:
                return False
            return 0 <= c < CHUNKS1 if s < 8 else c < CHUNKS1 - 1

        def bank(s):
            return (s - 4) % 2 if s < 8 else (s - 12 + 1) % 2

        def batch_of(s):
            return 1 if s < 8 else 0

        def each_chunk(engine, step):
            for s in (12, 13, 14, 15):
                step(-1, s)
            for s in range(STEPS1):
                step(0, s)
            with engine.Fori(1, CHUNKS1 - 1) as c:
                for s in range(STEPS1):
                    step(c, s)
            for s in range(STEPS1):
                step(CHUNKS1 - 1, s)
            for s in range(4):
                step(CHUNKS1, s)

        block = ctx.enter_context(nc.Block())

        @block.sync
        def _(sp):
            for name, dst in (("wq1", raw[:, 1, :]), ("wk1", raw[:, 2, :]), ("wv1", raw[:, 3, :])):
                w = ("wo1", "wq1", "wk1", "wv1").index(name)
                sp.dma_start(dst, dram[name][0]).then_inc(raw_in[w], 16)
            for dst, src in ((bias[:], dram["bias1"]), (parity[:], dram["parity"]), (causal[:], dram["causal"]),
                             (out_bias[:], dram["out_bias"].to_broadcast((P, D)))):
                sp.dma_start(dst, src).then_inc(consts_in, 16)

            def step(c, s):
                u = (s + 2) % STEPS1
                cu = c if s + 2 < STEPS1 else c + 1
                n = STEPS1 * c + s + 2
                if (not isinstance(c, int)) or 0 <= n < STEPS1 * CHUNKS1:
                    wait(sp, table_made, n - 1)
                    sp.sem_inc(wait_passed_sp, 1)
                    sp.dma_start(slope[:, u % 2, :], dram["slope"][cu, u % HPC].to_broadcast((P, SEQ))).then_inc(slope_in[u % 2], 16)
                for at, (what, when) in enumerate(PIECES1):
                    if s != when - 4:
                        continue
                    if what != "wo" and isinstance(c, int) and not 0 <= c < CHUNKS1 - 1:
                        continue
                    if what == "wo" and isinstance(c, int) and not 0 <= c < CHUNKS1:
                        continue
                    w = ("wo", "wq", "wk", "wv").index(what)
                    wait(sp, piece_split, piece_count(c - 1, what) if what == "wo" else piece_count(c, what))
                    sp.sem_inc(wait_passed_sp, 1)
                    sp.dma_start(raw[:, w, :], dram[what + "1"][c if what == "wo" else c + 1]).then_inc(raw_in[w], 16)

            step(-1, 14)
            each = [(0, s) for s in range(STEPS1)]
            step(-1, 15)
            for c, s in each:
                step(c, s)
            with sp.Fori(1, CHUNKS1 - 1) as c:
                for s in range(STEPS1):
                    step(c, s)
            for s in range(STEPS1):
                step(CHUNKS1 - 1, s)

        @block.gpsimd
        def _(pool):
            nc.gpsimd.memset(zeros[:], 0.0).then_inc(zeros_set, 1)
            for part in values:
                nc.gpsimd.memset(part[:].rearrange("p b t n -> p (b t n)").bitcast(F32), 0.0).then_inc(values_zero, 1)
            pool.wait_ge(zeros_set, 1)

            def split(count, landed, what):
                w = ("wo", "wq", "wk", "wv").index(what)
                pair_ = (wo, wq, wk, wv)[w]
                src, zero = raw[:, w, :], zeros[:]
                if what != "wo":
                    src, zero = (x.rearrange("p (c n) -> p c n", c=DC) for x in (src, zero))
                pool.wait_ge(raw_in[w], 16 * landed)
                nc.gpsimd.tensor_tensor(pair_[0][:], src, zero, ALU.add).then_inc(piece_hi, 1)
                pool.wait_ge(piece_hi, count + 1)
                nc.gpsimd.tensor_tensor(pair_[1][:], src, pair_[0][:].bitcast(F32), ALU.subtract).then_inc(piece_split, 1)

            def make_table(n, slot, landed):
                pool.wait_ge(slope_in[slot], 16 * landed)
                wait(pool, score_masked, 4 * n - 4)
                nc.gpsimd.tensor_tensor(table[:, slot, :], slope[:, slot, :], causal[:], ALU.add).then_inc(table_made, 1)

            for at, what in enumerate(("wq", "wk", "wv")):
                split(at, 1, what)
            pool.wait_ge(consts_in, 16 * 4)
            make_table(0, 0, 1)

            def step(c, s):
                n = STEPS1 * c + s + 1
                for at, (what, when) in enumerate(PIECES1):
                    if s != when or (isinstance(c, int) and c == CHUNKS1 - 1 and what != "wo"):
                        continue
                    if what == "wo":
                        wait(pool, out_made, out_count(c, 3))
                    else:
                        wait(pool, projected, operand(c, {"wq": 4, "wk": 5, "wv": 6}[what]))
                    split(3 + 4 * c + at, c + (1 if what == "wo" else 2), what)
                if (not isinstance(c, int)) or n < STEPS1 * CHUNKS1:
                    make_table(n, (s + 1) % 2, HPC * c + (s + 1) // 2 + 1)

            for s in range(STEPS1):
                step(0, s)
            with pool.Fori(1, CHUNKS1 - 1) as c:
                for s in range(STEPS1):
                    step(c, s)
            for s in range(STEPS1):
                step(CHUNKS1 - 1, s)

        @block.tensor
        def _(pe):
            def project(c, s):
                b = batch_of(s)
                what = SIDE1[s]
                w = {"query": wq, "keys": wk, "values": wv}[what]
                wait(pe, piece_split, piece_count(c if b else c + 1, {"query": "wq", "keys": "wk", "values": "wv"}[what]))
                wait(pe, operand_split, operand(c, s) - 2)
                if what == "values":
                    for t in range(QT):
                        for k in range(DC):
                            at = slice(b * SEQ + t * P, b * SEQ + (t + 1) * P)
                            last = product(nc, ps_proj[:, bank(s), t * P:(t + 1) * P], (m.xT_hi[:, k, at], m.xT_lo[:, k, at]),
                                           (w[0][:, k, :], w[1][:, k, :]), k == 0, k == DC - 1)
                else:
                    for k in range(DC):
                        at = slice(b * SEQ, (b + 1) * SEQ)
                        last = product(nc, ps_proj[:, bank(s), :], (w[0][:, k, :], w[1][:, k, :]),
                                       (m.xT_hi[:, k, at], m.xT_lo[:, k, at]), k == 0, k == DC - 1)
                last.then_inc(projected, 1)

            def score(c, s, i):
                u = (s + 1) % STEPS1
                n = STEPS1 * c + s + 1
                b, j = u // HPC, u % HPC
                if i == 0 and j == 0:
                    wait(pe, operand_split, operand(c, 13 if b == 0 else 5))
                wait(pe, score_masked, 4 * n + i - 1)
                rows = slice(32 * (j // 2), 32 * (j // 2) + 32)
                q = [x[rows, j % 2, b, i * P:(i + 1) * P] for x in query]
                k = [x[rows, b, 0:P * (i + 1)] for x in keys]
                product(nc, ps_score[:, i % 2, 0:P * (i + 1)], q, k, True, True).then_inc(score_made, 1)

            def turn(n, u, t):
                if t == 0:
                    wait(pe, probs_ready, 4 * n + 4)
                wait(pe, turned_split, 4 * n + t - 1)
                for i in range(t, QT):
                    at = SCORE_AT[i] + t * P
                    last = nc.tensor.transpose(ps_turn[:, t % 2, (i - t) * P:(i - t + 1) * P],
                                               probs[:, u % 2, at:at + P], m.ident[:])
                last.then_inc(turned, 1)

            def attend(c, u, t):
                n = STEPS1 * c + u
                b, j = u // HPC, u % HPC
                if t == 0 and j == 0:
                    wait(pe, operand_split, operand(c - 1, 14) if b == 0 else operand(c, 6))
                    wait(pe, attended_split, 2 * c + b)
                wait(pe, turned_split, 4 * n + t + 1)
                w = SEQ - t * P
                product(nc, ps_attend[:, t * P:SEQ], [x[:, b, t, j * P:(j + 1) * P] for x in values],
                        [x[:, t % 2, 0:w] for x in probsT], j == 0 and t == 0, j == HPC - 1 and t == QT - 1).then_inc(attend_made, 1)

            def make_out(c, s):
                b = batch_of(s)
                t = s % 4
                wait(pe, out_added, out_count(c, s) - 1)
                if t == 0:
                    wait(pe, attended_split, 2 * c if b else 2 * c + 1)
                    wait(pe, piece_split, piece_count(c - 1 if b else c, "wo"))
                at = slice(t * P, (t + 1) * P)
                product(nc, ps_out[:], [x[:, b, at] for x in attended], [x[:] for x in wo], True, True).then_inc(out_made, 1)

            def step(c, s):
                n = STEPS1 * c + s
                side = SIDE1.get(s) if present(c, s, SIDE1.get(s)) else None
                if present(c, s, "score") and s >= 0 and (not isinstance(c, int) or c >= 0 or s == 15):
                    score(c, s, 0)
                    score(c, s, 1)
                if present(c, s, "attend"):
                    turn(n, s, 0)
                    turn(n, s, 1)
                if side in ("query", "keys", "values"):
                    project(c, s)
                elif side == "out":
                    make_out(c, s)
                if present(c, s, "score") and (not isinstance(c, int) or c >= 0 or s == 15):
                    score(c, s, 2)
                    score(c, s, 3)
                if present(c, s, "attend"):
                    attend(c, s, 0)
                    turn(n, s, 2)
                    attend(c, s, 1)
                    turn(n, s, 3)
                    attend(c, s, 2)
                    attend(c, s, 3)

            each_chunk(pe, step)

        @block.vector
        def _(dve):
            dve.wait_ge(consts_in, 16 * 4)
            dve.wait_ge(values_zero, 2)
            for t in range(NT):
                nc.vector.tensor_tensor(m.x[:, t, :], m.x[:, t, :], out_bias[:], ALU.add).then_inc(bias_added, 1)
            dve.wait_ge(bias_added, NT)

            def add_bias(c, s):
                b = batch_of(s)
                cb = c if b else c + 1
                which = 0 if SIDE1[s] == "query" else 1
                dve.wait_ge(projected, operand(c, s))
                add = bias[:, which, bass.ds(cb, 1)]
                wait(dve, operand_split, operand(c, s) - 1)
                if which == 0:
                    for e in range(2):
                        nc.vector.tensor_scalar(keep[:, e, :], ps_proj[:, bank(s), :], add, parity[:, e:e + 1],
                                                ALU.add, ALU.mult).then_inc(biased, 1)
                else:
                    nc.vector.tensor_scalar(keep[:, 0, :], ps_proj[:, bank(s), :], add, None, ALU.add).then_inc(biased, 1)

            def split_operand(c, s):
                b = batch_of(s)
                dve.wait_ge(operand_hi, operand(c, s))
                if SIDE1[s] == "query":
                    nc.vector.tensor_tensor(query[1][:, :, b, :], keep[:], query[0][:, :, b, :].bitcast(F32),
                                            ALU.subtract).then_inc(operand_split, 1)
                elif SIDE1[s] == "keys":
                    nc.vector.tensor_tensor(keys[1][:, b, :], keep[:, 0, :], keys[0][:, b, :].bitcast(F32),
                                            ALU.subtract).then_inc(operand_split, 1)
                else:
                    for t in range(QT):
                        last = nc.vector.tensor_tensor(in_windows(values[1], b, t), made_values(s, t),
                                                       in_windows(values[0], b, t).bitcast(F32), ALU.subtract)
                    last.then_inc(operand_split, 1)

            def mask(c, s, i):
                n = STEPS1 * c + s + 1
                slot = (s + 1) % 2
                at, w = SCORE_AT[i], P * (i + 1)
                if i == 0:
                    wait(dve, turned, 4 * (n - 1))
                    dve.wait_ge(table_made, n + 1)
                dve.wait_ge(score_made, 4 * n + i + 1)
                dve.sem_inc(wait_passed, 1)
                nc.vector.tensor_tensor_reduce(
                    out=probs[:, slot, at:at + w], in0=ps_score[:, i % 2, 0:w], in1=table[:, slot, SEQ - w:SEQ],
                    scale=-float(HD1) ** -0.5, scalar=-LOWEST, op0=ALU.add, op1=ALU.min,
                    accum_out=least[:, slot, i:i + 1]).then_inc(score_masked, 1)

            def split_turned(c, s, t):
                n = STEPS1 * c + s
                w = SEQ - t * P
                dve.wait_ge(turned_hi, 4 * n + t + 1)
                nc.vector.tensor_tensor(probsT[1][:, t % 2, 0:w], ps_turn[:, t % 2, 0:w],
                                        probsT[0][:, t % 2, 0:w].bitcast(F32), ALU.subtract).then_inc(turned_split, 1)

            def step(c, s):
                n = STEPS1 * c + s
                side = SIDE1.get(s) if present(c, s, SIDE1.get(s)) else None
                scoring = present(c, s, "score") and (not isinstance(c, int) or c >= 0 or s == 15)
                attending = present(c, s, "attend")
                if attending and s == 0:
                    wait(dve, attended_split, 2 * c)
                    nc.vector.tensor_copy(value_bias[:], bias[:, 2, bass.ds(c, 1)]).then_inc(value_bias_set, 1)
                if scoring:
                    mask(c, s, 0)
                    mask(c, s, 1)
                if attending:
                    split_turned(c, s, 0)
                    split_turned(c, s, 1)
                if scoring:
                    mask(c, s, 2)
                    mask(c, s, 3)
                if side in ("query", "keys"):
                    add_bias(c, s)
                elif side == "out":
                    b = batch_of(s)
                    t = b * QT + s % 4
                    dve.wait_ge(out_made, out_count(c, s))
                    wait(dve, out_added, out_count(c, s) - QT)
                    nc.vector.tensor_tensor(m.x[:, t, :], ps_out[:], m.x[:, t, :], ALU.add).then_inc(out_added, 1)
                if attending:
                    split_turned(c, s, 2)
                    split_turned(c, s, 3)
                if scoring:
                    dve.wait_ge(exp_done, 4 * (n + 1) + 4)
                    nc.vector.reciprocal(inverse[:, (s + 1) % 2, :], total[:, (s + 1) % 2, :]).then_inc(total_inverted, 1)
                if side in ("query", "keys", "values"):
                    split_operand(c, s)
                if attending and s % HPC == HPC - 1:
                    b = s // HPC
                    dve.wait_ge(value_bias_set, c + 1)
                    dve.wait_ge(attended_hi, 2 * c + b + 1)
                    nc.vector.scalar_tensor_tensor(attended[1][:, b, :], ps_attend[:], value_bias[:],
                                                   attended[0][:, b, :].bitcast(F32), ALU.add, ALU.subtract).then_inc(attended_split, 1)

            def in_windows(x, b, t):
                return bass.AP(x, (b * QT + t) * HPC * P, [[BATCH * QT * HPC * P, P], [WINDOW, HPC], [1, HD1]])

            def made_values(s, t):
                return ps_proj[:, bank(s), t * P:(t + 1) * P].rearrange("p (j d) -> p j d", j=HPC)

            each_chunk(dve, step)

        @block.scalar
        def _(act):
            act.wait_ge(consts_in, 16 * 4)
            act.wait_ge(values_zero, 2)

            def in_windows(x, b, t):
                return bass.AP(x, (b * QT + t) * HPC * P, [[BATCH * QT * HPC * P, P], [WINDOW, HPC], [1, HD1]])

            def round_operand(c, s):
                b = batch_of(s)
                n0 = STEPS1 * c if b else STEPS1 * c + HPC
                if SIDE1[s] == "query":
                    act.wait_ge(biased, biased_count(c, s))
                    wait(act, score_made, 4 * n0)
                    nc.scalar.copy(query[0][:, :, b, :], keep[:]).then_inc(operand_hi, 1)
                elif SIDE1[s] == "keys":
                    act.wait_ge(biased, biased_count(c, s))
                    wait(act, score_made, 4 * n0)
                    nc.scalar.copy(keys[0][:, b, :], keep[:, 0, :]).then_inc(operand_hi, 1)
                else:
                    act.wait_ge(projected, operand(c, s))
                    wait(act, attend_made, 4 * n0)
                    for t in range(QT):
                        last = nc.scalar.copy(in_windows(values[0], b, t), ps_proj[:, bank(s), t * P:(t + 1) * P].rearrange(
                            "p (j d) -> p j d", j=HPC))
                    last.then_inc(operand_hi, 1)

            def biased_count(c, s):
                return 6 * c + {4: 5, 5: 6, 12: 8, 13: 9}[s]

            def exponent(c, s, i):
                n = STEPS1 * c + s + 1
                slot = (s + 1) % 2
                tile = probs[:, slot, SCORE_AT[i]:SCORE_AT[i + 1]]
                act.wait_ge(score_masked, 4 * n + i + 1)
                nc.scalar.activation(tile, tile, ACT.Exp, bias=least[:, slot, i:i + 1], scale=-1.0,
                                     accum_out=total[:, slot, i:i + 1]).then_inc(exp_done, 1)

            def round_turned(c, s, t):
                n = STEPS1 * c + s
                w = SEQ - t * P
                act.wait_ge(turned, 4 * n + t + 1)
                wait(act, attend_made, 4 * n + t - 1)
                nc.scalar.copy(probsT[0][:, t % 2, 0:w], ps_turn[:, t % 2, 0:w]).then_inc(turned_hi, 1)

            def step(c, s):
                n = STEPS1 * c + s
                side = SIDE1.get(s) if present(c, s, SIDE1.get(s)) else None
                scoring = present(c, s, "score") and (not isinstance(c, int) or c >= 0 or s == 15)
                attending = present(c, s, "attend")
                if scoring:
                    exponent(c, s, 0)
                    exponent(c, s, 1)
                if attending:
                    round_turned(c, s, 0)
                    round_turned(c, s, 1)
                if scoring:
                    exponent(c, s, 2)
                    exponent(c, s, 3)
                if attending:
                    round_turned(c, s, 2)
                    round_turned(c, s, 3)
                if scoring:
                    slot = (s + 1) % 2
                    act.wait_ge(total_inverted, n + 2)
                    for i in range(QT):
                        tile = probs[:, slot, SCORE_AT[i]:SCORE_AT[i + 1]]
                        nc.scalar.activation(tile, tile, ACT.Copy, scale=inverse[:, slot, i:i + 1]).then_inc(probs_ready, 1)
                if side in ("query", "keys", "values"):
                    round_operand(c, s)
                if attending and s % HPC == HPC - 1:
                    b = s // HPC
                    act.wait_ge(attend_made, 4 * n + 4)
                    wait(act, out_made, NT * c if b else NT * c - QT)
                    act.wait_ge(value_bias_set, c + 1)
                    nc.scalar.activation(attended[0][:, b, :], ps_attend[:], ACT.Identity, bias=value_bias[:]).then_inc(attended_hi, 1)

            each_chunk(act, step)



def moe_phase(nc, m, out):
    dram = m.dram
    with ExitStack() as ctx:
        def sb(what, shape, dt=F32):
            return ctx.enter_context(nc.sbuf_tensor(f"moe_{what}", shape, dt))

        def pair(what, shape):
            return sb(f"{what}_hi", shape, F32R), sb(f"{what}_lo", shape, F32R)

        def sem(what):
            return ctx.enter_context(nc.semaphore(f"moe_{what}"))

        KC = KR // P
        down_raw = sb("down_raw", [P, DC, KR])
        up_raw = sb("up_raw", [P, KC, D])
        router_raw = sb("router_raw", [P, DC, EXPERTS])
        down, up, router = pair("down", [P, DC, KR]), pair("up", [P, KC, D]), pair("router", [P, DC, EXPERTS])
        scores = sb("scores", [P, 2, EXPERTS])
        left1, left2 = sb("left1", [P, 2, EXPERTS]), sb("left2", [P, 2, EXPERTS])
        top1, top2 = sb("top1", [P, 2, 8]), sb("top2", [P, 2, 8])
        lowest = sb("lowest", [P, 2])
        chosen = sb("chosen", [P, 2, EXPERTS])
        expd = sb("expd", [P, 2, EXPERTS])
        gated = sb("gated", [P, 2, EXPERTS])
        total, inverse = sb("total", [P, 2]), sb("inverse", [P, 2])
        gates = sb("gates", [P, 2, EXPERTS])
        ranks = sb("ranks", [P, 2, KR])
        ranksT = pair("ranksT", [P, 2, KC, P])

        ps_score = ctx.enter_context(nc.psum_tensor("moe_ps_score", [P, 512], F32))
        ps_rank = ctx.enter_context(nc.psum_tensor("moe_ps_rank", [P, 2, 2, 512], F32))
        ps_turn = ctx.enter_context(nc.psum_tensor("moe_ps_turn", [P, 2, 512], F32))
        ps_out = ctx.enter_context(nc.psum_tensor("moe_ps_out", [P, 512], F32))

        router_in, down_in, up_in = sem("router_in"), [sem(f"down_in{i}") for i in range(DC)], [sem(f"up_in{i}") for i in range(2)]
        weights_hi, weights_split = sem("weights_hi"), sem("weights_split")
        score_made, ranks_made, turned, out_made = sem("score_made"), sem("ranks_made"), sem("turned"), sem("out_made")
        picked, exp_done, gates_made = sem("picked"), sem("exp_done"), sem("gates_made")
        ranks_gated, turned_hi, turned_split, added, stored = sem("ranks_gated"), sem("turned_hi"), sem("turned_split"), sem("added"), sem("stored")
        block = ctx.enter_context(nc.Block())
        pieces = [(router_raw[:], router, slice(None), router_in)]
        pieces += [(down_raw[:, c, :], down, c, down_in[c]) for c in range(DC)]
        pieces += [(up_raw[:, 4 * i:4 * i + 4, :], up, slice(4 * i, 4 * i + 4), up_in[i]) for i in range(2)]

        @block.sync
        def _(sp):
            sp.dma_start(router_raw[:], dram["router"]).then_inc(router_in, 16)
            for c in range(DC):
                sp.dma_start(down_raw[:, c, :], dram["down1"][:, c, :]).then_inc(down_in[c], 16)
            for i in range(2):
                sp.dma_start(up_raw[:, 4 * i:4 * i + 4, :], dram["up1"][:, 4 * i:4 * i + 4, :]).then_inc(up_in[i], 16)
            for t in range(NT):
                sp.wait_ge(added, t + 1)
                sp.dma_start(out[t * P:(t + 1) * P, :], m.x[:, t, :]).then_inc(stored, 16)
            sp.wait_ge(stored, 16 * NT)

        @block.tensor
        def _(pe):
            def score(t):
                at = slice(t * P, (t + 1) * P)
                if t == 0:
                    pe.wait_ge(weights_split, 1)
                else:
                    pe.wait_ge(picked, 5 * t - 4)
                for c in range(DC):
                    last = product(nc, ps_score[:, 0:EXPERTS], (m.xT_hi[:, c, at], m.xT_lo[:, c, at]),
                                   [x[:, c, :] for x in router], c == 0, c == DC - 1)
                last.then_inc(score_made, 1)

            def rank(t):
                at = slice(t * P, (t + 1) * P)
                if t >= 2:
                    pe.wait_ge(ranks_gated, 2 * (t - 1))
                for c in range(DC):
                    if t == 0:
                        pe.wait_ge(weights_split, 2 + c)
                    for half in range(2):
                        last = product(nc, ps_rank[:, t % 2, half, :], (m.xT_hi[:, c, at], m.xT_lo[:, c, at]),
                                       [x[:, c, half * 512:(half + 1) * 512] for x in down], c == 0, c == DC - 1)
                last.then_inc(ranks_made, 1)

            def turn(t):
                for half in range(2):
                    pe.wait_ge(ranks_gated, 2 * t + half + 1)
                    wait(pe, turned_split, 2 * t + half - 1)
                    for k in range(4):
                        at = (4 * half + k) * P
                        last = nc.tensor.transpose(ps_turn[:, half, k * P:(k + 1) * P], ranks[:, t % 2, at:at + P], m.ident[:])
                    last.then_inc(turned, 1)

            def make_out(t):
                if t >= 1:
                    pe.wait_ge(added, t)
                for k in range(KC):
                    if k % 4 == 0:
                        pe.wait_ge(turned_split, 2 * t + k // 4 + 1)
                        if t == 0:
                            pe.wait_ge(weights_split, 6 + k // 4)
                    last = product(nc, ps_out[:], [x[:, t % 2, k, :] for x in ranksT], [x[:, k, :] for x in up], k == 0, k == KC - 1)
                last.then_inc(out_made, 1)

            score(0)
            rank(0)
            for t in range(NT):
                if t + 1 < NT:
                    score(t + 1)
                    rank(t + 1)
                turn(t)
                make_out(t)

        @block.vector
        def _(dve):
            def split_lo(i):
                src, (hi, lo), at, _ = pieces[i]
                dve.wait_ge(weights_hi, i + 1)
                nc.vector.tensor_tensor(lo[:, at], src, hi[:, at].bitcast(F32), ALU.subtract).then_inc(weights_split, 1)

            def pick(t):
                k = t % 2
                dve.wait_ge(score_made, t + 1)
                nc.vector.tensor_copy(scores[:, k, :], ps_score[:, 0:EXPERTS]).then_inc(picked, 1)
                dve.wait_ge(picked, 5 * t + 1)
                nc.vector.max(top1[:, k, :], scores[:, k, :]).then_inc(picked, 1)
                dve.wait_ge(picked, 5 * t + 2)
                nc.vector.tensor_scalar(lowest[:, k:k + 1], top1[:, k, 0:1], -1.0, None, ALU.mult)
                nc.vector.match_replace(left1[:, k, :], top1[:, k, :], scores[:, k, :], LOWEST).then_inc(picked, 1)
                dve.wait_ge(picked, 5 * t + 3)
                nc.vector.max(top2[:, k, :], left1[:, k, :]).then_inc(picked, 1)
                dve.wait_ge(picked, 5 * t + 4)
                nc.vector.match_replace(left2[:, k, :], top2[:, k, :], left1[:, k, :], LOWEST).then_inc(picked, 1)
                dve.wait_ge(picked, 5 * t + 5)
                nc.vector.tensor_scalar(chosen[:, k, :], left2[:, k, :], LOWEST, None, ALU.is_equal).then_inc(gates_made, 1)
                dve.wait_ge(gates_made, 4 * t + 1)
                dve.wait_ge(exp_done, t + 1)
                nc.vector.tensor_tensor_reduce(out=gated[:, k, :], in0=expd[:, k, :], in1=chosen[:, k, :], scale=1.0, scalar=0.0,
                                               op0=ALU.mult, op1=ALU.add, accum_out=total[:, k:k + 1]).then_inc(gates_made, 1)
                dve.wait_ge(gates_made, 4 * t + 2)
                nc.vector.reciprocal(inverse[:, k:k + 1], total[:, k:k + 1]).then_inc(gates_made, 1)
                dve.wait_ge(gates_made, 4 * t + 3)
                nc.vector.tensor_scalar(gates[:, k, :], gated[:, k, :], inverse[:, k:k + 1], 2.0, ALU.mult, ALU.mult).then_inc(gates_made, 1)

            def gate_ranks(t):
                dve.wait_ge(gates_made, 4 * t + 4)
                dve.wait_ge(ranks_made, t + 1)
                if t >= 2:
                    dve.wait_ge(turned, 2 * (t - 1))
                for half in range(2):
                    n = EXPERTS // 2
                    nc.vector.tensor_tensor(
                        ranks[:, t % 2, half * 512:(half + 1) * 512].rearrange("p (k r) -> p k r", r=RANK),
                        ps_rank[:, t % 2, half, :].rearrange("p (k r) -> p k r", r=RANK),
                        gates[:, t % 2, half * n:(half + 1) * n].unsqueeze(2).to_broadcast((P, n, RANK)),
                        ALU.mult).then_inc(ranks_gated, 1)

            split_lo(0)
            pick(0)
            for i in range(1, 5):
                split_lo(i)
            gate_ranks(0)
            for i in range(5, 7):
                split_lo(i)
            for t in range(NT):
                if t + 1 < NT:
                    pick(t + 1)
                for half in range(2):
                    dve.wait_ge(turned_hi, 2 * t + half + 1)
                    nc.vector.tensor_tensor(ranksT[1][:, t % 2, 4 * half:4 * half + 4, :],
                                            ps_turn[:, half, :].rearrange("p (k n) -> p k n", k=4),
                                            ranksT[0][:, t % 2, 4 * half:4 * half + 4, :].bitcast(F32),
                                            ALU.subtract).then_inc(turned_split, 1)
                if t + 1 < NT:
                    gate_ranks(t + 1)
                dve.wait_ge(out_made, t + 1)
                nc.vector.tensor_tensor(m.x[:, t, :], ps_out[:], m.x[:, t, :], ALU.add).then_inc(added, 1)

        @block.scalar
        def _(act):
            def split_hi(i):
                src, (hi, _), at, landed = pieces[i]
                act.wait_ge(landed, 16)
                nc.scalar.copy(hi[:, at], src).then_inc(weights_hi, 1)

            def exponent(t):
                act.wait_ge(picked, 5 * t + 3)
                if t >= 2:
                    act.wait_ge(gates_made, 4 * (t - 1))
                nc.scalar.activation(expd[:, t % 2, :], scores[:, t % 2, :], ACT.Exp, bias=lowest[:, t % 2:t % 2 + 1]).then_inc(exp_done, 1)

            split_hi(0)
            for i in range(1, 7):
                split_hi(i)
            exponent(0)
            for t in range(NT):
                if t + 1 < NT:
                    exponent(t + 1)
                for half in range(2):
                    act.wait_ge(turned, 2 * t + half + 1)
                    if t >= 2:
                        act.wait_ge(out_made, t - 1)
                    nc.scalar.copy(ranksT[0][:, t % 2, 4 * half:4 * half + 4, :],
                                   ps_turn[:, half, :].rearrange("p (k n) -> p k n", k=4)).then_inc(turned_hi, 1)


def program(nc, dram, out):
    with ExitStack() as ctx:
        def sb(what, shape, dt=F32):
            return ctx.enter_context(nc.sbuf_tensor(what, shape, dt))

        m = Model(dram=dram, x=sb("x", [P, NT, D]), ident=sb("ident", [P, P]),
                            xT_hi=sb("xT_hi", [P, DC, TOK], F32R), xT_lo=sb("xT_lo", [P, DC, TOK], F32R),
                            ln_loaded=[ctx.enter_context(nc.semaphore(f"ln_loaded{t}")) for t in range(NT)],
                            ln_semaphores=[ctx.enter_context(nc.semaphore(f"ln_{what}")) for what in LN_SEMAPHORES])
        layernorm_phase(nc, m, 0, load=dram["x"])
        attention0_phase(nc, m)
        layernorm_phase(nc, m, 1)
        ffn0_phase(nc, m)
        layernorm_phase(nc, m, 2)
        attention1_phase(nc, m)
        layernorm_phase(nc, m, 3)
        moe_phase(nc, m, out)



def shape_constants():
    f = np.float32
    pos = np.arange(SEQ, dtype=f)
    inv_freq = (f(1.0) / f(10000.0) ** (np.arange(0, HD0, 2, dtype=f) / f(HD0))).astype(f)
    angle = np.concatenate([(pos[:, None] * inv_freq[None, :]).astype(f)] * 2, axis=1).T
    cos, sin = np.cos(angle).astype(f), np.sin(angle).astype(f)
    sin[HD0 // 2:] *= f(-1.0)
    scale = np.where(pos < SYS_LEN, f(0.5), np.where(pos < SYS_LEN + IMG_LEN, f(1.5), f(1.0))).astype(f)
    unscale = np.ones((P, P), f)
    unscale[:SYS_LEN + IMG_LEN] = (f(1.0) / scale[:P])[None, :]
    row, col = np.arange(P)[:, None], np.arange(P)[None, :]
    causal = np.zeros((P, SEQ), f)
    causal[:, SEQ - P:] = np.where(row >= col, f(0.0), f(MASKED))
    slopes = f(1.0) / f(2.0) ** (np.arange(1, HEADS1 + 1, dtype=f) * f(8.0 / HEADS1))
    slope = (slopes[:, None] * (pos - f(SEQ - 1))[None, :]).astype(f) * f(HD1 ** 0.5)
    parity = np.stack([(np.arange(P) // HD1 % 2 == e).astype(f) for e in range(2)], axis=1)
    return {"cos_q": cos, "sin_q": sin, "cos_k": cos * scale, "sin_k": sin * scale, "unscale": unscale,
            "causal": causal, "ident": np.eye(P, dtype=f), "slope": slope.reshape(CHUNKS1, HPC, 1, SEQ), "parity": parity}


def columns(w, n):
    return w.reshape(-1, n, DC, P).transpose(0, 3, 2, 1).reshape(-1, P, DC * n)


def lay_out(i):
    i = {k: np.asarray(v) for k, v in i.items()}
    w_qkv = columns(i["L1_attn_w_qkv"], P)
    return {
        "x": i["L0_attn_hidden_states"].reshape(TOK, D),
        "wq": columns(i["L0_attn_wq"], HD0).reshape(KV0, PER_KV, P, DC * HD0),
        "wk": columns(i["L0_attn_wk"], HD0),
        "wv": columns(i["L0_attn_wv"], HD0),
        "wo": i["L0_attn_wo"].T.reshape(KV0, PER_KV, HD0, D),
        "gate": columns(i["L0_ffn_gate_t"], P),
        "up": columns(i["L0_ffn_up_t"], P),
        "down": i["L0_ffn_down_t"].T.reshape(FC, P, D),
        "gate_s": i["L0_ffn_gate_s"].reshape(FC, P).T,
        "up_s": i["L0_ffn_up_s"].reshape(FC, P).T,
        "down_s": i["L0_ffn_down_s"].reshape(1, D),
        "wq1": w_qkv[0:4], "wk1": w_qkv[4:8], "wv1": w_qkv[8:12],
        "bias1": i["L1_attn_b_qkv"].reshape(3, CHUNKS1, P).transpose(2, 0, 1),
        "wo1": i["L1_attn_w_out"].T.reshape(CHUNKS1, P, D),
        "out_bias": i["L1_attn_b_out"].reshape(1, D),
        "router": i["L1_ffn_Wr"].T.reshape(DC, P, EXPERTS).transpose(1, 0, 2),
        "down1": i["L1_ffn_A"].reshape(KR, D).T.reshape(DC, P, KR).transpose(1, 0, 2),
        "up1": i["L1_ffn_B"].transpose(0, 2, 1).reshape(KR // P, P, D).transpose(1, 0, 2),
    }


def kernel(**inputs):
    import concourse.bacc as bacc
    from concourse.bass_utils import run_bass_kernel_spmd

    nc = bacc.Bacc("TRN2", target_bir_lowering=False, num_devices=1)
    arrays, dram = {}, {}
    for name, a in {**lay_out(inputs), **shape_constants()}.items():
        arrays[f"in_{name}"] = np.ascontiguousarray(a)
        dram[name] = nc.dram_tensor(f"in_{name}", a.shape, mybir.dt.from_np(a.dtype), kind="ExternalInput").ap()
    out = nc.dram_tensor("out", (TOK, D), F32, kind="ExternalOutput").ap()
    program(nc, dram, out)
    result = run_bass_kernel_spmd(nc, [arrays], core_ids=[0])
    return result.results[0]["out"].reshape(BATCH, SEQ, D)
```

```python
from contextlib import ExitStack

import numpy as np

import concourse.bass as bass
from concourse import mybir

P = 128
F32 = mybir.dt.float32
F32R = mybir.dt.float32r
I32 = mybir.dt.int32
ALU = mybir.AluOpType
ACT = mybir.ActivationFunctionType

BATCH, SEQ, D = 2, 512, 512
TOK = BATCH * SEQ
NT = TOK // P
DC = D // P
QT = SEQ // P
HEADS0, KV0, HD0 = 32, 8, 128
PER_KV = HEADS0 // KV0
FF = 1792
FC = FF // P
HEADS1, HD1 = 32, 16
EXPERTS, TOPK, RANK = 64, 16, 16
KR = EXPERTS * RANK
EPS = 1e-5
SYS_LEN, IMG_LEN = 35, 72
MASKED = -1.0e30
LOWEST = -3.0e38

SCORE_AT = [P * i * (i + 1) // 2 for i in range(QT + 1)]


class Model:

    def __init__(self, dram, x, ident, xT_hi, xT_lo, ln_loaded, ln_semaphores):
        self.dram, self.x, self.ident = dram, x, ident
        self.xT_hi, self.xT_lo = xT_hi, xT_lo
        self.ln_loaded, self.ln_semaphores = ln_loaded, ln_semaphores


def wait(engine, semaphore, value):
    if isinstance(value, int) and value <= 0:
        return
    engine.wait_ge(semaphore, value)


def product(nc, out, left, right, start, stop):
    nc.tensor.matmul(out, left[0], right[0], start=start, stop=False)
    nc.tensor.matmul(out, left[0], right[1], start=False, stop=False)
    return nc.tensor.matmul(out, left[1], right[0], start=False, stop=stop)


LN_SEMAPHORES = ("consts_in", "stats_done", "moments_done", "var_done", "root_done", "inverse_done", "normal_done",
                 "turned_done", "hi_done", "lo_done")


def layernorm_phase(nc, m, number, load=None):
    name, before, tiles_before = f"ln{number}", number, number * NT
    loaded, sems = m.ln_loaded, m.ln_semaphores
    with ExitStack() as ctx:
        stats = ctx.enter_context(nc.sbuf_tensor(f"{name}_stats", [P, NT, 6], F32))
        moments = ctx.enter_context(nc.sbuf_tensor(f"{name}_moments", [P, NT, 2], F32))
        shifted = ctx.enter_context(nc.sbuf_tensor(f"{name}_shifted", [P, NT], F32))
        deviation = ctx.enter_context(nc.sbuf_tensor(f"{name}_deviation", [P, NT], F32))
        inverse = ctx.enter_context(nc.sbuf_tensor(f"{name}_inverse", [P, NT], F32))
        normal = ctx.enter_context(nc.sbuf_tensor(f"{name}_normal", [P, 2, D], F32))
        turned = ctx.enter_context(nc.psum_tensor(f"{name}_turned", [P, 2, DC, P], F32))

        consts_in, stats_done, moments_done, var_done, root_done, inverse_done, normal_done, turned_done, hi_done, lo_done = sems
        block = ctx.enter_context(nc.Block())

        if load is not None:
            @block.sync
            def _(sp):
                for t in range(NT):
                    sp.dma_start(m.x[:, t, :], load[t * P:(t + 1) * P, :]).then_inc(loaded[t], 16)
                sp.dma_start(m.ident[:], m.dram["ident"]).then_inc(consts_in, 16)

        @block.vector
        def _(dve):
            for t in range(NT):
                if load is not None:
                    dve.wait_ge(loaded[t], 16)
                nc.vector.bn_stats(stats[:, t, :], m.x[:, t, :]).then_inc(stats_done, 1)
            for t in range(NT):
                dve.wait_ge(stats_done, tiles_before + t + 1)
                nc.vector.bn_aggr(moments[:, t, :], stats[:, t, :]).then_inc(moments_done, 1)
            dve.wait_ge(moments_done, tiles_before + NT)
            nc.vector.tensor_scalar(shifted[:], moments[:, :, 1], EPS, None, ALU.add).then_inc(var_done, 1)
            dve.wait_ge(root_done, before + 1)
            nc.vector.reciprocal(inverse[:], deviation[:]).then_inc(inverse_done, 1)
            dve.wait_ge(inverse_done, before + 1)

            def normalise(t):
                if t >= 2:
                    dve.wait_ge(turned_done, tiles_before + t - 1)
                nc.vector.tensor_scalar(normal[:, t % 2, :], m.x[:, t, :], moments[:, t, 0:1], inverse[:, t:t + 1],
                                        ALU.subtract, ALU.mult).then_inc(normal_done, 1)

            normalise(0)
            for t in range(NT):
                if t + 1 < NT:
                    normalise(t + 1)
                dve.wait_ge(hi_done, tiles_before + t + 1)
                nc.vector.tensor_tensor(m.xT_lo[:, :, t * P:(t + 1) * P], turned[:, t % 2],
                                        m.xT_hi[:, :, t * P:(t + 1) * P].bitcast(F32), ALU.subtract).then_inc(lo_done, 1)

        @block.scalar
        def _(act):
            act.wait_ge(var_done, before + 1)
            nc.scalar.activation(deviation[:], shifted[:], ACT.Sqrt).then_inc(root_done, 1)
            for t in range(NT):
                act.wait_ge(turned_done, tiles_before + t + 1)
                nc.scalar.copy(m.xT_hi[:, :, t * P:(t + 1) * P], turned[:, t % 2]).then_inc(hi_done, 1)

        @block.tensor
        def _(pe):
            if load is not None:
                pe.wait_ge(consts_in, 16)
            for t in range(NT):
                pe.wait_ge(normal_done, tiles_before + t + 1)
                if t >= 2:
                    pe.wait_ge(lo_done, tiles_before + t - 1)
                for c in range(DC):
                    last = nc.tensor.transpose(turned[:, t % 2, c], normal[:, t % 2, c * P:(c + 1) * P], m.ident[:])
                last.then_inc(turned_done, 1)


GROUP = 2 * PER_KV
UNITS = KV0 * GROUP
SIDE = {0: "out", 1: "out", 2: "keys", 3: "values", 4: "out", 5: "out", 6: "keys", 7: "values"}

PIECES = [("wo", 0, 2), ("wo", 1, 2), ("wq", 0, 2), ("wo", 2, 3), ("wo", 3, 3), ("wk", 0, 3),
          ("wq", 1, 4), ("wv", 0, 4), ("wq", 2, 5), ("wq", 3, 6)]
FIRST_PIECES = [("wq", 0), ("wk", 0), ("wq", 1), ("wv", 0), ("wq", 2), ("wq", 3)]
SLOTS = 5
PROJECTIONS = [(s, what) for s in range(GROUP) for what in
               ([SIDE[s]] if SIDE[s] != "out" else []) + ["query"]]
ROTATIONS = [x for x in PROJECTIONS if x[1] != "values"]
OUTPUTS = [x for s in range(GROUP) for x in
           ([(s, "out", 0), (s, "out", 1)] if SIDE[s] == "out" else []) + [(s, "attend", 0)]]


def attention0_phase(nc, m):
    dram = m.dram
    with ExitStack() as ctx:
        def sb(what, shape, dt=F32):
            return ctx.enter_context(nc.sbuf_tensor(f"a0_{what}", shape, dt))

        def pair(what, shape):
            return sb(f"{what}_hi", shape, F32R), sb(f"{what}_lo", shape, F32R)

        def sem(what):
            return ctx.enter_context(nc.semaphore(f"a0_{what}"))

        raw = sb("raw", [P, SLOTS, 512])
        zeros = sb("zeros", [P, 512])
        wq = pair("wq", [P, PER_KV, DC, HD0])
        wk = pair("wk", [P, DC, HD0])
        wv = pair("wv", [P, DC, HD0])
        wo = pair("wo", [P, PER_KV, D])
        keys = pair("keys", [P, BATCH, SEQ])
        values_turned = sb("values_turned", [P, SEQ])
        values = pair("values", [P, BATCH, QT, HD0])
        query = pair("query", [P, 4, SEQ])
        cos_q, sin_q = sb("cos_q", [P, SEQ]), sb("sin_q", [P, SEQ])
        cos_k, sin_k = sb("cos_k", [P, SEQ]), sb("sin_k", [P, SEQ])
        causal = sb("causal", [P, SEQ])
        unscale = sb("unscale", [P, P])
        by_cos, by_sin, rotated = sb("by_cos", [P, SEQ]), sb("by_sin", [P, SEQ]), sb("rotated", [P, SEQ])
        first_tile = sb("first_tile", [P, P])
        probs = sb("probs", [P, 2, SCORE_AT[QT]])
        least = sb("least", [P, 2, QT])
        total = sb("total", [P, 2, QT])
        inverse = sb("inverse", [P, 2, QT])
        probsT = pair("probsT", [P, 2, SEQ])
        attended = pair("attended", [P, BATCH, PER_KV, SEQ])

        ps_proj = ctx.enter_context(nc.psum_tensor("a0_ps_proj", [P, 2, 512], F32))
        ps_score = ctx.enter_context(nc.psum_tensor("a0_ps_score", [P, 2, 512], F32))
        ps_turn = ctx.enter_context(nc.psum_tensor("a0_ps_turn", [P, 2, 512], F32))
        ps_out = ctx.enter_context(nc.psum_tensor("a0_ps_out", [P, 2, 512], F32))

        raw_in = [sem(f"raw_in{s}") for s in range(SLOTS)]
        consts_in, zeros_set, wait_passed = sem("consts_in"), sem("zeros_set"), sem("wait_passed")
        piece_hi, piece_split = sem("piece_hi"), sem("piece_split")
        query_made, keys_made, values_made = sem("query_made"), sem("keys_made"), sem("values_made")
        rotation_scaled, rotation_added = sem("rotation_scaled"), sem("rotation_added")
        rotation_hi, rotation_split = sem("rotation_hi"), sem("rotation_split")
        values_copied, values_placed = sem("values_copied"), sem("values_placed")
        values_hi, values_split = sem("values_hi"), sem("values_split")
        score_made, first_scaled, score_masked = sem("score_made"), sem("first_scaled"), sem("score_masked")
        exp_done, total_inverted, probs_ready = sem("exp_done"), sem("total_inverted"), sem("probs_ready")
        turned, turned_hi, turned_split = sem("turned"), sem("turned_hi"), sem("turned_split")
        attend_made, attended_hi, attended_split = sem("attend_made"), sem("attended_hi"), sem("attended_split")
        out_made, out_added = sem("out_made"), sem("out_added")

        def rotation(g, s, what):
            return 10 * g + 4 + ROTATIONS.index((s, what)) + 1

        def query_rotation(g, u):
            return rotation(g, u - 3, "query") if u >= 3 else rotation(g - 1, u + 5, "query")

        def values_count(g, s):
            return 2 * g + (2 if s == 3 else 3)

        def out_count(g, s, half):
            return 8 * g + (2 * s - 4 if s < 2 else 2 * (s - 4)) + half + 1

        def piece_count(g, what, which):
            names = [x[:2] for x in PIECES]
            return len(FIRST_PIECES) + len(PIECES) * g + names.index((what, which)) + 1

        def present(g, s, what):
            if not isinstance(g, int):
                return True
            if what == "query":
                return 0 <= GROUP * g + s + 3 < UNITS
            if what in ("keys", "values"):
                return (g >= 0 if s < 4 else g < KV0 - 1) and g < KV0
            if what == "score":
                return 0 <= GROUP * g + s + 1 < UNITS
            if what == "attend":
                return 0 <= g < KV0
            return (1 <= g if s < 2 else 0 <= g < KV0)

        def projection_bank(g, s, what):
            return PROJECTIONS.index((s, what)) % 2

        def wait_projection_bank(pe, g, s, what):
            at = PROJECTIONS.index((s, what)) - 2
            gb = g if at >= 0 else g - 1
            sb_, before = PROJECTIONS[at]
            if isinstance(gb, int) and (gb < -1 or (gb == -1 and sb_ < 5)):
                return
            if before == "values":
                wait(pe, values_split, values_count(gb, sb_))
            else:
                wait(pe, rotation_scaled, rotation(gb, sb_, before))

        def wait_output_bank(pe, g, s, what, half):
            at = OUTPUTS.index((s, what, half)) - 2
            gb = g
            while True:
                if at < 0:
                    at, gb = at + len(OUTPUTS), gb - 1
                sb_, before, hb = OUTPUTS[at]
                if isinstance(gb, int) and gb < 0:
                    return
                if present(gb, sb_, before):
                    break
                at -= 2
            if before == "out":
                wait(pe, out_added, out_count(gb, sb_, hb))
            else:
                wait(pe, attended_split, GROUP * gb + sb_ + 1)

        block = ctx.enter_context(nc.Block())

        @block.sync
        def _(sp):
            for table, what in ((cos_q, "cos_q"), (sin_q, "sin_q"), (cos_k, "cos_k"), (sin_k, "sin_k"),
                                (causal, "causal"), (unscale, "unscale")):
                sp.dma_start(table[:], dram[what]).then_inc(consts_in, 16)

            def fetch(number, what, which, g):
                slot = number % SLOTS
                src = dram[what][g, which] if what in ("wq", "wo") else dram[what][g]
                sp.dma_start(raw[:, slot, :], src).then_inc(raw_in[slot], 16)

            for c, (what, which) in enumerate(FIRST_PIECES):
                wait(sp, piece_split, c - SLOTS + 1)
                fetch(c, what, which, 0)

            def group(g, last):
                for c, (what, which, _) in enumerate(PIECES):
                    if last and what != "wo":
                        continue
                    number = len(FIRST_PIECES) + c
                    done = len([x for x in PIECES[:c] if x[0] == "wo"]) if last else c
                    if last:
                        wait(sp, piece_split, len(FIRST_PIECES) + len(PIECES) * g + done)
                    else:
                        wait(sp, piece_split, len(PIECES) * g + number - SLOTS + 1)
                    fetch(number, what, which, g if what == "wo" else g + 1)

            with sp.Fori(0, KV0 - 1) as g:
                group(g, False)
            group(KV0 - 1, True)

        @block.gpsimd
        def _(pool):
            nc.gpsimd.memset(zeros[:], 0.0).then_inc(zeros_set, 1)
            pool.wait_ge(zeros_set, 1)
            targets = {"wq": wq, "wk": wk, "wv": wv, "wo": wo}

            def split(number, count, landed, what, which):
                slot = number % SLOTS
                hi, lo = targets[what]
                if what in ("wq", "wo"):
                    hi, lo = hi[:, which], lo[:, which]
                if what == "wo":
                    src = raw[:, slot, :]
                else:
                    src = raw[:, slot, :].rearrange("p (c n) -> p c n", c=DC)
                    if what in ("wk", "wv"):
                        hi, lo = hi[:], lo[:]
                pool.wait_ge(raw_in[slot], 16 * landed)
                zero = zeros[:] if what == "wo" else zeros[:].rearrange("p (c n) -> p c n", c=DC)
                nc.gpsimd.tensor_tensor(hi, src, zero, ALU.add).then_inc(piece_hi, 1)
                pool.wait_ge(piece_hi, count + 1)
                nc.gpsimd.tensor_tensor(lo, src, hi.bitcast(F32), ALU.subtract).then_inc(piece_split, 1)

            def add_rotation(count):
                pool.wait_ge(rotation_scaled, count)
                wait(pool, rotation_split, count - 1)
                nc.gpsimd.tensor_tensor(rotated[:], by_cos[:], by_sin[:], ALU.add).then_inc(rotation_added, 1)

            def free_for(g, what, which):
                if what == "wo":
                    wait(pool, out_made, out_count(g, 1, 1))
                elif what == "wk":
                    wait(pool, keys_made, 2 * g + 2)
                elif what == "wv":
                    wait(pool, values_made, 2 * g + 2)
                else:
                    wait(pool, query_made, GROUP * g + PER_KV + which + 1)

            for c, (what, which) in enumerate(FIRST_PIECES[:3]):
                split(c, c, 1, what, which)
            add_rotation(rotation(-1, 5, "query"))
            for c in (3, 4):
                split(c, c, 1, *FIRST_PIECES[c])
            add_rotation(rotation(-1, 6, "keys"))
            add_rotation(rotation(-1, 6, "query"))
            split(5, 5, 2, *FIRST_PIECES[5])
            add_rotation(rotation(-1, 7, "query"))

            def group(g, last):
                for s in range(GROUP):
                    if SIDE[s] == "keys" and present(g, s, "keys"):
                        add_rotation(rotation(g, s, "keys"))
                    for c, (what, which, step) in enumerate(PIECES):
                        if step != s or (last and what != "wo"):
                            continue
                        number = len(FIRST_PIECES) + c
                        slot = number % SLOTS
                        before = (2 if slot == 0 else 1) + len([x for x in range(c) if (len(FIRST_PIECES) + x) % SLOTS == slot])
                        if last:
                            done = len([x for x in PIECES[:c] if x[0] == "wo"])
                            before = (2 if slot == 0 else 1) + len(
                                [x for x in range(c) if (len(FIRST_PIECES) + x) % SLOTS == slot and PIECES[x][0] == "wo"])
                        else:
                            done = c
                        free_for(g, what, which)
                        split(number, len(FIRST_PIECES) + len(PIECES) * g + done, 2 * g + before + 1, what, which)
                    if present(g, s, "query"):
                        add_rotation(rotation(g, s, "query"))

            group(0, False)
            with pool.Fori(1, KV0 - 1) as g:
                group(g, False)
            group(KV0 - 1, True)

        @block.tensor
        def _(pe):
            def xT(part, c, at, size):
                return part[:, c, at:at + size]

            def make_query(g, s, chunks):
                u = (s + 3) % GROUP
                b, j = u // PER_KV, u % PER_KV
                bank = projection_bank(g, s, "query")
                gq = g if s + 3 < GROUP else g + 1
                if chunks[0] == 0:
                    wait_projection_bank(pe, g, s, "query")
                    wait(pe, piece_split, weights_ready("wq", j, gq))
                for c in chunks:
                    last = product(nc, ps_proj[:, bank, :], (wq[0][:, j, c, :], wq[1][:, j, c, :]),
                                   (xT(m.xT_hi, c, b * SEQ, SEQ), xT(m.xT_lo, c, b * SEQ, SEQ)), c == 0, c == DC - 1)
                if chunks[-1] == DC - 1:
                    last.then_inc(query_made, 1)

            def weights_ready(what, which, g):
                if isinstance(g, int) and g == 0 and what != "wo":
                    return FIRST_PIECES.index((what, which)) + 1
                if what == "wo":
                    if isinstance(g, int) and g == KV0 - 1:
                        return len(FIRST_PIECES) + len(PIECES) * g + which + 1
                    return piece_count(g, what, which)
                return piece_count(g - 1, what, which)

            def make_keys(g, s):
                b = 1 if s < 4 else 0
                bank = projection_bank(g, s, "keys")
                wait_projection_bank(pe, g, s, "keys")
                wait(pe, piece_split, weights_ready("wk", 0, g if b else g + 1))
                for c in range(DC):
                    last = product(nc, ps_proj[:, bank, :], (wk[0][:, c, :], wk[1][:, c, :]),
                                   (xT(m.xT_hi, c, b * SEQ, SEQ), xT(m.xT_lo, c, b * SEQ, SEQ)), c == 0, c == DC - 1)
                last.then_inc(keys_made, 1)

            def make_values(g, s):
                b = 1 if s < 4 else 0
                bank = projection_bank(g, s, "values")
                wait_projection_bank(pe, g, s, "values")
                wait(pe, piece_split, weights_ready("wv", 0, g if b else g + 1))
                for c in range(DC):
                    last = product(nc, ps_proj[:, bank, :], (wv[0][:, c, :], wv[1][:, c, :]),
                                   (xT(m.xT_hi, c, b * SEQ, SEQ), xT(m.xT_lo, c, b * SEQ, SEQ)), c == 0, c == DC - 1)
                last.then_inc(values_made, 1)

            def place_values(g, s):
                wait(pe, values_copied, values_count(g, s))
                for t in range(QT):
                    last = nc.tensor.transpose(ps_proj[:, projection_bank(g, s, "values"), t * P:(t + 1) * P],
                                               values_turned[:, t * P:(t + 1) * P], m.ident[:])
                last.then_inc(values_placed, 1)

            def score(g, s, i):
                u = (s + 1) % GROUP
                gu = g if s + 1 < GROUP else g + 1
                n = GROUP * gu + u
                b = u // PER_KV
                if i == 0:
                    wait(pe, rotation_split, query_rotation(gu, u))
                    if u == 0:
                        wait(pe, rotation_split, rotation(gu - 1, 6, "keys"))
                    elif u == PER_KV:
                        wait(pe, rotation_split, rotation(gu, 2, "keys"))
                wait(pe, score_masked, 4 * n + i - 1)
                q = (query[0][:, u % 4, i * P:(i + 1) * P], query[1][:, u % 4, i * P:(i + 1) * P])
                k = (keys[0][:, b, 0:P * (i + 1)], keys[1][:, b, 0:P * (i + 1)])
                product(nc, ps_score[:, i % 2, 0:P * (i + 1)], q, k, True, True).then_inc(score_made, 1)

            def turn(n, u, t):
                if t == 0:
                    wait(pe, probs_ready, 4 * n + 4)
                wait(pe, turned_split, 4 * n + t - 1)
                for i in range(t, QT):
                    at = SCORE_AT[i] + t * P
                    last = nc.tensor.transpose(ps_turn[:, t % 2, (i - t) * P:(i - t + 1) * P],
                                               probs[:, u % 2, at:at + P], m.ident[:])
                last.then_inc(turned, 1)

            def attend(g, u, t):
                n = GROUP * g + u
                b = u // PER_KV
                bank = OUTPUTS.index((u, "attend", 0)) % 2
                if t == 0:
                    wait_output_bank(pe, g, u, "attend", 0)
                    if u % PER_KV == 0:
                        wait(pe, values_split, 2 * g + b + 1)
                wait(pe, turned_split, 4 * n + t + 1)
                w = SEQ - t * P
                product(nc, ps_out[:, bank, t * P:SEQ], (values[0][:, b, t, :], values[1][:, b, t, :]),
                        (probsT[0][:, t % 2, 0:w], probsT[1][:, t % 2, 0:w]), t == 0, t == QT - 1).then_inc(attend_made, 1)

            def make_out(g, s, half):
                b = 1 if s < 2 else 0
                t = 2 * (s % 4) + half
                bank = OUTPUTS.index((s, "out", half)) % 2
                gw = g - 1 if b else g
                wait_output_bank(pe, g, s, "out", half)
                if half == 0 and s in (0, 4):
                    wait(pe, attended_split, GROUP * gw + PER_KV * (b + 1))
                    wait(pe, piece_split, weights_ready("wo", PER_KV - 1, gw))
                for j in range(PER_KV):
                    at = slice(t * P, (t + 1) * P)
                    last = product(nc, ps_out[:, bank, :], (attended[0][:, b, j, at], attended[1][:, b, j, at]),
                                   (wo[0][:, j, :], wo[1][:, j, :]), j == 0, j == PER_KV - 1)
                last.then_inc(out_made, 1)

            def step(g, s):
                n = GROUP * g + s
                if present(g, s, "score"):
                    score(g, s, 0)
                    score(g, s, 1)
                if present(g, s, "attend"):
                    turn(n, s, 0)
                    turn(n, s, 1)
                if present(g, s, SIDE[s]):
                    if SIDE[s] == "out":
                        make_out(g, s, 0)
                        make_out(g, s, 1)
                    elif SIDE[s] == "keys":
                        make_keys(g, s)
                    else:
                        make_values(g, s)
                if present(g, s, "score"):
                    score(g, s, 2)
                    score(g, s, 3)
                if SIDE[s] == "values" and present(g, s, "values"):
                    place_values(g, s)
                if present(g, s, "query"):
                    make_query(g, s, [0, 1])
                if present(g, s, "attend"):
                    attend(g, s, 0)
                    turn(n, s, 2)
                    attend(g, s, 1)
                    turn(n, s, 3)
                if present(g, s, "query"):
                    make_query(g, s, [2, 3])
                if present(g, s, "attend"):
                    attend(g, s, 2)
                    attend(g, s, 3)

            for s in (5, 6, 7):
                step(-1, s)
            for s in range(GROUP):
                step(0, s)
            with pe.Fori(1, KV0 - 1) as g:
                for s in range(GROUP):
                    step(g, s)
            for s in range(GROUP):
                step(KV0 - 1, s)
            for s in (0, 1):
                step(KV0, s)

        @block.vector
        def _(dve):
            half = P // 2
            dve.wait_ge(consts_in, 16 * 6)

            def mask(g, s, i):
                n = GROUP * g + s + 1
                slot = (s + 1) % 2
                at, w = SCORE_AT[i], P * (i + 1)
                dve.wait_ge(score_made, 4 * n + i + 1)
                if i > 0:
                    dve.sem_inc(wait_passed, 1)
                src = ps_score[:, i % 2, 0:w]
                if i == 0:
                    wait(dve, turned, 4 * (n - 1))
                    nc.vector.tensor_tensor(first_tile[:], src, unscale[:], ALU.mult).then_inc(first_scaled, 1)
                    dve.wait_ge(first_scaled, n + 1)
                    dve.sem_inc(wait_passed, 1)
                    src = first_tile[:]
                nc.vector.tensor_tensor_reduce(
                    out=probs[:, slot, at:at + w], in0=src, in1=causal[:, SEQ - w:SEQ], scale=-float(HD0) ** -0.5,
                    scalar=-LOWEST, op0=ALU.add, op1=ALU.min, accum_out=least[:, slot, i:i + 1]).then_inc(score_masked, 1)

            def split_turned(g, s, t):
                n = GROUP * g + s
                w = SEQ - t * P
                dve.wait_ge(turned_hi, 4 * n + t + 1)
                nc.vector.tensor_tensor(probsT[1][:, t % 2, 0:w], ps_turn[:, t % 2, 0:w],
                                        probsT[0][:, t % 2, 0:w].bitcast(F32), ALU.subtract).then_inc(turned_split, 1)

            def rotate(g, s, what):
                bank = projection_bank(g, s, what)
                src = ps_proj[:, bank, :]
                cos, sin = (cos_q, sin_q) if what == "query" else (cos_k, sin_k)
                if what == "query":
                    dve.wait_ge(query_made, GROUP * g + s + 4)
                else:
                    dve.wait_ge(keys_made, 2 * g + (2 if s == 2 else 3))
                wait(dve, rotation_added, rotation(g, s, what) - 1)
                nc.vector.tensor_tensor(by_cos[:], src, cos[:], ALU.mult)
                nc.vector.tensor_tensor(by_sin[0:half], src[half:P], sin[half:P], ALU.mult)
                nc.vector.tensor_tensor(by_sin[half:P], src[0:half], sin[0:half], ALU.mult).then_inc(rotation_scaled, 1)

            def split_rotated(g, s, what):
                dve.wait_ge(rotation_hi, rotation(g, s, what))
                if what == "query":
                    hi, lo = query[0][:, (s + 3) % 4, :], query[1][:, (s + 3) % 4, :]
                else:
                    b = 1 if s < 4 else 0
                    hi, lo = keys[0][:, b, :], keys[1][:, b, :]
                nc.vector.tensor_tensor(lo, rotated[:], hi.bitcast(F32), ALU.subtract).then_inc(rotation_split, 1)

            def step(g, s):
                n = GROUP * g + s
                if present(g, s, "score"):
                    mask(g, s, 0)
                    mask(g, s, 1)
                if present(g, s, "attend"):
                    split_turned(g, s, 0)
                    split_turned(g, s, 1)
                side = SIDE[s] if present(g, s, SIDE[s]) else None
                if side == "out":
                    b = 1 if s < 2 else 0
                    for h in range(2):
                        t = b * QT + 2 * (s % 4) + h
                        count = out_count(g, s, h)
                        dve.wait_ge(out_made, count)
                        wait(dve, out_added, count - QT)
                        nc.vector.tensor_tensor(m.x[:, t, :], ps_out[:, OUTPUTS.index((s, "out", h)) % 2, :],
                                                m.x[:, t, :], ALU.add).then_inc(out_added, 1)
                elif side == "keys":
                    rotate(g, s, "keys")
                if present(g, s, "score"):
                    mask(g, s, 2)
                    mask(g, s, 3)
                if side == "values":
                    b = 1 if s < 4 else 0
                    dve.wait_ge(values_hi, values_count(g, s))
                    nc.vector.tensor_tensor(values[1][:, b], ps_proj[:, projection_bank(g, s, "values"), :].rearrange(
                        "p (t d) -> p t d", t=QT), values[0][:, b].bitcast(F32), ALU.subtract).then_inc(values_split, 1)
                if side == "keys":
                    split_rotated(g, s, "keys")
                if present(g, s, "attend"):
                    split_turned(g, s, 2)
                if present(g, s, "score"):
                    dve.wait_ge(exp_done, 4 * (n + 1) + 4)
                    nc.vector.reciprocal(inverse[:, (s + 1) % 2, :], total[:, (s + 1) % 2, :]).then_inc(total_inverted, 1)
                if present(g, s, "attend"):
                    split_turned(g, s, 3)
                if present(g, s, "query"):
                    rotate(g, s, "query")
                if present(g, s, "attend"):
                    b, j = s // PER_KV, s % PER_KV
                    dve.wait_ge(attended_hi, n + 1)
                    nc.vector.tensor_tensor(attended[1][:, b, j, :], ps_out[:, OUTPUTS.index((s, "attend", 0)) % 2, :],
                                            attended[0][:, b, j, :].bitcast(F32), ALU.subtract).then_inc(attended_split, 1)
                if present(g, s, "query"):
                    split_rotated(g, s, "query")

            for s in (5, 6, 7):
                step(-1, s)
            for s in range(GROUP):
                step(0, s)
            with dve.Fori(1, KV0 - 1) as g:
                for s in range(GROUP):
                    step(g, s)
            for s in range(GROUP):
                step(KV0 - 1, s)
            for s in (0, 1):
                step(KV0, s)

        @block.scalar
        def _(act):
            def exponent(g, s, i):
                n = GROUP * g + s + 1
                slot = (s + 1) % 2
                tile = probs[:, slot, SCORE_AT[i]:SCORE_AT[i + 1]]
                act.wait_ge(score_masked, 4 * n + i + 1)
                nc.scalar.activation(tile, tile, ACT.Exp, bias=least[:, slot, i:i + 1], scale=-1.0,
                                     accum_out=total[:, slot, i:i + 1]).then_inc(exp_done, 1)

            def round_turned(g, s, t):
                n = GROUP * g + s
                w = SEQ - t * P
                act.wait_ge(turned, 4 * n + t + 1)
                wait(act, attend_made, 4 * n + t - 1)
                nc.scalar.copy(probsT[0][:, t % 2, 0:w], ps_turn[:, t % 2, 0:w]).then_inc(turned_hi, 1)

            def round_rotated(g, s, what):
                act.wait_ge(rotation_added, rotation(g, s, what))
                if what == "query":
                    hi = query[0][:, (s + 3) % 4, :]
                    wait(act, score_made, 4 * (GROUP * g + s + 3 - 4) + 4)
                else:
                    b = 1 if s < 4 else 0
                    hi = keys[0][:, b, :]
                    wait(act, score_made, 4 * GROUP * g if b else 4 * (GROUP * g + PER_KV))
                nc.scalar.copy(hi, rotated[:]).then_inc(rotation_hi, 1)

            def step(g, s):
                n = GROUP * g + s
                if present(g, s, "score"):
                    exponent(g, s, 0)
                    exponent(g, s, 1)
                if present(g, s, "attend"):
                    round_turned(g, s, 0)
                    round_turned(g, s, 1)
                side = SIDE[s] if present(g, s, SIDE[s]) else None
                if side == "values":
                    act.wait_ge(values_made, values_count(g, s))
                    nc.scalar.copy(values_turned[:], ps_proj[:, projection_bank(g, s, "values"), :]).then_inc(values_copied, 1)
                if present(g, s, "score"):
                    exponent(g, s, 2)
                    exponent(g, s, 3)
                if side == "values":
                    b = 1 if s < 4 else 0
                    act.wait_ge(values_placed, values_count(g, s))
                    wait(act, attend_made, 4 * GROUP * g if b else 4 * (GROUP * g + PER_KV))
                    nc.scalar.copy(values[0][:, b], ps_proj[:, projection_bank(g, s, "values"), :].rearrange(
                        "p (t d) -> p t d", t=QT)).then_inc(values_hi, 1)
                if side == "keys":
                    round_rotated(g, s, "keys")
                if present(g, s, "attend"):
                    round_turned(g, s, 2)
                    round_turned(g, s, 3)
                if present(g, s, "score"):
                    slot = (s + 1) % 2
                    act.wait_ge(total_inverted, n + 2)
                    for i in range(QT):
                        tile = probs[:, slot, SCORE_AT[i]:SCORE_AT[i + 1]]
                        nc.scalar.activation(tile, tile, ACT.Copy, scale=inverse[:, slot, i:i + 1]).then_inc(probs_ready, 1)
                if present(g, s, "attend"):
                    b, j = s // PER_KV, s % PER_KV
                    act.wait_ge(attend_made, 4 * n + 4)
                    wait(act, out_made, NT * g if b else NT * g - PER_KV)
                    nc.scalar.copy(attended[0][:, b, j, :],
                                   ps_out[:, OUTPUTS.index((s, "attend", 0)) % 2, :]).then_inc(attended_hi, 1)
                if present(g, s, "query"):
                    round_rotated(g, s, "query")

            for s in (5, 6, 7):
                step(-1, s)
            for s in range(GROUP):
                step(0, s)
            with act.Fori(1, KV0 - 1) as g:
                for s in range(GROUP):
                    step(g, s)
            for s in range(GROUP):
                step(KV0 - 1, s)



def ffn0_phase(nc, m):
    dram = m.dram
    with ExitStack() as ctx:
        def sb(what, shape, dt=F32):
            return ctx.enter_context(nc.sbuf_tensor(f"f0_{what}", shape, dt))

        def pair(what, shape):
            return sb(f"{what}_hi", shape, F32R), sb(f"{what}_lo", shape, F32R)

        def sem(what):
            return ctx.enter_context(nc.semaphore(f"f0_{what}"))

        raw = sb("raw", [P, 2, 3, 512], I32)
        gate = pair("gate", [P, 2, DC, P])
        up = pair("up", [P, 2, DC, P])
        down = pair("down", [P, FC, D])
        gate_s, up_s = sb("gate_s", [P, FC]), sb("up_s", [P, FC])
        down_s = sb("down_s", [P, D])
        gate_col, up_col = sb("gate_col", [P, 2]), sb("up_col", [P, 2])
        silu = sb("silu", [P, 2, SEQ])
        hidden = sb("hidden", [P, 2, SEQ])
        hidden0 = pair("hidden0", [P, 2, SEQ])
        hidden1 = pair("hidden1", [P, FC, SEQ])
        ps_gate = ctx.enter_context(nc.psum_tensor("f0_ps_gate", [P, 2, 512], F32))
        ps_up = ctx.enter_context(nc.psum_tensor("f0_ps_up", [P, 2, 512], F32))
        ps_out = ctx.enter_context(nc.psum_tensor("f0_ps_out", [P, QT, 512], F32))

        raw_in = [[sem(f"{w}_in{s}") for w in ("gate", "up", "down")] for s in range(2)]
        scales_in = sem("scales_in")
        weights_hi, weights_split = sem("weights_hi"), sem("weights_split")
        columns_copied = sem("columns_copied")
        made, silu_done, hidden_made = sem("made"), sem("silu_done"), sem("hidden_made")
        hidden_hi, hidden_split = sem("hidden_hi"), sem("hidden_split")
        summed, out_done, out_scaled, out_added = sem("summed"), sem("out_done"), sem("out_scaled"), sem("out_added")
        block = ctx.enter_context(nc.Block())

        @block.sync
        def _(sp):
            sp.dma_start(gate_s[:], dram["gate_s"]).then_inc(scales_in, 16)
            sp.dma_start(up_s[:], dram["up_s"]).then_inc(scales_in, 16)
            sp.dma_start(down_s[:], dram["down_s"].to_broadcast((P, D))).then_inc(scales_in, 16)

            def fetch(f, k):
                wait(sp, weights_split, 3 * f - 3)
                for w, name in enumerate(("gate", "up", "down")):
                    sp.dma_start(raw[:, k, w, :], dram[name][f]).then_inc(raw_in[k][w], 16)

            fetch(0, 0)
            fetch(1, 1)
            with sp.Fori(1, FC // 2) as i:
                for k in range(2):
                    fetch(2 * i + k, k)

        def split_hi(act, f, k, use):
            for w, hi in enumerate((gate[0][:, k], up[0][:, k], down[0][:, f, :])):
                act.wait_ge(raw_in[k][w], 16 * use)
                if w == 0:
                    wait(act, made, 2 * f - 2)
                src = raw[:, k, w, :]
                if w < 2:
                    src = src.rearrange("p (c n) -> p c n", c=DC)
                nc.scalar.copy(hi, src).then_inc(weights_hi, 1)

        def split_lo(dve, f, k):
            for w, (hi, lo) in enumerate(((gate[0][:, k], gate[1][:, k]), (up[0][:, k], up[1][:, k]),
                                          (down[0][:, f, :], down[1][:, f, :]))):
                src = raw[:, k, w, :]
                if w < 2:
                    src = src.rearrange("p (c n) -> p c n", c=DC)
                dve.wait_ge(weights_hi, 3 * f + w + 1)
                nc.vector.tensor_tensor(lo, src, hi.bitcast(F32), ALU.subtract).then_inc(weights_split, 1)

        @block.scalar
        def _(act):
            split_hi(act, 0, 0, 1)

            def chunk(f, k, use, last=False):
                if not last:
                    split_hi(act, f + 1, 1 - k, use + k)
                for b in range(BATCH):
                    q = 2 * f + b
                    act.wait_ge(columns_copied, f + 1)
                    act.wait_ge(made, q + 1)
                    wait(act, hidden_made, q - 1)
                    nc.scalar.activation(silu[:, b, :], ps_gate[:, b, :], ACT.Silu,
                                         scale=gate_col[:, k:k + 1]).then_inc(silu_done, 1)
                    act.wait_ge(hidden_made, q + 1)
                    if b == 0:
                        wait(act, summed, f - 1)
                        hi = hidden0[0][:, k, :]
                    else:
                        hi = hidden1[0][:, f, :]
                    nc.scalar.copy(hi, hidden[:, b, :]).then_inc(hidden_hi, 1)

            chunk(0, 0, 1)
            chunk(1, 1, 1)
            with act.Fori(1, FC // 2 - 1) as i:
                for k in range(2):
                    chunk(2 * i + k, k, i + 1)
            chunk(FC - 2, 0, FC // 2)
            chunk(FC - 1, 1, FC // 2, last=True)

        @block.vector
        def _(dve):
            dve.wait_ge(scales_in, 48)

            def copy_columns(f, k):
                wait(dve, hidden_made, 2 * f - 2)
                nc.vector.tensor_copy(gate_col[:, k:k + 1], gate_s[:, bass.ds(f, 1)])
                nc.vector.tensor_copy(up_col[:, k:k + 1], up_s[:, bass.ds(f, 1)]).then_inc(columns_copied, 1)

            copy_columns(0, 0)
            split_lo(dve, 0, 0)

            def chunk(f, k, last=False):
                if not last:
                    copy_columns(f + 1, 1 - k)
                    split_lo(dve, f + 1, 1 - k)
                for b in range(BATCH):
                    q = 2 * f + b
                    dve.wait_ge(columns_copied, f + 1)
                    dve.wait_ge(silu_done, q + 1)
                    wait(dve, hidden_split, q - 1)
                    nc.vector.scalar_tensor_tensor(hidden[:, b, :], ps_up[:, b, :], up_col[:, k:k + 1], silu[:, b, :],
                                                   ALU.mult, ALU.mult).then_inc(hidden_made, 1)
                    hi, lo = (hidden0[0][:, k, :], hidden0[1][:, k, :]) if b == 0 else \
                             (hidden1[0][:, f, :], hidden1[1][:, f, :])
                    dve.wait_ge(hidden_hi, q + 1)
                    nc.vector.tensor_tensor(lo, hidden[:, b, :], hi.bitcast(F32), ALU.subtract).then_inc(hidden_split, 1)

            for f in range(2):
                chunk(f, f)
            with dve.Fori(1, FC // 2 - 1) as i:
                for k in range(2):
                    chunk(2 * i + k, k)
            chunk(FC - 2, 0)
            chunk(FC - 1, 1, last=True)
            for t in range(NT):
                dve.wait_ge(out_done, t + 1)
                nc.vector.tensor_tensor(hidden[:, t % 2, :], ps_out[:, t % QT, :], down_s[:], ALU.mult).then_inc(out_scaled, 1)
                dve.wait_ge(out_scaled, t + 1)
                nc.vector.tensor_tensor(m.x[:, t, :], m.x[:, t, :], hidden[:, t % 2, :], ALU.add).then_inc(out_added, 1)
            dve.wait_ge(out_added, NT)

        @block.tensor
        def _(pe):
            def make(f, k, b):
                q = 2 * f + b
                if b == 0:
                    pe.wait_ge(weights_split, 3 * f + 3)
                wait(pe, hidden_made, q - 1)
                for out, w in ((ps_gate, gate), (ps_up, up)):
                    for c in range(DC):
                        at = slice(b * SEQ, (b + 1) * SEQ)
                        last = product(nc, out[:, b, :], (w[0][:, k, c, :], w[1][:, k, c, :]),
                                       (m.xT_hi[:, c, at], m.xT_lo[:, c, at]), c == 0, c == DC - 1)
                last.then_inc(made, 1)

            def add_to_sums(f, k, first=False, last=False):
                pe.wait_ge(hidden_split, 2 * f + 1)
                for t in range(QT):
                    at = slice(t * P, (t + 1) * P)
                    mm = product(nc, ps_out[:, t, :], (hidden0[0][:, k, at], hidden0[1][:, k, at]),
                                 (down[0][:, f, :], down[1][:, f, :]), first, last)
                    if last:
                        mm.then_inc(out_done, 1)
                    elif t == QT - 1:
                        mm.then_inc(summed, 1)

            make(0, 0, 0)
            make(0, 0, 1)
            make(1, 1, 0)
            add_to_sums(0, 0, first=True)
            make(1, 1, 1)
            with pe.Fori(1, FC // 2) as i:
                for k in range(2):
                    make(2 * i + k, k, 0)
                    add_to_sums(2 * i + k - 1, 1 - k)
                    make(2 * i + k, k, 1)
            add_to_sums(FC - 1, 1, last=True)
            pe.wait_ge(hidden_split, 2 * FC)
            for t in range(QT):
                at = slice(t * P, (t + 1) * P)
                pe.wait_ge(out_scaled, t + 1)
                for f in range(FC):
                    mm = product(nc, ps_out[:, t, :], (hidden1[0][:, f, at], hidden1[1][:, f, at]),
                                 (down[0][:, f, :], down[1][:, f, :]), f == 0, f == FC - 1)
                mm.then_inc(out_done, 1)


HPC = P // HD1
CHUNKS1 = HEADS1 // HPC
STEPS1 = 2 * HPC
UNITS1 = CHUNKS1 * STEPS1
PAIRS = HPC // 2
TURNED_AT = [0, SEQ, 2 * SEQ - P]
TURNED_WIDTH = [SEQ, SEQ - P, SEQ - P]
KEY_AT = [0, SEQ, 2 * SEQ - P, 3 * SEQ - 3 * P]
SIDE1 = {0: "keys", 1: "values", 2: "spread", 3: "out", 4: "out", 5: "out", 6: "out", 7: "query"}


def attention1_phase(nc, m):
    dram = m.dram
    with ExitStack() as ctx:
        def sb(what, shape, dt=F32):
            return ctx.enter_context(nc.sbuf_tensor(f"a1_{what}", shape, dt))

        def pair(what, shape):
            return sb(f"{what}_hi", shape, F32R), sb(f"{what}_lo", shape, F32R)

        def sem(what):
            return ctx.enter_context(nc.semaphore(f"a1_{what}"))

        raw = sb("raw", [P, 4, 512])
        zeros = sb("zeros", [P, 512])
        wq, wk, wv = pair("wq", [P, DC, P]), pair("wk", [P, DC, P]), pair("wv", [P, DC, P])
        wo = pair("wo", [P, D])
        bias = sb("bias", [P, 3, CHUNKS1])
        value_bias = sb("value_bias", [P, 1])
        out_bias = sb("out_bias", [P, D])
        biased_q, biased_k = sb("biased_q", [P, SEQ]), sb("biased_k", [P, SEQ])
        query, keys = pair("query", [P, SEQ]), pair("keys", [P, SEQ])
        stacked_q = sb("stacked_q", [P, BATCH, PAIRS, 2, SEQ], F32R)
        stacked_k = sb("stacked_k", [P, BATCH, PAIRS, SEQ], F32R)
        values_turned = sb("values_turned", [P, SEQ])
        values = sb("values", [P, BATCH, QT, HPC, 2, HD1], F32R)
        causal = sb("causal", [P, SEQ])
        probs = sb("probs", [P, 2, SCORE_AT[QT]])
        least = sb("least", [P, 2, QT])
        total = sb("total", [P, 2, QT, 4])
        inverse = sb("inverse", [P, QT, 4])
        probsT = pair("probsT", [P, 2, SCORE_AT[QT]])
        gathered = sb("gathered", [P, SEQ])
        summed = sb("summed", [P, QT, 4, HD1])
        result = sb("result", [P, QT, HPC, HD1])
        attended = pair("attended", [P, SEQ])

        ps_score = ctx.enter_context(nc.psum_tensor("a1_ps_score", [P, 2, 512], F32))
        ps_turn = ctx.enter_context(nc.psum_tensor("a1_ps_turn", [P, 3, 512], F32))
        ps_attend = ctx.enter_context(nc.psum_tensor("a1_ps_attend", [P, SEQ], F32))
        ps_back = ctx.enter_context(nc.psum_tensor("a1_ps_back", [P, QT, P], F32))
        ps_side = ctx.enter_context(nc.psum_tensor("a1_ps_side", [P, 512], F32))

        raw_in = [sem(f"{w}_in") for w in ("wq", "wk", "wv", "wo")]
        query_out, keys_out, stacked_q_in, stacked_k_in = sem("query_out"), sem("keys_out"), sem("stacked_q_in"), sem("stacked_k_in")
        consts_in, pick_in, zeros_set, stack_zero = sem("consts_in"), sem("pick_in"), sem("zeros_set"), sem("stack_zero")
        wait_passed, wait_passed_sp = sem("wait_passed"), sem("wait_passed_sp")
        wait_passed_pool = sem("wait_passed_pool")
        piece_hi, piece_split = sem("piece_hi"), sem("piece_split")
        side_made, side_read = sem("side_made"), sem("side_read")
        operand_hi, operand_split, values_hi = sem("operand_hi"), sem("operand_split"), sem("values_hi")
        score_made, score_masked, exp_done = sem("score_made"), sem("score_masked"), sem("exp_done")
        turned, turned_hi, turned_split, attend_made = sem("turned"), sem("turned_hi"), sem("turned_split"), sem("attend_made")
        total_inverted, attend_summed, result_made = sem("total_inverted"), sem("attend_summed"), sem("result_made")
        value_bias_set, attended_hi, bias_added = sem("value_bias_set"), sem("attended_hi"), sem("bias_added")
        attend_read, gathered_turned = sem("attend_read"), sem("gathered_turned")
        result_turned, attended_split = sem("result_turned"), sem("attended_split")

        def side(c, s):
            what = SIDE1[s % 8]
            if not isinstance(c, int):
                return what
            if what == "out":
                there = 1 <= c if s < 8 else 0 <= c < CHUNKS1
            elif what == "query" or s >= 8:
                there = c < CHUNKS1 - 1
            else:
                there = 0 <= c < CHUNKS1
            return what if there else None

        def side_count(c, s):
            if not isinstance(c, int):
                return STEPS1 * c + s + 2
            steps = [(-1, k) for k in range(7, STEPS1)] + [(d, k) for d in range(CHUNKS1 + 1) for k in range(8 if d == CHUNKS1 else STEPS1)]
            return len([x for x in steps if side(*x) and x <= (c, s)])

        def earlier(c, s, steps):
            c, s = (c, s - steps) if s >= steps else (c - 1, s - steps + STEPS1)
            return c, s, side(c, s)

        def period(c, s):
            return 2 * c + {"keys": 1, "values": 1, "spread": 1, "query": 2, "out": -1}[SIDE1[s % 8]] + s // 8

        def batch_of(s):
            return (1 if SIDE1[s % 8] != "query" else 0) ^ s // 8

        def operand_count(c, s):
            return 3 + 4 * c + {0: 1, 7: 2, 8: 3, 15: 4}[s]

        def piece_count(c, what):
            if what == "wo":
                return 3 + 4 * c + (1 if isinstance(c, int) and c == CHUNKS1 - 1 else 4)
            at = ("wq", "wk", "wv").index(what)
            return at + 1 if isinstance(c, int) and c == 0 else 3 + 4 * (c - 1) + at + 1

        def unit(c, s, ahead):
            c, u = (c, s + ahead) if s + ahead < STEPS1 else (c + 1, s + ahead - STEPS1)
            return (c, u) if not isinstance(c, int) or 0 <= c < CHUNKS1 else None

        def result_period(c, s):
            return 2 * c - 1 + s // 8 if s % 8 == 1 and (not isinstance(c, int) or (1 <= c if s < 8 else 0 <= c < CHUNKS1)) else None

        def each_chunk(engine, step):
            for s in range(7, STEPS1):
                step(-1, s)
            for s in range(STEPS1):
                step(0, s)
            with engine.Fori(1, CHUNKS1 - 1) as c:
                for s in range(STEPS1):
                    step(c, s)
            for s in range(STEPS1):
                step(CHUNKS1 - 1, s)
            for s in range(8):
                step(CHUNKS1, s)

        DMAS_Q, DMAS_K = 6, 4
        spill_q = nc.dram_tensor("a1_spill_q", (BATCH, 2, P, SEQ), F32).ap()
        spill_k = nc.dram_tensor("a1_spill_k", (BATCH, 2, P, SEQ), F32).ap()
        block = ctx.enter_context(nc.Block())

        @block.sync
        def _(sp):
            for w, name in enumerate(("wq1", "wk1", "wv1")):
                sp.dma_start(raw[:, w, :], dram[name][0]).then_inc(raw_in[w], 16)
            for dst, src in ((bias[:], dram["bias1"]), (causal[:], dram["causal"]),
                             (out_bias[:], dram["out_bias"].to_broadcast((P, D)))):
                sp.dma_start(dst, src).then_inc(consts_in, 16)
            sp.dma_start(raw[:, 3, :], dram["wo1"][0]).then_inc(raw_in[3], 16)

            def write_out(c, s):
                what, b = SIDE1[s % 8], batch_of(s)
                wait(sp, operand_split, operand_count(c, s))
                sp.sem_inc(wait_passed_sp, 1)
                if what == "query":
                    wait(sp, stacked_q_in, 16 * DMAS_Q * (period(c, s) - 1))
                else:
                    wait(sp, stacked_k_in, 16 * DMAS_K * (period(c, s) - 1))
                for part in range(2):
                    src, dst, done = (query, spill_q, query_out) if what == "query" else (keys, spill_k, keys_out)
                    sp.dma_start(dst[b, part], src[part][:].bitcast(F32)).then_inc(done, 16)

            def load(c, what, of):
                w = ("wq", "wk", "wv", "wo").index(what)
                wait(sp, piece_split, piece_count(of - 1, what))
                sp.sem_inc(wait_passed_sp, 1)
                sp.dma_start(raw[:, w, :], dram[what + "1"][of]).then_inc(raw_in[w], 16)

            def chunk(c):
                write_out(c, 0)
                if not isinstance(c, int) or c < CHUNKS1 - 1:
                    for what in ("wq", "wk", "wv"):
                        load(c, what, c + 1)
                if not isinstance(c, int) or c > 0:
                    load(c, "wo", c)
                if not isinstance(c, int) or c < CHUNKS1 - 1:
                    for s in (7, 8, 15):
                        write_out(c, s)

            for s in (7, 8, 15):
                write_out(-1, s)
            chunk(0)
            with sp.Fori(1, CHUNKS1 - 1) as c:
                chunk(c)
            chunk(CHUNKS1 - 1)

        @block.gpsimd
        def _(pool):
            nc.gpsimd.memset(zeros[:], 0.0).then_inc(zeros_set, 1)
            pool.dma_start(stacked_q[96:P].rearrange("p b a e n -> p (b a e n)"), dram["pick"]).then_inc(pick_in, 16)
            pool.wait_ge(zeros_set, 1)

            def read_back(c, s):
                what, b = SIDE1[s % 8], batch_of(s)
                p = period(c, s)
                wait(pool, score_made, 4 * HPC * (p - 1))
                wait(pool, query_out if what == "query" else keys_out, 2 * 16 * (p + 1))
                pool.sem_inc(wait_passed_pool, 1)
                if what == "query":
                    for place, part in enumerate((0, 0, 1)):
                        for e in range(2):
                            rows = spill_q[b, part].rearrange("(a e d) n -> e d a n", a=PAIRS, e=2)
                            at = 32 * place + HD1 * e
                            pool.dma_start(stacked_q[at:at + HD1, b, :, e, :], rows[e]).then_inc(stacked_q_in, 16)
                else:
                    for place, part in enumerate((0, 1, 0)):
                        rows = spill_k[b, part].rearrange("(a r) n -> r a n", a=PAIRS)
                        pool.dma_start(stacked_k[32 * place:32 * place + 32, b], rows).then_inc(stacked_k_in, 16)
                    pool.dma_start(stacked_k[96:P, b].rearrange("p a n -> p (a n)"),
                                   dram["slope"][c if s < 8 else c + 1]).then_inc(stacked_k_in, 16)

            def split(landed, count, what):
                w = ("wq", "wk", "wv", "wo").index(what)
                pair_ = (wq, wk, wv, wo)[w]
                src, zero = raw[:, w, :], zeros[:]
                if what != "wo":
                    src, zero = (x.rearrange("p (c n) -> p c n", c=DC) for x in (src, zero))
                pool.wait_ge(raw_in[w], 16 * landed)
                nc.gpsimd.tensor_tensor(pair_[0][:], src, zero, ALU.add).then_inc(piece_hi, 1)
                pool.wait_ge(piece_hi, count)
                nc.gpsimd.tensor_tensor(pair_[1][:], src, pair_[0][:].bitcast(F32), ALU.subtract).then_inc(piece_split, 1)

            def chunk(c):
                more = not isinstance(c, int) or c < CHUNKS1 - 1
                if more:
                    wait(pool, side_made, side_count(c - 1, 15))
                    split(c + 2, piece_count(c + 1, "wq"), "wq")
                read_back(c, 0)
                if more:
                    for what, s in (("wk", 0), ("wv", 1)):
                        wait(pool, side_made, side_count(c, s))
                        split(c + 2, piece_count(c + 1, what), what)
                wait(pool, side_made, side_count(c, 6))
                split(c + 1, piece_count(c, "wo"), "wo")
                if more:
                    for s in (7, 8, 15):
                        read_back(c, s)

            for what in ("wq", "wk", "wv"):
                split(1, piece_count(0, what), what)
            pool.wait_ge(stack_zero, 1)
            for s in (7, 8, 15):
                read_back(-1, s)
            chunk(0)
            with pool.Fori(1, CHUNKS1 - 1) as c:
                chunk(c)
            chunk(CHUNKS1 - 1)

        @block.tensor
        def _(pe):
            def side_work(c, s):
                what, b = side(c, s), batch_of(s)
                if what in ("query", "keys", "values"):
                    w = {"query": wq, "keys": wk, "values": wv}[what]
                    of = c + 1 if what == "query" or s >= 8 else c
                    wait(pe, piece_split, piece_count(of, {"query": "wq", "keys": "wk", "values": "wv"}[what]))
                elif what == "out":
                    wait(pe, attended_split, period(c, s) + 1)
                    wait(pe, piece_split, piece_count(c if s >= 8 else c - 1, "wo"))
                wait(pe, side_read, side_count(c, s) - 1)
                at = slice(b * SEQ, (b + 1) * SEQ)
                if what in ("query", "keys", "values"):
                    for k in range(DC):
                        last = product(nc, ps_side[:], [x[:, k, :] for x in w],
                                       (m.xT_hi[:, k, at], m.xT_lo[:, k, at]), k == 0, k == DC - 1)
                elif what == "spread":
                    for t in range(QT):
                        last = nc.tensor.transpose(ps_side[:, t * P:(t + 1) * P], values_turned[:, t * P:(t + 1) * P], m.ident[:])
                else:
                    t = s % 8 - 3
                    last = product(nc, ps_side[:], [x[:, t * P:(t + 1) * P] for x in attended], [x[:] for x in wo], True, True)
                last.then_inc(side_made, 1)

            def score(cu, u, i):
                n, b, j = STEPS1 * cu + u, u // HPC, u % HPC
                if i == 0 and j == 0:
                    wait(pe, stacked_q_in, 16 * DMAS_Q * (2 * cu + b + 1))
                    wait(pe, stacked_k_in, 16 * DMAS_K * (2 * cu + b + 1))
                wait(pe, score_masked, 4 * n + i - 1)
                nc.tensor.matmul(ps_score[:, i % 2, 0:P * (i + 1)], stacked_q[:, b, j // 2, j % 2, i * P:(i + 1) * P],
                                 stacked_k[:, b, j // 2, 0:P * (i + 1)], start=True, stop=True).then_inc(score_made, 1)

            def turn(cu, u, t):
                n = STEPS1 * cu + u
                if t == 0:
                    wait(pe, exp_done, 4 * n + 4)
                wait(pe, turned_split, 3 * n - 2 + t)
                for k in ((t,) if t < 2 else (2, 3)):
                    for i in range(k, QT):
                        at = SCORE_AT[i] + k * P
                        to = KEY_AT[k] - TURNED_AT[t] + (i - k) * P
                        last = nc.tensor.transpose(ps_turn[:, t, to:to + P], probs[:, u % 2, at:at + P], m.ident[:])
                last.then_inc(turned, 1)

            def attend(cu, u, part):
                n, b, j = STEPS1 * cu + u, u // HPC, u % HPC
                if part == 0:
                    if j == 0:
                        wait(pe, side_read, side_count(cu, 2) if b else side_count(cu - 1, 10))
                    wait(pe, attend_read, n)
                    wait(pe, turned_split, 3 * n + 3)
                for k in range(QT):
                    last = nc.tensor.matmul(
                        ps_attend[0:2 * HD1, k * P:SEQ], values[:, b, k, j].rearrange("p h d -> p (h d)"),
                        probsT[part][:, u % 2, KEY_AT[k]:KEY_AT[k] + SEQ - k * P],
                        start=part == 0 and k == 0, stop=part == 1 and k == QT - 1)
                if part == 1:
                    last.then_inc(attend_made, 1)

            def turn_gathered(cu, u):
                four = 4 * cu + u // 4
                wait(pe, attend_read, STEPS1 * cu + u + 1)
                if u // 4 % 2 == 0:
                    wait(pe, attended_split, 2 * cu + u // HPC)
                else:
                    wait(pe, result_made, four)
                for t in range(QT):
                    last = nc.tensor.transpose(ps_back[:, t], gathered[:, t * P:(t + 1) * P], m.ident[:])
                last.then_inc(gathered_turned, 1)

            def turn_result(p):
                wait(pe, result_made, 2 * p + 2)
                for t in range(QT):
                    last = nc.tensor.transpose(ps_back[:, t], result[:, t].rearrange("p j d -> p (j d)"), m.ident[:])
                last.then_inc(result_turned, 1)

            pe.wait_ge(pick_in, 16)

            def step(c, s):
                scoring, turning, attending = unit(c, s, 2), unit(c, s, 1), unit(c, s, 0)
                if turning:
                    turn(*turning, 0)
                    turn(*turning, 1)
                if scoring:
                    score(*scoring, 0)
                    score(*scoring, 1)
                if turning:
                    turn(*turning, 2)
                if attending:
                    attend(*attending, 0)
                if scoring:
                    score(*scoring, 2)
                    score(*scoring, 3)
                if attending:
                    attend(*attending, 1)
                if s % 4 == 0 and unit(*earlier(c, s, 1)[:2], 0):
                    turn_gathered(*earlier(c, s, 1)[:2])
                if result_period(c, s) is not None:
                    turn_result(result_period(c, s))
                if side(c, s):
                    side_work(c, s)

            each_chunk(pe, step)

        @block.vector
        def _(dve):
            nc.vector.memset(stacked_q[0:96].rearrange("p b a e n -> p (b a e n)").bitcast(F32), 0.0).then_inc(stack_zero, 1)
            dve.wait_ge(consts_in, 16 * 3)
            for t in range(NT):
                nc.vector.tensor_tensor(m.x[:, t, :], m.x[:, t, :], out_bias[:], ALU.add).then_inc(bias_added, 1)
            dve.wait_ge(bias_added, NT)

            def add_bias(c, s):
                what = side(c, s)
                of = c + 1 if what == "query" or s >= 8 else c
                add = bias[:, 0 if what == "query" else 1, bass.ds(of, 1)]
                dve.wait_ge(side_made, side_count(c, s))
                wait(dve, operand_split, operand_count(c, s) - 2)
                if what == "query":
                    nc.vector.tensor_scalar(biased_q[:], ps_side[:], add, None, ALU.add).then_inc(side_read, 1)
                else:
                    nc.vector.tensor_scalar(biased_k[:], ps_side[:], add, None, ALU.add).then_inc(side_read, 1)

            def split_operand(c, s):
                src, (hi, lo) = (biased_q, query) if side(c, s) == "query" else (biased_k, keys)
                dve.wait_ge(operand_hi, operand_count(c, s))
                nc.vector.tensor_tensor(lo[:], src[:], hi[:].bitcast(F32), ALU.subtract).then_inc(operand_split, 1)

            def mask(cu, u, i):
                n = STEPS1 * cu + u
                at, w = SCORE_AT[i], P * (i + 1)
                if i == 0:
                    wait(dve, turned, 3 * (n - 1))
                dve.wait_ge(score_made, 4 * n + i + 1)
                dve.sem_inc(wait_passed, 1)
                nc.vector.tensor_tensor_reduce(
                    out=probs[:, u % 2, at:at + w], in0=ps_score[:, i % 2, 0:w], in1=causal[:, SEQ - w:SEQ],
                    scale=-float(HD1) ** -0.5, scalar=-LOWEST, op0=ALU.add, op1=ALU.min,
                    accum_out=least[:, u % 2, i:i + 1]).then_inc(score_masked, 1)

            def split_turned(cu, u, t):
                at = slice(TURNED_AT[t], TURNED_AT[t] + TURNED_WIDTH[t])
                dve.wait_ge(turned_hi, 3 * (STEPS1 * cu + u) + t + 1)
                nc.vector.tensor_tensor(probsT[1][:, u % 2, at], ps_turn[:, t, 0:TURNED_WIDTH[t]],
                                        probsT[0][:, u % 2, at].bitcast(F32), ALU.subtract).then_inc(turned_split, 1)

            def divide(cu, u):
                half, count = u // 4 % 2, 4 * cu + u // 4 + 1
                wait(dve, gathered_turned, count)
                nc.vector.reciprocal(inverse[:], total[:, half]).then_inc(total_inverted, 1)
                nc.vector.tensor_reduce(summed[:].rearrange("p i j d -> p (i j) d"),
                                        ps_back[:].rearrange("p i (j h d) -> p (i j) d h", j=4, h=2),
                                        mybir.AxisListType.X, ALU.add).then_inc(attend_summed, 1)
                dve.wait_ge(total_inverted, count)
                dve.wait_ge(attend_summed, count)
                nc.vector.tensor_tensor(result[:, :, 4 * half:4 * half + 4, :], summed[:],
                                        inverse[:].unsqueeze(3).to_broadcast((P, QT, 4, HD1)), ALU.mult).then_inc(result_made, 1)

            def step(c, s):
                scoring, turning = unit(c, s, 2), unit(c, s, 1)
                c1, s1, side1 = earlier(c, s, 1)
                c2, s2, side2 = earlier(c, s, 2)
                if s == 5 and unit(c, s, 0):
                    wait(dve, attended_split, 2 * c)
                    nc.vector.tensor_copy(value_bias[:], bias[:, 2, bass.ds(c, 1)]).then_inc(value_bias_set, 1)
                if s % 4 == 1 and unit(c2, s2, 0):
                    divide(c2, s2)
                if side1 in ("query", "keys"):
                    add_bias(c1, s1)
                elif side1 == "out":
                    t = QT * batch_of(s1) + s1 % 8 - 3
                    dve.wait_ge(side_made, side_count(c1, s1))
                    wait(dve, side_read, side_count(c1, s1) - 1)
                    nc.vector.tensor_tensor(m.x[:, t, :], ps_side[:], m.x[:, t, :], ALU.add).then_inc(side_read, 1)
                if side2 in ("query", "keys"):
                    split_operand(c2, s2)
                if scoring:
                    mask(*scoring, 0)
                    mask(*scoring, 1)
                if turning:
                    split_turned(*turning, 0)
                    split_turned(*turning, 1)
                if side1 == "spread":
                    b = batch_of(s1)
                    dve.wait_ge(values_hi, period(c1, s1) + 1)
                    heads = values[:, b].rearrange("p t j h d -> p (t j) h d")
                    nc.vector.tensor_tensor(heads[:, :, 1, :], ps_side[:].rearrange("p (n d) -> p n d", d=HD1),
                                            heads[:, :, 0, :].bitcast(F32), ALU.subtract).then_inc(side_read, 1)
                if result_period(c1, s1) is not None:
                    p = result_period(c1, s1)
                    dve.wait_ge(value_bias_set, c1 + 1 if s1 >= 8 else c1)
                    dve.wait_ge(attended_hi, p + 1)
                    nc.vector.scalar_tensor_tensor(attended[1][:], ps_back[:].rearrange("p t n -> p (t n)"), value_bias[:],
                                                   attended[0][:].bitcast(F32), ALU.add, ALU.subtract).then_inc(attended_split, 1)
                if scoring:
                    mask(*scoring, 2)
                    mask(*scoring, 3)
                if turning:
                    split_turned(*turning, 2)

            each_chunk(dve, step)

        @block.scalar
        def _(act):
            act.wait_ge(consts_in, 16 * 3)

            def exponent(cu, u, i):
                n = STEPS1 * cu + u
                tile = probs[:, u % 2, SCORE_AT[i]:SCORE_AT[i + 1]]
                if i == 0 and u % 4 == 0:
                    wait(act, total_inverted, 4 * cu + u // 4 - 1)
                act.wait_ge(score_masked, 4 * n + i + 1)
                nc.scalar.activation(tile, tile, ACT.Exp, bias=least[:, u % 2, i:i + 1], scale=-1.0,
                                     accum_out=total[:, u // 4 % 2, i, u % 4:u % 4 + 1]).then_inc(exp_done, 1)

            def round_turned(cu, u, t):
                n = STEPS1 * cu + u
                at = slice(TURNED_AT[t], TURNED_AT[t] + TURNED_WIDTH[t])
                if t == 0:
                    wait(act, attend_made, n - 1)
                act.wait_ge(turned, 3 * n + t + 1)
                nc.scalar.copy(probsT[0][:, u % 2, at], ps_turn[:, t, 0:TURNED_WIDTH[t]]).then_inc(turned_hi, 1)

            def gather(cu, u):
                rows, four = slice(32 * (u % 4), 32 * (u % 4) + 32), 4 * cu + u // 4
                if u % 4 == 0:
                    wait(act, gathered_turned, four)
                act.wait_ge(attend_made, STEPS1 * cu + u + 1)
                nc.scalar.copy(gathered[rows], ps_attend[0:2 * HD1]).then_inc(attend_read, 1)

            def round_operand(c, s):
                what = side(c, s)
                src, hi = (biased_q, query[0]) if what == "query" else (biased_k, keys[0])
                wait(act, query_out if what == "query" else keys_out, 2 * 16 * period(c, s))
                act.wait_ge(side_read, side_count(c, s))
                nc.scalar.copy(hi[:], src[:]).then_inc(operand_hi, 1)

            def step(c, s):
                scoring, turning = unit(c, s, 2), unit(c, s, 1)
                c1, s1, side1 = earlier(c, s, 1)
                if turning:
                    for t in range(3):
                        round_turned(*turning, t)
                if side1 == "values":
                    act.wait_ge(side_made, side_count(c1, s1))
                    nc.scalar.copy(values_turned[:], ps_side[:]).then_inc(side_read, 1)
                elif side1 == "spread":
                    act.wait_ge(side_made, side_count(c1, s1))
                    heads = values[:, batch_of(s1)].rearrange("p t j h d -> p (t j) h d")
                    nc.scalar.copy(heads[:, :, 0, :], ps_side[:].rearrange("p (n d) -> p n d", d=HD1)).then_inc(values_hi, 1)
                if result_period(c1, s1) is not None:
                    act.wait_ge(value_bias_set, c1 + 1 if s1 >= 8 else c1)
                    act.wait_ge(result_turned, result_period(c1, s1) + 1)
                    nc.scalar.activation(attended[0][:], ps_back[:].rearrange("p t n -> p (t n)"), ACT.Identity,
                                         bias=value_bias[:]).then_inc(attended_hi, 1)
                if scoring:
                    for t in range(QT):
                        exponent(*scoring, t)
                if unit(c, s, 0):
                    gather(c, s)
                if side1 in ("query", "keys"):
                    round_operand(c1, s1)

            each_chunk(act, step)



def moe_phase(nc, m, out):
    dram = m.dram
    with ExitStack() as ctx:
        def sb(what, shape, dt=F32):
            return ctx.enter_context(nc.sbuf_tensor(f"moe_{what}", shape, dt))

        def pair(what, shape):
            return sb(f"{what}_hi", shape, F32R), sb(f"{what}_lo", shape, F32R)

        def sem(what):
            return ctx.enter_context(nc.semaphore(f"moe_{what}"))

        KC = KR // P
        down_raw = sb("down_raw", [P, DC, KR])
        up_raw = sb("up_raw", [P, KC, D])
        router_raw = sb("router_raw", [P, DC, EXPERTS])
        down, up, router = pair("down", [P, DC, KR]), pair("up", [P, KC, D]), pair("router", [P, DC, EXPERTS])
        scores = sb("scores", [P, 2, EXPERTS])
        left1, left2 = sb("left1", [P, 2, EXPERTS]), sb("left2", [P, 2, EXPERTS])
        top1, top2 = sb("top1", [P, 2, 8]), sb("top2", [P, 2, 8])
        lowest = sb("lowest", [P, 2])
        chosen = sb("chosen", [P, 2, EXPERTS])
        expd = sb("expd", [P, 2, EXPERTS])
        gated = sb("gated", [P, 2, EXPERTS])
        total, inverse = sb("total", [P, 2]), sb("inverse", [P, 2])
        gates = sb("gates", [P, 2, EXPERTS])
        ranks = sb("ranks", [P, 2, KR])
        ranksT = pair("ranksT", [P, 2, KC, P])

        ps_score = ctx.enter_context(nc.psum_tensor("moe_ps_score", [P, 512], F32))
        ps_rank = ctx.enter_context(nc.psum_tensor("moe_ps_rank", [P, 2, 2, 512], F32))
        ps_turn = ctx.enter_context(nc.psum_tensor("moe_ps_turn", [P, 2, 512], F32))
        ps_out = ctx.enter_context(nc.psum_tensor("moe_ps_out", [P, 512], F32))

        router_in, down_in, up_in = sem("router_in"), [sem(f"down_in{i}") for i in range(DC)], [sem(f"up_in{i}") for i in range(2)]
        weights_hi, weights_split = sem("weights_hi"), sem("weights_split")
        score_made, ranks_made, turned, out_made = sem("score_made"), sem("ranks_made"), sem("turned"), sem("out_made")
        picked, exp_done, gates_made = sem("picked"), sem("exp_done"), sem("gates_made")
        ranks_gated, turned_hi, turned_split, added, stored = sem("ranks_gated"), sem("turned_hi"), sem("turned_split"), sem("added"), sem("stored")
        block = ctx.enter_context(nc.Block())
        pieces = [(router_raw[:], router, slice(None), router_in)]
        pieces += [(down_raw[:, c, :], down, c, down_in[c]) for c in range(DC)]
        pieces += [(up_raw[:, 4 * i:4 * i + 4, :], up, slice(4 * i, 4 * i + 4), up_in[i]) for i in range(2)]

        @block.sync
        def _(sp):
            sp.dma_start(router_raw[:], dram["router"]).then_inc(router_in, 16)
            for c in range(DC):
                sp.dma_start(down_raw[:, c, :], dram["down1"][:, c, :]).then_inc(down_in[c], 16)
            for i in range(2):
                sp.dma_start(up_raw[:, 4 * i:4 * i + 4, :], dram["up1"][:, 4 * i:4 * i + 4, :]).then_inc(up_in[i], 16)
            for t in range(NT):
                sp.wait_ge(added, t + 1)
                sp.dma_start(out[t * P:(t + 1) * P, :], m.x[:, t, :]).then_inc(stored, 16)
            sp.wait_ge(stored, 16 * NT)

        @block.tensor
        def _(pe):
            def score(t):
                at = slice(t * P, (t + 1) * P)
                if t == 0:
                    pe.wait_ge(weights_split, 1)
                else:
                    pe.wait_ge(picked, 5 * t - 4)
                for c in range(DC):
                    last = product(nc, ps_score[:, 0:EXPERTS], (m.xT_hi[:, c, at], m.xT_lo[:, c, at]),
                                   [x[:, c, :] for x in router], c == 0, c == DC - 1)
                last.then_inc(score_made, 1)

            def rank(t):
                at = slice(t * P, (t + 1) * P)
                if t >= 2:
                    pe.wait_ge(ranks_gated, 2 * (t - 1))
                for c in range(DC):
                    if t == 0:
                        pe.wait_ge(weights_split, 2 + c)
                    for half in range(2):
                        last = product(nc, ps_rank[:, t % 2, half, :], (m.xT_hi[:, c, at], m.xT_lo[:, c, at]),
                                       [x[:, c, half * 512:(half + 1) * 512] for x in down], c == 0, c == DC - 1)
                last.then_inc(ranks_made, 1)

            def turn(t):
                for half in range(2):
                    pe.wait_ge(ranks_gated, 2 * t + half + 1)
                    wait(pe, turned_split, 2 * t + half - 1)
                    for k in range(4):
                        at = (4 * half + k) * P
                        last = nc.tensor.transpose(ps_turn[:, half, k * P:(k + 1) * P], ranks[:, t % 2, at:at + P], m.ident[:])
                    last.then_inc(turned, 1)

            def make_out(t):
                if t >= 1:
                    pe.wait_ge(added, t)
                for k in range(KC):
                    if k % 4 == 0:
                        pe.wait_ge(turned_split, 2 * t + k // 4 + 1)
                        if t == 0:
                            pe.wait_ge(weights_split, 6 + k // 4)
                    last = product(nc, ps_out[:], [x[:, t % 2, k, :] for x in ranksT], [x[:, k, :] for x in up], k == 0, k == KC - 1)
                last.then_inc(out_made, 1)

            score(0)
            rank(0)
            for t in range(NT):
                if t + 1 < NT:
                    score(t + 1)
                    rank(t + 1)
                turn(t)
                make_out(t)

        @block.vector
        def _(dve):
            def split_lo(i):
                src, (hi, lo), at, _ = pieces[i]
                dve.wait_ge(weights_hi, i + 1)
                nc.vector.tensor_tensor(lo[:, at], src, hi[:, at].bitcast(F32), ALU.subtract).then_inc(weights_split, 1)

            def pick(t):
                k = t % 2
                dve.wait_ge(score_made, t + 1)
                nc.vector.tensor_copy(scores[:, k, :], ps_score[:, 0:EXPERTS]).then_inc(picked, 1)
                dve.wait_ge(picked, 5 * t + 1)
                nc.vector.max(top1[:, k, :], scores[:, k, :]).then_inc(picked, 1)
                dve.wait_ge(picked, 5 * t + 2)
                nc.vector.tensor_scalar(lowest[:, k:k + 1], top1[:, k, 0:1], -1.0, None, ALU.mult)
                nc.vector.match_replace(left1[:, k, :], top1[:, k, :], scores[:, k, :], LOWEST).then_inc(picked, 1)
                dve.wait_ge(picked, 5 * t + 3)
                nc.vector.max(top2[:, k, :], left1[:, k, :]).then_inc(picked, 1)
                dve.wait_ge(picked, 5 * t + 4)
                nc.vector.match_replace(left2[:, k, :], top2[:, k, :], left1[:, k, :], LOWEST).then_inc(picked, 1)
                dve.wait_ge(picked, 5 * t + 5)
                nc.vector.tensor_scalar(chosen[:, k, :], left2[:, k, :], LOWEST, None, ALU.is_equal).then_inc(gates_made, 1)
                dve.wait_ge(gates_made, 4 * t + 1)
                dve.wait_ge(exp_done, t + 1)
                nc.vector.tensor_tensor_reduce(out=gated[:, k, :], in0=expd[:, k, :], in1=chosen[:, k, :], scale=1.0, scalar=0.0,
                                               op0=ALU.mult, op1=ALU.add, accum_out=total[:, k:k + 1]).then_inc(gates_made, 1)
                dve.wait_ge(gates_made, 4 * t + 2)
                nc.vector.reciprocal(inverse[:, k:k + 1], total[:, k:k + 1]).then_inc(gates_made, 1)
                dve.wait_ge(gates_made, 4 * t + 3)
                nc.vector.tensor_scalar(gates[:, k, :], gated[:, k, :], inverse[:, k:k + 1], 2.0, ALU.mult, ALU.mult).then_inc(gates_made, 1)

            def gate_ranks(t):
                dve.wait_ge(gates_made, 4 * t + 4)
                dve.wait_ge(ranks_made, t + 1)
                if t >= 2:
                    dve.wait_ge(turned, 2 * (t - 1))
                for half in range(2):
                    n = EXPERTS // 2
                    nc.vector.tensor_tensor(
                        ranks[:, t % 2, half * 512:(half + 1) * 512].rearrange("p (k r) -> p k r", r=RANK),
                        ps_rank[:, t % 2, half, :].rearrange("p (k r) -> p k r", r=RANK),
                        gates[:, t % 2, half * n:(half + 1) * n].unsqueeze(2).to_broadcast((P, n, RANK)),
                        ALU.mult).then_inc(ranks_gated, 1)

            split_lo(0)
            pick(0)
            for i in range(1, 5):
                split_lo(i)
            gate_ranks(0)
            for i in range(5, 7):
                split_lo(i)
            for t in range(NT):
                if t + 1 < NT:
                    pick(t + 1)
                for half in range(2):
                    dve.wait_ge(turned_hi, 2 * t + half + 1)
                    nc.vector.tensor_tensor(ranksT[1][:, t % 2, 4 * half:4 * half + 4, :],
                                            ps_turn[:, half, :].rearrange("p (k n) -> p k n", k=4),
                                            ranksT[0][:, t % 2, 4 * half:4 * half + 4, :].bitcast(F32),
                                            ALU.subtract).then_inc(turned_split, 1)
                if t + 1 < NT:
                    gate_ranks(t + 1)
                dve.wait_ge(out_made, t + 1)
                nc.vector.tensor_tensor(m.x[:, t, :], ps_out[:], m.x[:, t, :], ALU.add).then_inc(added, 1)

        @block.scalar
        def _(act):
            def split_hi(i):
                src, (hi, _), at, landed = pieces[i]
                act.wait_ge(landed, 16)
                nc.scalar.copy(hi[:, at], src).then_inc(weights_hi, 1)

            def exponent(t):
                act.wait_ge(picked, 5 * t + 3)
                if t >= 2:
                    act.wait_ge(gates_made, 4 * (t - 1))
                nc.scalar.activation(expd[:, t % 2, :], scores[:, t % 2, :], ACT.Exp, bias=lowest[:, t % 2:t % 2 + 1]).then_inc(exp_done, 1)

            split_hi(0)
            for i in range(1, 7):
                split_hi(i)
            exponent(0)
            for t in range(NT):
                if t + 1 < NT:
                    exponent(t + 1)
                for half in range(2):
                    act.wait_ge(turned, 2 * t + half + 1)
                    if t >= 2:
                        act.wait_ge(out_made, t - 1)
                    nc.scalar.copy(ranksT[0][:, t % 2, 4 * half:4 * half + 4, :],
                                   ps_turn[:, half, :].rearrange("p (k n) -> p k n", k=4)).then_inc(turned_hi, 1)


def program(nc, dram, out):
    with ExitStack() as ctx:
        def sb(what, shape, dt=F32):
            return ctx.enter_context(nc.sbuf_tensor(what, shape, dt))

        m = Model(dram=dram, x=sb("x", [P, NT, D]), ident=sb("ident", [P, P]),
                            xT_hi=sb("xT_hi", [P, DC, TOK], F32R), xT_lo=sb("xT_lo", [P, DC, TOK], F32R),
                            ln_loaded=[ctx.enter_context(nc.semaphore(f"ln_loaded{t}")) for t in range(NT)],
                            ln_semaphores=[ctx.enter_context(nc.semaphore(f"ln_{what}")) for what in LN_SEMAPHORES])
        layernorm_phase(nc, m, 0, load=dram["x"])
        attention0_phase(nc, m)
        layernorm_phase(nc, m, 1)
        ffn0_phase(nc, m)
        layernorm_phase(nc, m, 2)
        attention1_phase(nc, m)
        layernorm_phase(nc, m, 3)
        moe_phase(nc, m, out)



def shape_constants():
    f = np.float32
    pos = np.arange(SEQ, dtype=f)
    inv_freq = (f(1.0) / f(10000.0) ** (np.arange(0, HD0, 2, dtype=f) / f(HD0))).astype(f)
    angle = np.concatenate([(pos[:, None] * inv_freq[None, :]).astype(f)] * 2, axis=1).T
    cos, sin = np.cos(angle).astype(f), np.sin(angle).astype(f)
    sin[HD0 // 2:] *= f(-1.0)
    scale = np.where(pos < SYS_LEN, f(0.5), np.where(pos < SYS_LEN + IMG_LEN, f(1.5), f(1.0))).astype(f)
    unscale = np.ones((P, P), f)
    unscale[:SYS_LEN + IMG_LEN] = (f(1.0) / scale[:P])[None, :]
    row, col = np.arange(P)[:, None], np.arange(P)[None, :]
    causal = np.zeros((P, SEQ), f)
    causal[:, SEQ - P:] = np.where(row >= col, f(0.0), f(MASKED))
    slopes = f(1.0) / f(2.0) ** (np.arange(1, HEADS1 + 1, dtype=f) * f(8.0 / HEADS1))
    slope = (slopes[:, None] * (pos - f(SEQ - 1))[None, :]).astype(f) * f(HD1 ** 0.5)
    slope_hi = (slope.view(np.uint32) + np.uint32(0x800) & np.uint32(0xFFFFF000)).view(f)
    slopes = np.zeros((CHUNKS1, 32, PAIRS, SEQ), f)
    pick = np.zeros((32, BATCH, PAIRS, 2, SEQ), f)
    for head in range(2):
        of_head = slope.reshape(CHUNKS1, PAIRS, 2, SEQ)[:, :, head], slope_hi.reshape(CHUNKS1, PAIRS, 2, SEQ)[:, :, head]
        slopes[:, 2 * head], slopes[:, 2 * head + 1] = of_head[1], of_head[0] - of_head[1]
        pick[2 * head:2 * head + 2, :, :, head] = f(1.0)
    return {"cos_q": cos, "sin_q": sin, "cos_k": cos * scale, "sin_k": sin * scale, "unscale": unscale,
            "causal": causal, "ident": np.eye(P, dtype=f), "slope": slopes.reshape(CHUNKS1, 32, PAIRS * SEQ),
            "pick": pick.reshape(32, BATCH * PAIRS * 2 * SEQ)}


def columns(w, n):
    return w.reshape(-1, n, DC, P).transpose(0, 3, 2, 1).reshape(-1, P, DC * n)


def lay_out(i):
    i = {k: np.asarray(v) for k, v in i.items()}
    w_qkv = columns(i["L1_attn_w_qkv"], P)
    return {
        "x": i["L0_attn_hidden_states"].reshape(TOK, D),
        "wq": columns(i["L0_attn_wq"], HD0).reshape(KV0, PER_KV, P, DC * HD0),
        "wk": columns(i["L0_attn_wk"], HD0),
        "wv": columns(i["L0_attn_wv"], HD0),
        "wo": i["L0_attn_wo"].T.reshape(KV0, PER_KV, HD0, D),
        "gate": columns(i["L0_ffn_gate_t"], P),
        "up": columns(i["L0_ffn_up_t"], P),
        "down": i["L0_ffn_down_t"].T.reshape(FC, P, D),
        "gate_s": i["L0_ffn_gate_s"].reshape(FC, P).T,
        "up_s": i["L0_ffn_up_s"].reshape(FC, P).T,
        "down_s": i["L0_ffn_down_s"].reshape(1, D),
        "wq1": w_qkv[0:4], "wk1": w_qkv[4:8], "wv1": w_qkv[8:12],
        "bias1": i["L1_attn_b_qkv"].reshape(3, CHUNKS1, P).transpose(2, 0, 1),
        "wo1": i["L1_attn_w_out"].T.reshape(CHUNKS1, P, D),
        "out_bias": i["L1_attn_b_out"].reshape(1, D),
        "router": i["L1_ffn_Wr"].T.reshape(DC, P, EXPERTS).transpose(1, 0, 2),
        "down1": i["L1_ffn_A"].reshape(KR, D).T.reshape(DC, P, KR).transpose(1, 0, 2),
        "up1": i["L1_ffn_B"].transpose(0, 2, 1).reshape(KR // P, P, D).transpose(1, 0, 2),
    }


def kernel(**inputs):
    import concourse.bacc as bacc
    from concourse.bass_utils import run_bass_kernel_spmd

    nc = bacc.Bacc("TRN2", target_bir_lowering=False, num_devices=1)
    arrays, dram = {}, {}
    for name, a in {**lay_out(inputs), **shape_constants()}.items():
        arrays[f"in_{name}"] = np.ascontiguousarray(a)
        dram[name] = nc.dram_tensor(f"in_{name}", a.shape, mybir.dt.from_np(a.dtype), kind="ExternalInput").ap()
    out = nc.dram_tensor("out", (TOK, D), F32, kind="ExternalOutput").ap()
    program(nc, dram, out)
    result = run_bass_kernel_spmd(nc, [arrays], core_ids=[0])
    return result.results[0]["out"].reshape(BATCH, SEQ, D)
```

```python
from contextlib import ExitStack

import numpy as np

import concourse.bass as bass
from concourse import mybir

P = 128
F32 = mybir.dt.float32
F32R = mybir.dt.float32r
I32 = mybir.dt.int32
ALU = mybir.AluOpType
ACT = mybir.ActivationFunctionType

BATCH, SEQ, D = 2, 512, 512
TOK = BATCH * SEQ
NT = TOK // P
DC = D // P
QT = SEQ // P
HEADS0, KV0, HD0 = 32, 8, 128
PER_KV = HEADS0 // KV0
FF = 1792
FC = FF // P
HEADS1, HD1 = 32, 16
EXPERTS, TOPK, RANK = 64, 16, 16
KR = EXPERTS * RANK
EPS = 1e-5
SYS_LEN, IMG_LEN = 35, 72
MASKED = -1.0e30
LOWEST = -3.0e38

SCORE_AT = [P * i * (i + 1) // 2 for i in range(QT + 1)]


class Model:

    def __init__(self, dram, x, ident, xT_hi, xT_lo, ident_in, ln_loaded, ln_semaphores, stats, moments):
        self.dram, self.x, self.ident = dram, x, ident
        self.xT_hi, self.xT_lo = xT_hi, xT_lo
        self.ident_in, self.ln_loaded, self.ln_semaphores = ident_in, ln_loaded, ln_semaphores
        self.stats, self.moments = stats, moments


def wait(engine, semaphore, value):
    if isinstance(value, int) and value <= 0:
        return
    engine.wait_ge(semaphore, value)


def product(nc, out, left, right, start, stop):
    nc.tensor.matmul(out, left[0], right[0], start=start, stop=False)
    nc.tensor.matmul(out, left[0], right[1], start=False, stop=False)
    return nc.tensor.matmul(out, left[1], right[0], start=False, stop=stop)


LN_SEMAPHORES = ("stats_done", "moments_done", "var_done", "root_done", "inverse_done", "normal_done",
                 "turned_done", "hi_done", "lo_done")


def take_moments(nc, dve, m, number, t):
    stats_done, moments_done = m.ln_semaphores[:2]
    nc.vector.bn_stats(m.stats[:, t, :], m.x[:, t, :]).then_inc(stats_done, 1)
    dve.wait_ge(stats_done, number * NT + t + 1)
    nc.vector.bn_aggr(m.moments[:, t, :], m.stats[:, t, :]).then_inc(moments_done, 1)


class LayerNorm:

    def __init__(self, nc, m, ctx, number, normal, turned, load=None):
        self.nc, self.m, self.load, self.normal, self.turned = nc, m, load, normal, turned
        self.before, self.tiles_before = number, number * NT
        self.moments = m.moments
        self.shifted, self.deviation, self.inverse = (
            ctx.enter_context(nc.sbuf_tensor(f"ln{number}_{what}", [P, NT], F32)) for what in ("shifted", "deviation", "inverse"))

    def sync(self, sp):
        m = self.m
        for t in range(NT):
            sp.dma_start(m.x[:, t, :], self.load[t * P:(t + 1) * P, :]).then_inc(m.ln_loaded[t], 16)
        sp.dma_start(m.ident[:], m.dram["ident"]).then_inc(m.ident_in, 16)

    def vector(self, dve):
        nc, m, before, tiles_before = self.nc, self.m, self.before, self.tiles_before
        _, moments_done, var_done, root_done, inverse_done, normal_done, turned_done, hi_done, lo_done = m.ln_semaphores
        if self.load is not None:
            for t in range(NT):
                dve.wait_ge(m.ln_loaded[t], 16)
                take_moments(nc, dve, m, 0, t)
        dve.wait_ge(moments_done, tiles_before + NT)
        nc.vector.tensor_scalar(self.shifted[:], self.moments[:, :, 1], EPS, None, ALU.add).then_inc(var_done, 1)
        dve.wait_ge(root_done, before + 1)
        nc.vector.reciprocal(self.inverse[:], self.deviation[:]).then_inc(inverse_done, 1)
        dve.wait_ge(inverse_done, before + 1)

        def normalise(t):
            if t >= 4:
                dve.wait_ge(turned_done, tiles_before + t - 3)
            nc.vector.tensor_scalar(self.normal[t % 4], m.x[:, t, :], self.moments[:, t, 0:1], self.inverse[:, t:t + 1],
                                    ALU.subtract, ALU.mult).then_inc(normal_done, 1)

        for t in range(3):
            normalise(t)
        for t in range(NT):
            dve.wait_ge(hi_done, tiles_before + t + 1)
            nc.vector.tensor_tensor(m.xT_lo[:, :, t * P:(t + 1) * P], self.turned[t % 4].rearrange("p (c n) -> p c n", c=DC),
                                    m.xT_hi[:, :, t * P:(t + 1) * P].bitcast(F32), ALU.subtract).then_inc(lo_done, 1)
            if t + 3 < NT:
                normalise(t + 3)
        dve.wait_ge(turned_done, tiles_before + NT)

    def scalar(self, act):
        nc, m, before, tiles_before = self.nc, self.m, self.before, self.tiles_before
        _, _, var_done, root_done, _, _, turned_done, hi_done, _ = m.ln_semaphores
        act.wait_ge(var_done, before + 1)
        nc.scalar.activation(self.deviation[:], self.shifted[:], ACT.Sqrt).then_inc(root_done, 1)
        for t in range(NT):
            act.wait_ge(turned_done, tiles_before + t + 1)
            nc.scalar.copy(m.xT_hi[:, :, t * P:(t + 1) * P], self.turned[t % 4].rearrange("p (c n) -> p c n", c=DC)).then_inc(hi_done, 1)

    def tensor(self, pe):
        nc, m, tiles_before = self.nc, self.m, self.tiles_before
        _, _, _, _, _, normal_done, turned_done, _, lo_done = m.ln_semaphores
        if self.load is not None:
            pe.wait_ge(m.ident_in, 16)
        for t in range(NT):
            pe.wait_ge(normal_done, tiles_before + t + 1)
            if t >= 4:
                pe.wait_ge(lo_done, tiles_before + t - 3)
            for c in range(DC):
                last = nc.tensor.transpose(self.turned[t % 4][:, c * P:(c + 1) * P], self.normal[t % 4][:, c * P:(c + 1) * P], m.ident[:])
            last.then_inc(turned_done, 1)
        pe.wait_ge(lo_done, tiles_before + NT)


GROUP = 2 * PER_KV
UNITS = KV0 * GROUP
SIDE = {0: "keys", 1: "values", 2: "out", 3: "out", 4: "keys", 5: "values", 6: "out", 7: "out"}

PIECES = [("wk", 0, 1), ("wq", 0, 2), ("wv", 0, 2), ("wq", 1, 3), ("wo", 0, 4), ("wo", 1, 4), ("wq", 2, 4),
          ("wo", 2, 5), ("wo", 3, 5), ("wq", 3, 5)]
FIRST_PIECES = [("wk", 0), ("wv", 0), ("wq", 0), ("wq", 1), ("wq", 2), ("wq", 3)]
SLOTS = 5
PROJECTIONS = [(s, what) for s in range(GROUP) for what in
               ([SIDE[s]] if SIDE[s] != "out" else []) + ["query"]]
ROTATIONS = [x for x in PROJECTIONS if x[1] != "values"]
OUTPUTS = [x for s in range(GROUP) for x in
           ([(s, "out", 0), (s, "out", 1)] if SIDE[s] == "out" else []) + [(s, "attend", 0)]]


def attention0_phase(nc, m):
    dram = m.dram
    with ExitStack() as ctx:
        def sb(what, shape, dt=F32):
            return ctx.enter_context(nc.sbuf_tensor(f"a0_{what}", shape, dt))

        def pair(what, shape):
            return sb(f"{what}_hi", shape, F32R), sb(f"{what}_lo", shape, F32R)

        def sem(what):
            return ctx.enter_context(nc.semaphore(f"a0_{what}"))

        raw = sb("raw", [P, SLOTS, 512])
        zeros = sb("zeros", [P, 512])
        wq = pair("wq", [P, PER_KV, DC, HD0])
        wk = pair("wk", [P, DC, HD0])
        wv = pair("wv", [P, DC, HD0])
        wo = pair("wo", [P, PER_KV, D])
        keys = pair("keys", [P, BATCH, SEQ])
        values_turned = sb("values_turned", [P, SEQ])
        values = pair("values", [P, BATCH, QT, HD0])
        query = pair("query", [P, 4, SEQ])
        cos_q, sin_q = sb("cos_q", [P, SEQ]), sb("sin_q", [P, SEQ])
        cos_k, sin_k = sb("cos_k", [P, SEQ]), sb("sin_k", [P, SEQ])
        causal = sb("causal", [P, SEQ])
        unscale = sb("unscale", [P, P])
        by_cos, by_sin, rotated = sb("by_cos", [P, SEQ]), sb("by_sin", [P, SEQ]), sb("rotated", [P, SEQ])
        first_tile = sb("first_tile", [P, P])
        probs = sb("probs", [P, 2, SCORE_AT[QT]])
        least = sb("least", [P, 2, QT])
        total = sb("total", [P, 2, QT])
        inverse = sb("inverse", [P, 2, QT])
        probsT = pair("probsT", [P, 2, SEQ])
        attended = pair("attended", [P, BATCH, PER_KV, SEQ])

        ps_proj = ctx.enter_context(nc.psum_tensor("a0_ps_proj", [P, 2, 512], F32))
        ps_score = ctx.enter_context(nc.psum_tensor("a0_ps_score", [P, 2, 512], F32))
        ps_turn = ctx.enter_context(nc.psum_tensor("a0_ps_turn", [P, 2, 512], F32))
        ps_out = ctx.enter_context(nc.psum_tensor("a0_ps_out", [P, 2, 512], F32))

        raw_in = [sem(f"raw_in{s}") for s in range(SLOTS)]
        consts_in, zeros_set, wait_passed = sem("consts_in"), sem("zeros_set"), sem("wait_passed")
        piece_hi, piece_split = sem("piece_hi"), sem("piece_split")
        query_made, keys_made, values_made = sem("query_made"), sem("keys_made"), sem("values_made")
        rotation_scaled, rotation_added = sem("rotation_scaled"), sem("rotation_added")
        rotation_hi, rotation_split = sem("rotation_hi"), sem("rotation_split")
        values_copied, values_placed = sem("values_copied"), sem("values_placed")
        values_hi, values_split = sem("values_hi"), sem("values_split")
        score_made, first_scaled, score_masked = sem("score_made"), sem("first_scaled"), sem("score_masked")
        exp_done, total_inverted, probs_ready = sem("exp_done"), sem("total_inverted"), sem("probs_ready")
        turned, turned_hi, turned_split = sem("turned"), sem("turned_hi"), sem("turned_split")
        attend_made, attended_hi, attended_split = sem("attend_made"), sem("attended_hi"), sem("attended_split")
        out_made, out_added = sem("out_made"), sem("out_added")

        def rotation(g, s, what):
            if isinstance(g, int) and g == -1 and s == 4:
                return 1
            if isinstance(g, int) and g == KV0 - 1 and (s, what) == (4, "query"):
                return rotation(g, 3, "query") + 1
            return 10 * g + 4 + ROTATIONS.index((s, what)) + 1

        def query_rotation(g, u):
            return rotation(g, u - 3, "query") if u >= 3 else rotation(g - 1, u + 5, "query")

        def values_count(g, s):
            return 2 * g + (2 if s == 1 else 3)

        def out_count(g, s, half):
            return 8 * g + (2 * s - 8 if s < 4 else 2 * s - 12) + half + 1

        def piece_count(g, what, which):
            names = [x[:2] for x in PIECES]
            return len(FIRST_PIECES) + len(PIECES) * g + names.index((what, which)) + 1

        def present(g, s, what):
            if not isinstance(g, int):
                return True
            if what == "query":
                return 0 <= GROUP * g + s + 3 < UNITS
            if what in ("keys", "values"):
                return (g >= 0 if s < 4 else g < KV0 - 1) and g < KV0
            if what == "score":
                return 0 <= GROUP * g + s + 1 < UNITS
            if what == "attend":
                return 0 <= g < KV0
            return (1 <= g if s < 4 else 0 <= g < KV0)

        def step_before(g, s):
            return (g, s - 1) if s > 0 else (g - 1, GROUP - 1)

        def projection_bank(g, s, what):
            return PROJECTIONS.index((s, what)) % 2

        def wait_projection_bank(pe, g, s, what):
            at = PROJECTIONS.index((s, what)) - 2
            gb = g if at >= 0 else g - 1
            sb_, before = PROJECTIONS[at]
            if isinstance(gb, int) and (gb < -1 or not present(gb, sb_, before)):
                return
            if before == "values":
                wait(pe, values_split, values_count(gb, sb_))
            else:
                wait(pe, rotation_scaled, rotation(gb, sb_, before))

        def wait_output_bank(pe, g, s, what, half):
            at = OUTPUTS.index((s, what, half)) - 2
            gb = g
            while True:
                if at < 0:
                    at, gb = at + len(OUTPUTS), gb - 1
                sb_, before, hb = OUTPUTS[at]
                if isinstance(gb, int) and gb < 0:
                    return
                if present(gb, sb_, before):
                    break
                at -= 2
            if before == "out":
                wait(pe, out_added, out_count(gb, sb_, hb))
            else:
                wait(pe, attended_split, GROUP * gb + sb_ + 1)

        norm = LayerNorm(nc, m, ctx, 0, [probs[:, k // 2, k % 2 * D:(k % 2 + 1) * D] for k in range(4)],
                         [ps[:, k, :] for ps in (ps_turn, ps_score) for k in range(2)], load=dram["x"])
        block = ctx.enter_context(nc.Block())

        @block.sync
        def _(sp):
            norm.sync(sp)

            def fetch(number, what, which, g):
                slot = number % SLOTS
                src = dram[what][g, which] if what in ("wq", "wo") else dram[what][g]
                sp.dma_start(raw[:, slot, :], src).then_inc(raw_in[slot], 16)

            for c, (what, which) in enumerate(FIRST_PIECES):
                if c == SLOTS:
                    for table, name in ((cos_q, "cos_q"), (sin_q, "sin_q"), (cos_k, "cos_k"), (sin_k, "sin_k"),
                                        (causal, "causal"), (unscale, "unscale")):
                        sp.dma_start(table[:], dram[name]).then_inc(consts_in, 16)
                wait(sp, piece_split, c - SLOTS + 1)
                fetch(c, what, which, 0)

            def group(g, last):
                for c, (what, which, _) in enumerate(PIECES):
                    if last and what != "wo":
                        continue
                    number = len(FIRST_PIECES) + c
                    done = len([x for x in PIECES[:c] if x[0] == "wo"]) if last else c
                    if last:
                        wait(sp, piece_split, len(FIRST_PIECES) + len(PIECES) * g + done)
                    else:
                        wait(sp, piece_split, len(PIECES) * g + number - SLOTS + 1)
                    fetch(number, what, which, g if what == "wo" else g + 1)

            with sp.Fori(0, KV0 - 1) as g:
                group(g, False)
            group(KV0 - 1, True)

        @block.gpsimd
        def _(pool):
            nc.gpsimd.memset(zeros[:], 0.0).then_inc(zeros_set, 1)
            pool.wait_ge(zeros_set, 1)
            targets = {"wq": wq, "wk": wk, "wv": wv, "wo": wo}

            def split(number, count, landed, what, which):
                slot = number % SLOTS
                hi, lo = targets[what]
                if what in ("wq", "wo"):
                    hi, lo = hi[:, which], lo[:, which]
                if what == "wo":
                    src = raw[:, slot, :]
                else:
                    src = raw[:, slot, :].rearrange("p (c n) -> p c n", c=DC)
                    if what in ("wk", "wv"):
                        hi, lo = hi[:], lo[:]
                pool.wait_ge(raw_in[slot], 16 * landed)
                zero = zeros[:] if what == "wo" else zeros[:].rearrange("p (c n) -> p c n", c=DC)
                nc.gpsimd.tensor_tensor(hi, src, zero, ALU.add).then_inc(piece_hi, 1)
                pool.wait_ge(piece_hi, count + 1)
                nc.gpsimd.tensor_tensor(lo, src, hi.bitcast(F32), ALU.subtract).then_inc(piece_split, 1)

            def add_rotation(count):
                pool.wait_ge(rotation_scaled, count)
                wait(pool, rotation_split, count - 1)
                nc.gpsimd.tensor_tensor(rotated[:], by_cos[:], by_sin[:], ALU.add).then_inc(rotation_added, 1)

            def free_for(g, what, which):
                if what == "wo":
                    wait(pool, out_made, out_count(g, 3, 1))
                elif what == "wk":
                    wait(pool, keys_made, 2 * g + 2)
                elif what == "wv":
                    wait(pool, values_made, 2 * g + 2)
                else:
                    wait(pool, query_made, GROUP * g + PER_KV + which + 1)

            for c, (what, which) in enumerate(FIRST_PIECES[:3]):
                split(c, c, 1, what, which)
            add_rotation(rotation(-1, 4, "keys"))
            for c, s in ((3, 5), (4, 6), (5, 7)):
                split(c, c, 1 if c < SLOTS else 2, *FIRST_PIECES[c])
                add_rotation(rotation(-1, s, "query"))

            def group(g, last):
                for s in range(GROUP):
                    if SIDE[s] == "keys" and present(g, s, "keys"):
                        add_rotation(rotation(g, s, "keys"))
                    for c, (what, which, step) in enumerate(PIECES):
                        if step != s or (last and what != "wo"):
                            continue
                        number = len(FIRST_PIECES) + c
                        slot = number % SLOTS
                        before = (2 if slot == 0 else 1) + len([x for x in range(c) if (len(FIRST_PIECES) + x) % SLOTS == slot])
                        if last:
                            done = len([x for x in PIECES[:c] if x[0] == "wo"])
                            before = (2 if slot == 0 else 1) + len(
                                [x for x in range(c) if (len(FIRST_PIECES) + x) % SLOTS == slot and PIECES[x][0] == "wo"])
                        else:
                            done = c
                        free_for(g, what, which)
                        split(number, len(FIRST_PIECES) + len(PIECES) * g + done, 2 * g + before + 1, what, which)
                    if present(g, s, "query"):
                        add_rotation(rotation(g, s, "query"))

            group(0, False)
            with pool.Fori(1, KV0 - 1) as g:
                group(g, False)
            group(KV0 - 1, True)

        @block.tensor
        def _(pe):
            norm.tensor(pe)

            def xT(part, c, at, size):
                return part[:, c, at:at + size]

            def make_query(g, s, chunks):
                u = (s + 3) % GROUP
                b, j = u // PER_KV, u % PER_KV
                bank = projection_bank(g, s, "query")
                gq = g if s + 3 < GROUP else g + 1
                if chunks[0] == 0:
                    wait_projection_bank(pe, g, s, "query")
                    wait(pe, piece_split, weights_ready("wq", j, gq))
                for c in chunks:
                    last = product(nc, ps_proj[:, bank, :], (wq[0][:, j, c, :], wq[1][:, j, c, :]),
                                   (xT(m.xT_hi, c, b * SEQ, SEQ), xT(m.xT_lo, c, b * SEQ, SEQ)), c == 0, c == DC - 1)
                if chunks[-1] == DC - 1:
                    last.then_inc(query_made, 1)

            def weights_ready(what, which, g):
                if isinstance(g, int) and g == 0 and what != "wo":
                    return FIRST_PIECES.index((what, which)) + 1
                if what == "wo":
                    if isinstance(g, int) and g == KV0 - 1:
                        return len(FIRST_PIECES) + len(PIECES) * g + which + 1
                    return piece_count(g, what, which)
                return piece_count(g - 1, what, which)

            def make_keys(g, s):
                b = 1 if s < 4 else 0
                bank = projection_bank(g, s, "keys")
                wait_projection_bank(pe, g, s, "keys")
                wait(pe, piece_split, weights_ready("wk", 0, g if b else g + 1))
                for c in range(DC):
                    last = product(nc, ps_proj[:, bank, :], (wk[0][:, c, :], wk[1][:, c, :]),
                                   (xT(m.xT_hi, c, b * SEQ, SEQ), xT(m.xT_lo, c, b * SEQ, SEQ)), c == 0, c == DC - 1)
                last.then_inc(keys_made, 1)

            def make_values(g, s):
                b = 1 if s < 4 else 0
                bank = projection_bank(g, s, "values")
                wait_projection_bank(pe, g, s, "values")
                wait(pe, piece_split, weights_ready("wv", 0, g if b else g + 1))
                for c in range(DC):
                    last = product(nc, ps_proj[:, bank, :], (wv[0][:, c, :], wv[1][:, c, :]),
                                   (xT(m.xT_hi, c, b * SEQ, SEQ), xT(m.xT_lo, c, b * SEQ, SEQ)), c == 0, c == DC - 1)
                last.then_inc(values_made, 1)

            def place_values(g, s):
                wait(pe, values_copied, values_count(g, s))
                for t in range(QT):
                    last = nc.tensor.transpose(ps_proj[:, projection_bank(g, s, "values"), t * P:(t + 1) * P],
                                               values_turned[:, t * P:(t + 1) * P], m.ident[:])
                last.then_inc(values_placed, 1)

            def score(g, s, i):
                u = (s + 1) % GROUP
                gu = g if s + 1 < GROUP else g + 1
                n = GROUP * gu + u
                b = u // PER_KV
                if i == 0:
                    wait(pe, rotation_split, query_rotation(gu, u))
                    if u == 0:
                        wait(pe, rotation_split, rotation(gu - 1, 4, "keys"))
                    elif u == PER_KV:
                        wait(pe, rotation_split, rotation(gu, 0, "keys"))
                wait(pe, score_masked, 4 * n + i - 1)
                q = (query[0][:, u % 4, i * P:(i + 1) * P], query[1][:, u % 4, i * P:(i + 1) * P])
                k = (keys[0][:, b, 0:P * (i + 1)], keys[1][:, b, 0:P * (i + 1)])
                product(nc, ps_score[:, i % 2, 0:P * (i + 1)], q, k, True, True).then_inc(score_made, 1)

            def turn(n, u, t):
                if t == 0:
                    wait(pe, probs_ready, 4 * n + 4)
                wait(pe, turned_split, 4 * n + t - 1)
                for i in range(t, QT):
                    at = SCORE_AT[i] + t * P
                    last = nc.tensor.transpose(ps_turn[:, t % 2, (i - t) * P:(i - t + 1) * P],
                                               probs[:, u % 2, at:at + P], m.ident[:])
                last.then_inc(turned, 1)

            def attend(g, u, t):
                n = GROUP * g + u
                b = u // PER_KV
                bank = OUTPUTS.index((u, "attend", 0)) % 2
                if t == 0:
                    wait_output_bank(pe, g, u, "attend", 0)
                    if u % PER_KV == 0:
                        wait(pe, values_split, 2 * g + b + 1)
                wait(pe, turned_split, 4 * n + t + 1)
                w = SEQ - t * P
                product(nc, ps_out[:, bank, t * P:SEQ], (values[0][:, b, t, :], values[1][:, b, t, :]),
                        (probsT[0][:, t % 2, 0:w], probsT[1][:, t % 2, 0:w]), t == 0, t == QT - 1).then_inc(attend_made, 1)

            def make_out(g, s, half):
                b = 1 if s < 4 else 0
                t = 2 * (s % 2) + half
                bank = OUTPUTS.index((s, "out", half)) % 2
                gw = g - 1 if b else g
                wait_output_bank(pe, g, s, "out", half)
                if half == 0 and s in (2, 6):
                    wait(pe, attended_split, GROUP * gw + PER_KV * (b + 1))
                    wait(pe, piece_split, weights_ready("wo", PER_KV - 1, gw))
                for j in range(PER_KV):
                    at = slice(t * P, (t + 1) * P)
                    last = product(nc, ps_out[:, bank, :], (attended[0][:, b, j, at], attended[1][:, b, j, at]),
                                   (wo[0][:, j, :], wo[1][:, j, :]), j == 0, j == PER_KV - 1)
                last.then_inc(out_made, 1)

            def step(g, s):
                n = GROUP * g + s
                if present(g, s, "score"):
                    score(g, s, 0)
                    score(g, s, 1)
                if present(g, s, "attend"):
                    turn(n, s, 0)
                    turn(n, s, 1)
                if present(g, s, SIDE[s]):
                    if SIDE[s] == "out":
                        make_out(g, s, 0)
                        make_out(g, s, 1)
                    elif SIDE[s] == "keys":
                        make_keys(g, s)
                    else:
                        make_values(g, s)
                if present(g, s, "score"):
                    score(g, s, 2)
                    score(g, s, 3)
                if present(g, s, "query"):
                    make_query(g, s, [0, 1])
                if SIDE[s] == "values" and present(g, s, "values"):
                    place_values(g, s)
                if present(g, s, "attend"):
                    attend(g, s, 0)
                    turn(n, s, 2)
                    attend(g, s, 1)
                    turn(n, s, 3)
                if present(g, s, "query"):
                    make_query(g, s, [2, 3])
                if present(g, s, "attend"):
                    attend(g, s, 2)
                    attend(g, s, 3)

            for s in (4, 5, 6, 7):
                step(-1, s)
            for s in range(GROUP):
                step(0, s)
            with pe.Fori(1, KV0 - 1) as g:
                for s in range(GROUP):
                    step(g, s)
            for s in range(GROUP):
                step(KV0 - 1, s)
            for s in range(4):
                step(KV0, s)

        @block.vector
        def _(dve):
            half = P // 2
            norm.vector(dve)
            dve.wait_ge(consts_in, 16 * 6)

            def mask(g, s, i):
                n = GROUP * g + s + 1
                slot = (s + 1) % 2
                at, w = SCORE_AT[i], P * (i + 1)
                dve.wait_ge(score_made, 4 * n + i + 1)
                if i > 0:
                    dve.sem_inc(wait_passed, 1)
                src = ps_score[:, i % 2, 0:w]
                if i == 0:
                    wait(dve, turned, 4 * (n - 1))
                    nc.vector.tensor_tensor(first_tile[:], src, unscale[:], ALU.mult).then_inc(first_scaled, 1)
                    dve.wait_ge(first_scaled, n + 1)
                    dve.sem_inc(wait_passed, 1)
                    src = first_tile[:]
                nc.vector.tensor_tensor_reduce(
                    out=probs[:, slot, at:at + w], in0=src, in1=causal[:, SEQ - w:SEQ], scale=-float(HD0) ** -0.5,
                    scalar=-LOWEST, op0=ALU.add, op1=ALU.min, accum_out=least[:, slot, i:i + 1]).then_inc(score_masked, 1)

            def split_turned(g, s, t):
                n = GROUP * g + s
                w = SEQ - t * P
                dve.wait_ge(turned_hi, 4 * n + t + 1)
                nc.vector.tensor_tensor(probsT[1][:, t % 2, 0:w], ps_turn[:, t % 2, 0:w],
                                        probsT[0][:, t % 2, 0:w].bitcast(F32), ALU.subtract).then_inc(turned_split, 1)

            def rotate(g, s, what):
                bank = projection_bank(g, s, what)
                src = ps_proj[:, bank, :]
                cos, sin = (cos_q, sin_q) if what == "query" else (cos_k, sin_k)
                if what == "query":
                    dve.wait_ge(query_made, GROUP * g + s + 4)
                else:
                    dve.wait_ge(keys_made, 2 * g + (2 if s == 0 else 3))
                wait(dve, rotation_added, rotation(g, s, what) - 1)
                nc.vector.tensor_tensor(by_cos[:], src, cos[:], ALU.mult)
                nc.vector.tensor_tensor(by_sin[0:half], src[half:P], sin[half:P], ALU.mult)
                nc.vector.tensor_tensor(by_sin[half:P], src[0:half], sin[0:half], ALU.mult).then_inc(rotation_scaled, 1)

            def split_rotated(g, s, what):
                dve.wait_ge(rotation_hi, rotation(g, s, what))
                if what == "query":
                    hi, lo = query[0][:, (s + 3) % 4, :], query[1][:, (s + 3) % 4, :]
                else:
                    b = 1 if s < 4 else 0
                    hi, lo = keys[0][:, b, :], keys[1][:, b, :]
                nc.vector.tensor_tensor(lo, rotated[:], hi.bitcast(F32), ALU.subtract).then_inc(rotation_split, 1)

            def step(g, s):
                n = GROUP * g + s
                if present(g, s, "score"):
                    mask(g, s, 0)
                    mask(g, s, 1)
                if present(g, s, "attend"):
                    split_turned(g, s, 0)
                    split_turned(g, s, 1)
                if present(*step_before(g, s), "query"):
                    split_rotated(*step_before(g, s), "query")
                side = SIDE[s] if present(g, s, SIDE[s]) else None
                last_steps = isinstance(g, int) and g == KV0
                if side == "out":
                    b = 1 if s < 4 else 0
                    for h in range(2):
                        t = b * QT + 2 * (s % 2) + h
                        count = out_count(g, s, h)
                        dve.wait_ge(out_made, count)
                        wait(dve, out_added, count - QT)
                        nc.vector.tensor_tensor(m.x[:, t, :], ps_out[:, OUTPUTS.index((s, "out", h)) % 2, :],
                                                m.x[:, t, :], ALU.add).then_inc(out_added, 1)
                        if last_steps:
                            dve.wait_ge(out_added, count)
                            take_moments(nc, dve, m, 1, t)
                elif last_steps and s == 0:
                    dve.wait_ge(out_added, out_count(KV0 - 1, 7, 1))
                    for t in range(QT):
                        take_moments(nc, dve, m, 1, t)
                if present(g, s, "score"):
                    mask(g, s, 2)
                    mask(g, s, 3)
                if side == "keys":
                    rotate(g, s, "keys")
                if present(g, s, "attend"):
                    split_turned(g, s, 2)
                if present(g, s, "score"):
                    dve.wait_ge(exp_done, 4 * (n + 1) + 4)
                    nc.vector.reciprocal(inverse[:, (s + 1) % 2, :], total[:, (s + 1) % 2, :]).then_inc(total_inverted, 1)
                if present(g, s, "attend"):
                    split_turned(g, s, 3)
                if side == "values":
                    b = 1 if s < 4 else 0
                    dve.wait_ge(values_hi, values_count(g, s))
                    nc.vector.tensor_tensor(values[1][:, b], ps_proj[:, projection_bank(g, s, "values"), :].rearrange(
                        "p (t d) -> p t d", t=QT), values[0][:, b].bitcast(F32), ALU.subtract).then_inc(values_split, 1)
                if side == "keys":
                    split_rotated(g, s, "keys")
                if present(g, s, "query"):
                    rotate(g, s, "query")
                if present(g, s, "attend"):
                    b, j = s // PER_KV, s % PER_KV
                    dve.wait_ge(attended_hi, n + 1)
                    nc.vector.tensor_tensor(attended[1][:, b, j, :], ps_out[:, OUTPUTS.index((s, "attend", 0)) % 2, :],
                                            attended[0][:, b, j, :].bitcast(F32), ALU.subtract).then_inc(attended_split, 1)

            for s in (4, 5, 6, 7):
                step(-1, s)
            for s in range(GROUP):
                step(0, s)
            with dve.Fori(1, KV0 - 1) as g:
                for s in range(GROUP):
                    step(g, s)
            for s in range(GROUP):
                step(KV0 - 1, s)
            for s in range(4):
                step(KV0, s)

        @block.scalar
        def _(act):
            norm.scalar(act)

            def exponent(g, s, i):
                n = GROUP * g + s + 1
                slot = (s + 1) % 2
                tile = probs[:, slot, SCORE_AT[i]:SCORE_AT[i + 1]]
                act.wait_ge(score_masked, 4 * n + i + 1)
                nc.scalar.activation(tile, tile, ACT.Exp, bias=least[:, slot, i:i + 1], scale=-1.0,
                                     accum_out=total[:, slot, i:i + 1]).then_inc(exp_done, 1)

            def round_turned(g, s, t):
                n = GROUP * g + s
                w = SEQ - t * P
                act.wait_ge(turned, 4 * n + t + 1)
                wait(act, attend_made, 4 * n + t - 1)
                nc.scalar.copy(probsT[0][:, t % 2, 0:w], ps_turn[:, t % 2, 0:w]).then_inc(turned_hi, 1)

            def round_rotated(g, s, what):
                act.wait_ge(rotation_added, rotation(g, s, what))
                if what == "query":
                    hi = query[0][:, (s + 3) % 4, :]
                    wait(act, score_made, 4 * (GROUP * g + s + 3 - 4) + 4)
                else:
                    b = 1 if s < 4 else 0
                    hi = keys[0][:, b, :]
                    wait(act, score_made, 4 * GROUP * g if b else 4 * (GROUP * g + PER_KV))
                nc.scalar.copy(hi, rotated[:]).then_inc(rotation_hi, 1)

            def step(g, s):
                n = GROUP * g + s
                if present(g, s, "score"):
                    exponent(g, s, 0)
                    exponent(g, s, 1)
                if present(g, s, "attend"):
                    round_turned(g, s, 0)
                    round_turned(g, s, 1)
                side = SIDE[s] if present(g, s, SIDE[s]) else None
                if side == "values":
                    act.wait_ge(values_made, values_count(g, s))
                    nc.scalar.copy(values_turned[:], ps_proj[:, projection_bank(g, s, "values"), :]).then_inc(values_copied, 1)
                if present(*step_before(g, s), "query"):
                    round_rotated(*step_before(g, s), "query")
                if present(g, s, "score"):
                    exponent(g, s, 2)
                    exponent(g, s, 3)
                if present(g, s, "attend"):
                    round_turned(g, s, 2)
                    round_turned(g, s, 3)
                if side == "values":
                    b = 1 if s < 4 else 0
                    act.wait_ge(values_placed, values_count(g, s))
                    wait(act, attend_made, 4 * GROUP * g if b else 4 * (GROUP * g + PER_KV))
                    nc.scalar.copy(values[0][:, b], ps_proj[:, projection_bank(g, s, "values"), :].rearrange(
                        "p (t d) -> p t d", t=QT)).then_inc(values_hi, 1)
                if present(g, s, "score"):
                    slot = (s + 1) % 2
                    act.wait_ge(total_inverted, n + 2)
                    for i in range(QT):
                        tile = probs[:, slot, SCORE_AT[i]:SCORE_AT[i + 1]]
                        nc.scalar.activation(tile, tile, ACT.Copy, scale=inverse[:, slot, i:i + 1]).then_inc(probs_ready, 1)
                if side == "keys":
                    round_rotated(g, s, "keys")
                if present(g, s, "attend"):
                    b, j = s // PER_KV, s % PER_KV
                    act.wait_ge(attend_made, 4 * n + 4)
                    wait(act, out_made, NT * g if b else NT * g - PER_KV)
                    nc.scalar.copy(attended[0][:, b, j, :],
                                   ps_out[:, OUTPUTS.index((s, "attend", 0)) % 2, :]).then_inc(attended_hi, 1)

            for s in (4, 5, 6, 7):
                step(-1, s)
            for s in range(GROUP):
                step(0, s)
            with act.Fori(1, KV0 - 1) as g:
                for s in range(GROUP):
                    step(g, s)
            for s in range(GROUP):
                step(KV0 - 1, s)



def ffn0_phase(nc, m):
    dram = m.dram
    with ExitStack() as ctx:
        def sb(what, shape, dt=F32):
            return ctx.enter_context(nc.sbuf_tensor(f"f0_{what}", shape, dt))

        def pair(what, shape):
            return sb(f"{what}_hi", shape, F32R), sb(f"{what}_lo", shape, F32R)

        def sem(what):
            return ctx.enter_context(nc.semaphore(f"f0_{what}"))

        raw = sb("raw", [P, 2, 3, 512], I32)
        gate = pair("gate", [P, 2, DC, P])
        up = pair("up", [P, 2, DC, P])
        down = pair("down", [P, FC, D])
        gate_s, up_s = sb("gate_s", [P, FC]), sb("up_s", [P, FC])
        down_s = sb("down_s", [P, D])
        gate_col, up_col = sb("gate_col", [P, 2]), sb("up_col", [P, 2])
        silu = sb("silu", [P, 2, SEQ])
        hidden = sb("hidden", [P, 2, SEQ])
        hidden0 = pair("hidden0", [P, 2, SEQ])
        hidden1 = pair("hidden1", [P, FC, SEQ])
        ps_gate = ctx.enter_context(nc.psum_tensor("f0_ps_gate", [P, 2, 512], F32))
        ps_up = ctx.enter_context(nc.psum_tensor("f0_ps_up", [P, 2, 512], F32))
        ps_out = ctx.enter_context(nc.psum_tensor("f0_ps_out", [P, QT, 512], F32))

        raw_in = [[sem(f"{w}_in{s}") for w in ("gate", "up", "down")] for s in range(2)]
        scales_in = sem("scales_in")
        weights_hi, weights_split = sem("weights_hi"), sem("weights_split")
        columns_copied = sem("columns_copied")
        made, silu_done, hidden_made = sem("made"), sem("silu_done"), sem("hidden_made")
        hidden_hi, hidden_split = sem("hidden_hi"), sem("hidden_split")
        summed, out_done, out_scaled, out_added = sem("summed"), sem("out_done"), sem("out_scaled"), sem("out_added")
        norm = LayerNorm(nc, m, ctx, 1, [x[:, k, :] for x in (hidden, silu) for k in range(2)],
                         [ps_out[:, k, :] for k in range(4)])
        block = ctx.enter_context(nc.Block())

        @block.sync
        def _(sp):
            sp.dma_start(gate_s[:], dram["gate_s"]).then_inc(scales_in, 16)
            sp.dma_start(up_s[:], dram["up_s"]).then_inc(scales_in, 16)
            sp.dma_start(down_s[:], dram["down_s"].to_broadcast((P, D))).then_inc(scales_in, 16)

            def fetch(f, k):
                wait(sp, weights_split, 3 * f - 3)
                for w, name in enumerate(("gate", "up", "down")):
                    sp.dma_start(raw[:, k, w, :], dram[name][f]).then_inc(raw_in[k][w], 16)

            fetch(0, 0)
            fetch(1, 1)
            with sp.Fori(1, FC // 2) as i:
                for k in range(2):
                    fetch(2 * i + k, k)

        def split_hi(act, f, k, use):
            for w, hi in enumerate((gate[0][:, k], up[0][:, k], down[0][:, f, :])):
                act.wait_ge(raw_in[k][w], 16 * use)
                if w == 0:
                    wait(act, made, 2 * f - 2)
                src = raw[:, k, w, :]
                if w < 2:
                    src = src.rearrange("p (c n) -> p c n", c=DC)
                nc.scalar.copy(hi, src).then_inc(weights_hi, 1)

        def split_lo(dve, f, k):
            for w, (hi, lo) in enumerate(((gate[0][:, k], gate[1][:, k]), (up[0][:, k], up[1][:, k]),
                                          (down[0][:, f, :], down[1][:, f, :]))):
                src = raw[:, k, w, :]
                if w < 2:
                    src = src.rearrange("p (c n) -> p c n", c=DC)
                dve.wait_ge(weights_hi, 3 * f + w + 1)
                nc.vector.tensor_tensor(lo, src, hi.bitcast(F32), ALU.subtract).then_inc(weights_split, 1)

        @block.scalar
        def _(act):
            norm.scalar(act)
            split_hi(act, 0, 0, 1)

            def chunk(f, k, use, last=False):
                if not last:
                    split_hi(act, f + 1, 1 - k, use + k)
                for b in range(BATCH):
                    q = 2 * f + b
                    act.wait_ge(columns_copied, f + 1)
                    act.wait_ge(made, q + 1)
                    wait(act, hidden_made, q - 1)
                    nc.scalar.activation(silu[:, b, :], ps_gate[:, b, :], ACT.Silu,
                                         scale=gate_col[:, k:k + 1]).then_inc(silu_done, 1)
                    act.wait_ge(hidden_made, q + 1)
                    if b == 0:
                        wait(act, summed, f - 1)
                        hi = hidden0[0][:, k, :]
                    else:
                        hi = hidden1[0][:, f, :]
                    nc.scalar.copy(hi, hidden[:, b, :]).then_inc(hidden_hi, 1)

            chunk(0, 0, 1)
            chunk(1, 1, 1)
            with act.Fori(1, FC // 2 - 1) as i:
                for k in range(2):
                    chunk(2 * i + k, k, i + 1)
            chunk(FC - 2, 0, FC // 2)
            chunk(FC - 1, 1, FC // 2, last=True)

        @block.vector
        def _(dve):
            def copy_columns(f, k):
                if isinstance(f, int) and f == 0:
                    dve.wait_ge(scales_in, 48)
                wait(dve, hidden_made, 2 * f - 2)
                nc.vector.tensor_copy(gate_col[:, k:k + 1], gate_s[:, bass.ds(f, 1)])
                nc.vector.tensor_copy(up_col[:, k:k + 1], up_s[:, bass.ds(f, 1)]).then_inc(columns_copied, 1)

            norm.vector(dve)
            copy_columns(0, 0)
            split_lo(dve, 0, 0)

            def chunk(f, k, last=False):
                if not last:
                    copy_columns(f + 1, 1 - k)
                    split_lo(dve, f + 1, 1 - k)
                for b in range(BATCH):
                    q = 2 * f + b
                    dve.wait_ge(columns_copied, f + 1)
                    dve.wait_ge(silu_done, q + 1)
                    wait(dve, hidden_split, q - 1)
                    nc.vector.scalar_tensor_tensor(hidden[:, b, :], ps_up[:, b, :], up_col[:, k:k + 1], silu[:, b, :],
                                                   ALU.mult, ALU.mult).then_inc(hidden_made, 1)
                    hi, lo = (hidden0[0][:, k, :], hidden0[1][:, k, :]) if b == 0 else \
                             (hidden1[0][:, f, :], hidden1[1][:, f, :])
                    dve.wait_ge(hidden_hi, q + 1)
                    nc.vector.tensor_tensor(lo, hidden[:, b, :], hi.bitcast(F32), ALU.subtract).then_inc(hidden_split, 1)

            for f in range(2):
                chunk(f, f)
            with dve.Fori(1, FC // 2 - 1) as i:
                for k in range(2):
                    chunk(2 * i + k, k)
            chunk(FC - 2, 0)
            chunk(FC - 1, 1, last=True)
            for t in range(NT):
                dve.wait_ge(out_done, t + 1)
                nc.vector.tensor_tensor(hidden[:, t % 2, :], ps_out[:, t % QT, :], down_s[:], ALU.mult).then_inc(out_scaled, 1)
                dve.wait_ge(out_scaled, t + 1)
                nc.vector.tensor_tensor(m.x[:, t, :], m.x[:, t, :], hidden[:, t % 2, :], ALU.add).then_inc(out_added, 1)
                dve.wait_ge(out_added, t + 1)
                take_moments(nc, dve, m, 2, t)

        @block.tensor
        def _(pe):
            def make(f, k, b):
                q = 2 * f + b
                if b == 0:
                    pe.wait_ge(weights_split, 3 * f + 3)
                wait(pe, hidden_made, q - 1)
                for out, w in ((ps_gate, gate), (ps_up, up)):
                    for c in range(DC):
                        at = slice(b * SEQ, (b + 1) * SEQ)
                        last = product(nc, out[:, b, :], (w[0][:, k, c, :], w[1][:, k, c, :]),
                                       (m.xT_hi[:, c, at], m.xT_lo[:, c, at]), c == 0, c == DC - 1)
                last.then_inc(made, 1)

            def add_to_sums(f, k, first=False, last=False):
                pe.wait_ge(hidden_split, 2 * f + 1)
                for t in range(QT):
                    at = slice(t * P, (t + 1) * P)
                    mm = product(nc, ps_out[:, t, :], (hidden0[0][:, k, at], hidden0[1][:, k, at]),
                                 (down[0][:, f, :], down[1][:, f, :]), first, last)
                    if last:
                        mm.then_inc(out_done, 1)
                    elif t == QT - 1:
                        mm.then_inc(summed, 1)

            norm.tensor(pe)
            make(0, 0, 0)
            make(0, 0, 1)
            make(1, 1, 0)
            add_to_sums(0, 0, first=True)
            make(1, 1, 1)
            with pe.Fori(1, FC // 2) as i:
                for k in range(2):
                    make(2 * i + k, k, 0)
                    add_to_sums(2 * i + k - 1, 1 - k)
                    make(2 * i + k, k, 1)
            add_to_sums(FC - 1, 1, last=True)
            pe.wait_ge(hidden_split, 2 * FC)
            for t in range(QT):
                at = slice(t * P, (t + 1) * P)
                pe.wait_ge(out_scaled, t + 1)
                for f in range(FC):
                    mm = product(nc, ps_out[:, t, :], (hidden1[0][:, f, at], hidden1[1][:, f, at]),
                                 (down[0][:, f, :], down[1][:, f, :]), f == 0, f == FC - 1)
                mm.then_inc(out_done, 1)


HPC = P // HD1
CHUNKS1 = HEADS1 // HPC
STEPS1 = 2 * HPC
UNITS1 = CHUNKS1 * STEPS1
PAIRS = HPC // 2
TURNED_AT = [0, SEQ, 2 * SEQ - P]
TURNED_WIDTH = [SEQ, SEQ - P, SEQ - P]
KEY_AT = [0, SEQ, 2 * SEQ - P, 3 * SEQ - 3 * P]
SIDE1 = {0: "keys", 1: "values", 2: "spread", 3: "out", 4: "out", 5: "out", 6: "out", 7: "query"}


def attention1_phase(nc, m):
    dram = m.dram
    with ExitStack() as ctx:
        def sb(what, shape, dt=F32):
            return ctx.enter_context(nc.sbuf_tensor(f"a1_{what}", shape, dt))

        def pair(what, shape):
            return sb(f"{what}_hi", shape, F32R), sb(f"{what}_lo", shape, F32R)

        def sem(what):
            return ctx.enter_context(nc.semaphore(f"a1_{what}"))

        raw = sb("raw", [P, 4, 512])
        zeros = sb("zeros", [P, 512])
        wq, wk, wv = pair("wq", [P, DC, P]), pair("wk", [P, DC, P]), pair("wv", [P, DC, P])
        wo = pair("wo", [P, D])
        bias = sb("bias", [P, 3, CHUNKS1])
        value_bias = sb("value_bias", [P, 1])
        out_bias = sb("out_bias", [P, D])
        biased_q, biased_k = sb("biased_q", [P, SEQ]), sb("biased_k", [P, SEQ])
        query, keys = pair("query", [P, SEQ]), pair("keys", [P, SEQ])
        stacked_q = sb("stacked_q", [P, BATCH, PAIRS, 2, SEQ], F32R)
        stacked_k = sb("stacked_k", [P, BATCH, PAIRS, SEQ], F32R)
        values_turned = sb("values_turned", [P, SEQ])
        values = sb("values", [P, BATCH, QT, HPC, 2, HD1], F32R)
        causal = sb("causal", [P, SEQ])
        probs = sb("probs", [P, 4, SCORE_AT[QT]])
        least = sb("least", [P, 4, QT])
        total = sb("total", [P, 2, QT, 4])
        inverse = sb("inverse", [P, QT, 4])
        probsT = pair("probsT", [P, 2, SCORE_AT[QT]])
        gathered = sb("gathered", [P, SEQ])
        summed = sb("summed", [P, QT, 4, HD1])
        result = sb("result", [P, QT, HPC, HD1])
        attended = pair("attended", [P, SEQ])

        ps_score = ctx.enter_context(nc.psum_tensor("a1_ps_score", [P, 2, 512], F32))
        ps_turn = ctx.enter_context(nc.psum_tensor("a1_ps_turn", [P, 3, 512], F32))
        ps_attend = ctx.enter_context(nc.psum_tensor("a1_ps_attend", [P, SEQ], F32))
        ps_back = ctx.enter_context(nc.psum_tensor("a1_ps_back", [P, QT, P], F32))
        ps_side = ctx.enter_context(nc.psum_tensor("a1_ps_side", [P, 512], F32))

        raw_in = [sem(f"{w}_in") for w in ("wq", "wk", "wv", "wo")]
        query_out, keys_out, stacked_q_in, stacked_k_in = sem("query_out"), sem("keys_out"), sem("stacked_q_in"), sem("stacked_k_in")
        consts_in, pick_in, zeros_set, stack_zero = sem("consts_in"), sem("pick_in"), sem("zeros_set"), sem("stack_zero")
        wait_passed, wait_passed_sp = sem("wait_passed"), sem("wait_passed_sp")
        wait_passed_pool = sem("wait_passed_pool")
        piece_hi, piece_split = sem("piece_hi"), sem("piece_split")
        side_made, side_read = sem("side_made"), sem("side_read")
        operand_hi, operand_split, values_hi = sem("operand_hi"), sem("operand_split"), sem("values_hi")
        score_made, score_masked, exp_done = sem("score_made"), sem("score_masked"), sem("exp_done")
        turned, turned_hi, turned_split, attend_made = sem("turned"), sem("turned_hi"), sem("turned_split"), sem("attend_made")
        total_inverted, attend_summed, result_made = sem("total_inverted"), sem("attend_summed"), sem("result_made")
        value_bias_set, attended_hi, bias_added = sem("value_bias_set"), sem("attended_hi"), sem("bias_added")
        attend_read, gathered_turned = sem("attend_read"), sem("gathered_turned")
        result_turned, attended_split = sem("result_turned"), sem("attended_split")

        def side(c, s):
            what = SIDE1[s % 8]
            if not isinstance(c, int):
                return what
            if what == "out":
                there = 1 <= c if s < 8 else 0 <= c < CHUNKS1
            elif what == "query" or s >= 8:
                there = c < CHUNKS1 - 1
            else:
                there = 0 <= c < CHUNKS1
            return what if there else None

        def side_count(c, s):
            if not isinstance(c, int):
                return STEPS1 * c + s + 2
            steps = [(-1, k) for k in range(7, STEPS1)] + [(d, k) for d in range(CHUNKS1 + 1) for k in range(8 if d == CHUNKS1 else STEPS1)]
            return len([x for x in steps if side(*x) and x <= (c, s)])

        def earlier(c, s, steps):
            c, s = (c, s - steps) if s >= steps else (c - 1, s - steps + STEPS1)
            return c, s, side(c, s)

        def period(c, s):
            return 2 * c + {"keys": 1, "values": 1, "spread": 1, "query": 2, "out": -1}[SIDE1[s % 8]] + s // 8

        def batch_of(s):
            return (1 if SIDE1[s % 8] != "query" else 0) ^ s // 8

        def operand_count(c, s):
            return 3 + 4 * c + {0: 1, 7: 2, 8: 3, 15: 4}[s]

        def piece_count(c, what):
            if what == "wo":
                return 3 + 4 * c + (1 if isinstance(c, int) and c == CHUNKS1 - 1 else 4)
            at = ("wq", "wk", "wv").index(what)
            return at + 1 if isinstance(c, int) and c == 0 else 3 + 4 * (c - 1) + at + 1

        def unit(c, s, ahead):
            c, u = (c, s + ahead) if s + ahead < STEPS1 else (c + 1, s + ahead - STEPS1)
            return (c, u) if not isinstance(c, int) or 0 <= c < CHUNKS1 else None

        def result_period(c, s):
            return 2 * c - 1 + s // 8 if s % 8 == 1 and (not isinstance(c, int) or (1 <= c if s < 8 else 0 <= c < CHUNKS1)) else None

        def each_chunk(engine, step):
            for s in range(7, STEPS1):
                step(-1, s)
            for s in range(STEPS1):
                step(0, s)
            with engine.Fori(1, CHUNKS1 - 1) as c:
                for s in range(STEPS1):
                    step(c, s)
            for s in range(STEPS1):
                step(CHUNKS1 - 1, s)
            for s in range(8):
                step(CHUNKS1, s)

        DMAS_Q, DMAS_K = 6, 4
        spill_q = nc.dram_tensor("a1_spill_q", (BATCH, 2, P, SEQ), F32).ap()
        spill_k = nc.dram_tensor("a1_spill_k", (BATCH, 2, P, SEQ), F32).ap()
        norm = LayerNorm(nc, m, ctx, 2, [probs[:, k, 0:D] for k in range(4)],
                         [ps[:, k, :] for ps in (ps_turn, ps_score) for k in range(2)])
        block = ctx.enter_context(nc.Block())

        @block.sync
        def _(sp):
            for w, name in enumerate(("wq1", "wk1", "wv1")):
                sp.dma_start(raw[:, w, :], dram[name][0]).then_inc(raw_in[w], 16)
            for dst, src in ((bias[:], dram["bias1"]), (causal[:], dram["causal"]),
                             (out_bias[:], dram["out_bias"].to_broadcast((P, D)))):
                sp.dma_start(dst, src).then_inc(consts_in, 16)
            sp.dma_start(raw[:, 3, :], dram["wo1"][0]).then_inc(raw_in[3], 16)

            def write_out(c, s):
                what, b = SIDE1[s % 8], batch_of(s)
                wait(sp, operand_split, operand_count(c, s))
                sp.sem_inc(wait_passed_sp, 1)
                if what == "query":
                    wait(sp, stacked_q_in, 16 * DMAS_Q * (period(c, s) - 1))
                else:
                    wait(sp, stacked_k_in, 16 * DMAS_K * (period(c, s) - 1))
                for part in range(2):
                    src, dst, done = (query, spill_q, query_out) if what == "query" else (keys, spill_k, keys_out)
                    sp.dma_start(dst[b, part], src[part][:].bitcast(F32)).then_inc(done, 16)

            def load(c, what, of):
                w = ("wq", "wk", "wv", "wo").index(what)
                wait(sp, piece_split, piece_count(of - 1, what))
                sp.sem_inc(wait_passed_sp, 1)
                sp.dma_start(raw[:, w, :], dram[what + "1"][of]).then_inc(raw_in[w], 16)

            def chunk(c):
                write_out(c, 0)
                if not isinstance(c, int) or c < CHUNKS1 - 1:
                    for what in ("wq", "wk", "wv"):
                        load(c, what, c + 1)
                if not isinstance(c, int) or c > 0:
                    load(c, "wo", c)
                if not isinstance(c, int) or c < CHUNKS1 - 1:
                    for s in (7, 8, 15):
                        write_out(c, s)

            for s in (7, 8, 15):
                write_out(-1, s)
            chunk(0)
            with sp.Fori(1, CHUNKS1 - 1) as c:
                chunk(c)
            chunk(CHUNKS1 - 1)

        @block.gpsimd
        def _(pool):
            nc.gpsimd.memset(zeros[:], 0.0).then_inc(zeros_set, 1)
            pool.dma_start(stacked_q[96:P].rearrange("p b a e n -> p (b a e n)"), dram["pick"]).then_inc(pick_in, 16)
            pool.wait_ge(zeros_set, 1)

            def read_back(c, s):
                what, b = SIDE1[s % 8], batch_of(s)
                p = period(c, s)
                wait(pool, score_made, 4 * HPC * (p - 1))
                wait(pool, query_out if what == "query" else keys_out, 2 * 16 * (p + 1))
                pool.sem_inc(wait_passed_pool, 1)
                if what == "query":
                    for place, part in enumerate((0, 0, 1)):
                        for e in range(2):
                            rows = spill_q[b, part].rearrange("(a e d) n -> e d a n", a=PAIRS, e=2)
                            at = 32 * place + HD1 * e
                            pool.dma_start(stacked_q[at:at + HD1, b, :, e, :], rows[e]).then_inc(stacked_q_in, 16)
                else:
                    for place, part in enumerate((0, 1, 0)):
                        rows = spill_k[b, part].rearrange("(a r) n -> r a n", a=PAIRS)
                        pool.dma_start(stacked_k[32 * place:32 * place + 32, b], rows).then_inc(stacked_k_in, 16)
                    pool.dma_start(stacked_k[96:P, b].rearrange("p a n -> p (a n)"),
                                   dram["slope"][c if s < 8 else c + 1]).then_inc(stacked_k_in, 16)

            def split(landed, count, what):
                w = ("wq", "wk", "wv", "wo").index(what)
                pair_ = (wq, wk, wv, wo)[w]
                src, zero = raw[:, w, :], zeros[:]
                if what != "wo":
                    src, zero = (x.rearrange("p (c n) -> p c n", c=DC) for x in (src, zero))
                pool.wait_ge(raw_in[w], 16 * landed)
                nc.gpsimd.tensor_tensor(pair_[0][:], src, zero, ALU.add).then_inc(piece_hi, 1)
                pool.wait_ge(piece_hi, count)
                nc.gpsimd.tensor_tensor(pair_[1][:], src, pair_[0][:].bitcast(F32), ALU.subtract).then_inc(piece_split, 1)

            def chunk(c):
                more = not isinstance(c, int) or c < CHUNKS1 - 1
                if more:
                    wait(pool, side_made, side_count(c - 1, 15))
                    split(c + 2, piece_count(c + 1, "wq"), "wq")
                read_back(c, 0)
                if more:
                    for what, s in (("wk", 0), ("wv", 1)):
                        wait(pool, side_made, side_count(c, s))
                        split(c + 2, piece_count(c + 1, what), what)
                wait(pool, side_made, side_count(c, 6))
                split(c + 1, piece_count(c, "wo"), "wo")
                if more:
                    for s in (7, 8, 15):
                        read_back(c, s)

            for what in ("wq", "wk", "wv"):
                split(1, piece_count(0, what), what)
            nc.gpsimd.memset(stacked_q[0:96].rearrange("p b a e n -> p (b a e n)").bitcast(F32), 0.0).then_inc(stack_zero, 1)
            pool.wait_ge(stack_zero, 1)
            for s in (7, 8, 15):
                read_back(-1, s)
            pool.wait_ge(consts_in, 16 * 3)
            pool.wait_ge(m.ln_semaphores[LN_SEMAPHORES.index("normal_done")], 3 * NT)
            for t in range(NT):
                nc.gpsimd.tensor_tensor(m.x[:, t, :], m.x[:, t, :], out_bias[:], ALU.add).then_inc(bias_added, 1)
            chunk(0)
            with pool.Fori(1, CHUNKS1 - 1) as c:
                chunk(c)
            chunk(CHUNKS1 - 1)

        @block.tensor
        def _(pe):
            def side_work(c, s):
                what, b = side(c, s), batch_of(s)
                if what in ("query", "keys", "values"):
                    w = {"query": wq, "keys": wk, "values": wv}[what]
                    of = c + 1 if what == "query" or s >= 8 else c
                    wait(pe, piece_split, piece_count(of, {"query": "wq", "keys": "wk", "values": "wv"}[what]))
                elif what == "out":
                    wait(pe, attended_split, period(c, s) + 1)
                    wait(pe, piece_split, piece_count(c if s >= 8 else c - 1, "wo"))
                wait(pe, side_read, side_count(c, s) - 1)
                at = slice(b * SEQ, (b + 1) * SEQ)
                if what in ("query", "keys", "values"):
                    for k in range(DC):
                        last = product(nc, ps_side[:], [x[:, k, :] for x in w],
                                       (m.xT_hi[:, k, at], m.xT_lo[:, k, at]), k == 0, k == DC - 1)
                elif what == "spread":
                    for t in range(QT):
                        last = nc.tensor.transpose(ps_side[:, t * P:(t + 1) * P], values_turned[:, t * P:(t + 1) * P], m.ident[:])
                else:
                    t = s % 8 - 3
                    last = product(nc, ps_side[:], [x[:, t * P:(t + 1) * P] for x in attended], [x[:] for x in wo], True, True)
                last.then_inc(side_made, 1)

            def score(cu, u, i):
                n, b, j = STEPS1 * cu + u, u // HPC, u % HPC
                if i == 0 and j == 0:
                    wait(pe, stacked_q_in, 16 * DMAS_Q * (2 * cu + b + 1))
                    wait(pe, stacked_k_in, 16 * DMAS_K * (2 * cu + b + 1))
                wait(pe, score_masked, 4 * n + i - 1)
                nc.tensor.matmul(ps_score[:, i % 2, 0:P * (i + 1)], stacked_q[:, b, j // 2, j % 2, i * P:(i + 1) * P],
                                 stacked_k[:, b, j // 2, 0:P * (i + 1)], start=True, stop=True).then_inc(score_made, 1)

            def turn(cu, u, t):
                n = STEPS1 * cu + u
                if t == 0:
                    wait(pe, exp_done, 4 * n + 4)
                wait(pe, turned_split, 3 * n - 2 + t)
                for k in ((t,) if t < 2 else (2, 3)):
                    for i in range(k, QT):
                        at = SCORE_AT[i] + k * P
                        to = KEY_AT[k] - TURNED_AT[t] + (i - k) * P
                        last = nc.tensor.transpose(ps_turn[:, t, to:to + P], probs[:, u % 4, at:at + P], m.ident[:])
                last.then_inc(turned, 1)

            def attend(cu, u, part):
                n, b, j = STEPS1 * cu + u, u // HPC, u % HPC
                if part == 0:
                    if j == 0:
                        wait(pe, side_read, side_count(cu, 2) if b else side_count(cu - 1, 10))
                    wait(pe, attend_read, n)
                    wait(pe, turned_split, 3 * n + 3)
                for k in range(QT):
                    last = nc.tensor.matmul(
                        ps_attend[0:2 * HD1, k * P:SEQ], values[:, b, k, j].rearrange("p h d -> p (h d)"),
                        probsT[part][:, u % 2, KEY_AT[k]:KEY_AT[k] + SEQ - k * P],
                        start=part == 0 and k == 0, stop=part == 1 and k == QT - 1)
                if part == 1:
                    last.then_inc(attend_made, 1)

            def turn_gathered(cu, u):
                four = 4 * cu + u // 4
                wait(pe, attend_read, STEPS1 * cu + u + 1)
                if u // 4 % 2 == 0:
                    wait(pe, attended_split, 2 * cu + u // HPC)
                else:
                    wait(pe, result_made, four)
                for t in range(QT):
                    last = nc.tensor.transpose(ps_back[:, t], gathered[:, t * P:(t + 1) * P], m.ident[:])
                last.then_inc(gathered_turned, 1)

            def turn_result(p):
                wait(pe, result_made, 2 * p + 2)
                for t in range(QT):
                    last = nc.tensor.transpose(ps_back[:, t], result[:, t].rearrange("p j d -> p (j d)"), m.ident[:])
                last.then_inc(result_turned, 1)

            norm.tensor(pe)
            pe.wait_ge(pick_in, 16)

            def step(c, s):
                scoring, turning, attending = unit(c, s, 3), unit(c, s, 1), unit(c, s, 0)
                if turning:
                    turn(*turning, 0)
                    turn(*turning, 1)
                if scoring:
                    score(*scoring, 0)
                    score(*scoring, 1)
                if turning:
                    turn(*turning, 2)
                if attending:
                    attend(*attending, 0)
                if scoring:
                    score(*scoring, 2)
                    score(*scoring, 3)
                if attending:
                    attend(*attending, 1)
                if s % 4 == 0 and unit(*earlier(c, s, 1)[:2], 0):
                    turn_gathered(*earlier(c, s, 1)[:2])
                if result_period(c, s) is not None:
                    turn_result(result_period(c, s))
                if side(c, s):
                    side_work(c, s)

            each_chunk(pe, step)

        @block.vector
        def _(dve):
            norm.vector(dve)
            dve.wait_ge(consts_in, 16 * 3)

            def add_bias(c, s):
                what = side(c, s)
                of = c + 1 if what == "query" or s >= 8 else c
                add = bias[:, 0 if what == "query" else 1, bass.ds(of, 1)]
                dve.wait_ge(side_made, side_count(c, s))
                wait(dve, operand_split, operand_count(c, s) - 2)
                if what == "query":
                    nc.vector.tensor_scalar(biased_q[:], ps_side[:], add, None, ALU.add).then_inc(side_read, 1)
                else:
                    nc.vector.tensor_scalar(biased_k[:], ps_side[:], add, None, ALU.add).then_inc(side_read, 1)

            def split_operand(c, s):
                src, (hi, lo) = (biased_q, query) if side(c, s) == "query" else (biased_k, keys)
                dve.wait_ge(operand_hi, operand_count(c, s))
                nc.vector.tensor_tensor(lo[:], src[:], hi[:].bitcast(F32), ALU.subtract).then_inc(operand_split, 1)

            def mask(cu, u, i):
                n = STEPS1 * cu + u
                at, w = SCORE_AT[i], P * (i + 1)
                if i == 0:
                    wait(dve, turned, 3 * (n - 3))
                dve.wait_ge(score_made, 4 * n + i + 1)
                dve.sem_inc(wait_passed, 1)
                nc.vector.tensor_tensor_reduce(
                    out=probs[:, u % 4, at:at + w], in0=ps_score[:, i % 2, 0:w], in1=causal[:, SEQ - w:SEQ],
                    scale=-float(HD1) ** -0.5, scalar=-LOWEST, op0=ALU.add, op1=ALU.min,
                    accum_out=least[:, u % 4, i:i + 1]).then_inc(score_masked, 1)

            def split_turned(cu, u, t):
                at = slice(TURNED_AT[t], TURNED_AT[t] + TURNED_WIDTH[t])
                dve.wait_ge(turned_hi, 3 * (STEPS1 * cu + u) + t + 1)
                nc.vector.tensor_tensor(probsT[1][:, u % 2, at], ps_turn[:, t, 0:TURNED_WIDTH[t]],
                                        probsT[0][:, u % 2, at].bitcast(F32), ALU.subtract).then_inc(turned_split, 1)

            def divide(cu, u):
                half, count = u // 4 % 2, 4 * cu + u // 4 + 1
                wait(dve, gathered_turned, count)
                nc.vector.reciprocal(inverse[:], total[:, half]).then_inc(total_inverted, 1)
                nc.vector.tensor_reduce(summed[:].rearrange("p i j d -> p (i j) d"),
                                        ps_back[:].rearrange("p i (j h d) -> p (i j) d h", j=4, h=2),
                                        mybir.AxisListType.X, ALU.add).then_inc(attend_summed, 1)
                dve.wait_ge(total_inverted, count)
                dve.wait_ge(attend_summed, count)
                nc.vector.tensor_tensor(result[:, :, 4 * half:4 * half + 4, :], summed[:],
                                        inverse[:].unsqueeze(3).to_broadcast((P, QT, 4, HD1)), ALU.mult).then_inc(result_made, 1)

            def step(c, s):
                scoring, turning = unit(c, s, 3), unit(c, s, 1)
                c1, s1, side1 = earlier(c, s, 1)
                c2, s2, side2 = earlier(c, s, 2)
                last_steps = isinstance(c, int) and c == CHUNKS1
                if s == 5 and unit(c, s, 0):
                    wait(dve, attended_split, 2 * c)
                    nc.vector.tensor_copy(value_bias[:], bias[:, 2, bass.ds(c, 1)]).then_inc(value_bias_set, 1)
                if s % 4 == 1 and unit(c2, s2, 0):
                    divide(c2, s2)
                if side1 in ("query", "keys"):
                    add_bias(c1, s1)
                elif side1 == "out":
                    t = QT * batch_of(s1) + s1 % 8 - 3
                    dve.wait_ge(side_made, side_count(c1, s1))
                    if isinstance(c1, int) and c1 == 0 and s1 == 11:
                        dve.wait_ge(bias_added, NT)
                    wait(dve, side_read, side_count(c1, s1) - 1)
                    nc.vector.tensor_tensor(m.x[:, t, :], ps_side[:], m.x[:, t, :], ALU.add).then_inc(side_read, 1)
                    if last_steps:
                        dve.wait_ge(side_read, side_count(c1, s1))
                        take_moments(nc, dve, m, 3, t)
                elif last_steps and s == 0:
                    dve.wait_ge(side_read, side_count(CHUNKS1 - 1, 14))
                    for t in range(QT):
                        take_moments(nc, dve, m, 3, t)
                at_once = isinstance(c, int) and c < 0
                if at_once and side1 in ("query", "keys"):
                    split_operand(c1, s1)
                if not at_once and side2 in ("query", "keys"):
                    split_operand(c2, s2)
                if scoring:
                    mask(*scoring, 0)
                    mask(*scoring, 1)
                if turning:
                    split_turned(*turning, 0)
                    split_turned(*turning, 1)
                if side1 == "spread":
                    b = batch_of(s1)
                    dve.wait_ge(values_hi, period(c1, s1) + 1)
                    heads = values[:, b].rearrange("p t j h d -> p (t j) h d")
                    nc.vector.tensor_tensor(heads[:, :, 1, :], ps_side[:].rearrange("p (n d) -> p n d", d=HD1),
                                            heads[:, :, 0, :].bitcast(F32), ALU.subtract).then_inc(side_read, 1)
                if result_period(c1, s1) is not None:
                    p = result_period(c1, s1)
                    dve.wait_ge(value_bias_set, c1 + 1 if s1 >= 8 else c1)
                    dve.wait_ge(attended_hi, p + 1)
                    nc.vector.scalar_tensor_tensor(attended[1][:], ps_back[:].rearrange("p t n -> p (t n)"), value_bias[:],
                                                   attended[0][:].bitcast(F32), ALU.add, ALU.subtract).then_inc(attended_split, 1)
                if scoring:
                    mask(*scoring, 2)
                    mask(*scoring, 3)
                if turning:
                    split_turned(*turning, 2)

            each_chunk(dve, step)

        @block.scalar
        def _(act):
            norm.scalar(act)
            act.wait_ge(consts_in, 16 * 3)

            def exponent(cu, u, i):
                n = STEPS1 * cu + u
                tile = probs[:, u % 4, SCORE_AT[i]:SCORE_AT[i + 1]]
                if i == 0 and u % 4 == 0:
                    wait(act, total_inverted, 4 * cu + u // 4 - 1)
                act.wait_ge(score_masked, 4 * n + i + 1)
                nc.scalar.activation(tile, tile, ACT.Exp, bias=least[:, u % 4, i:i + 1], scale=-1.0,
                                     accum_out=total[:, u // 4 % 2, i, u % 4:u % 4 + 1]).then_inc(exp_done, 1)

            def round_turned(cu, u, t):
                n = STEPS1 * cu + u
                at = slice(TURNED_AT[t], TURNED_AT[t] + TURNED_WIDTH[t])
                if t == 0:
                    wait(act, attend_made, n - 1)
                act.wait_ge(turned, 3 * n + t + 1)
                nc.scalar.copy(probsT[0][:, u % 2, at], ps_turn[:, t, 0:TURNED_WIDTH[t]]).then_inc(turned_hi, 1)

            def gather(cu, u):
                rows, four = slice(32 * (u % 4), 32 * (u % 4) + 32), 4 * cu + u // 4
                if u % 4 == 0:
                    wait(act, gathered_turned, four)
                act.wait_ge(attend_made, STEPS1 * cu + u + 1)
                nc.scalar.copy(gathered[rows], ps_attend[0:2 * HD1]).then_inc(attend_read, 1)

            def round_operand(c, s):
                what = side(c, s)
                src, hi = (biased_q, query[0]) if what == "query" else (biased_k, keys[0])
                wait(act, query_out if what == "query" else keys_out, 2 * 16 * period(c, s))
                act.wait_ge(side_read, side_count(c, s))
                nc.scalar.copy(hi[:], src[:]).then_inc(operand_hi, 1)

            def step(c, s):
                masked, turning = unit(c, s, 2), unit(c, s, 1)
                c1, s1, side1 = earlier(c, s, 1)
                if masked:
                    exponent(*masked, 0)
                    exponent(*masked, 1)
                if turning:
                    for t in range(3):
                        round_turned(*turning, t)
                if side1 == "values":
                    act.wait_ge(side_made, side_count(c1, s1))
                    nc.scalar.copy(values_turned[:], ps_side[:]).then_inc(side_read, 1)
                elif side1 == "spread":
                    act.wait_ge(side_made, side_count(c1, s1))
                    heads = values[:, batch_of(s1)].rearrange("p t j h d -> p (t j) h d")
                    nc.scalar.copy(heads[:, :, 0, :], ps_side[:].rearrange("p (n d) -> p n d", d=HD1)).then_inc(values_hi, 1)
                if result_period(c1, s1) is not None:
                    act.wait_ge(value_bias_set, c1 + 1 if s1 >= 8 else c1)
                    act.wait_ge(result_turned, result_period(c1, s1) + 1)
                    nc.scalar.activation(attended[0][:], ps_back[:].rearrange("p t n -> p (t n)"), ACT.Identity,
                                         bias=value_bias[:]).then_inc(attended_hi, 1)
                if masked:
                    exponent(*masked, 2)
                    exponent(*masked, 3)
                if unit(c, s, 0):
                    gather(c, s)
                if side1 in ("query", "keys"):
                    round_operand(c1, s1)

            each_chunk(act, step)



def moe_phase(nc, m, out):
    dram = m.dram
    with ExitStack() as ctx:
        def sb(what, shape, dt=F32):
            return ctx.enter_context(nc.sbuf_tensor(f"moe_{what}", shape, dt))

        def pair(what, shape):
            return sb(f"{what}_hi", shape, F32R), sb(f"{what}_lo", shape, F32R)

        def sem(what):
            return ctx.enter_context(nc.semaphore(f"moe_{what}"))

        KC = KR // P
        down_raw = sb("down_raw", [P, DC, KR])
        up_raw = sb("up_raw", [P, KC, D])
        router_raw = sb("router_raw", [P, DC, EXPERTS])
        zeros = sb("zeros", [P, D])
        down, up, router = pair("down", [P, DC, KR]), pair("up", [P, KC, D]), pair("router", [P, DC, EXPERTS])
        scoresT = sb("scoresT", [EXPERTS, TOK])
        scores = sb("scores", [P, 2, EXPERTS])
        left1, left2 = sb("left1", [P, 2, EXPERTS]), sb("left2", [P, 2, EXPERTS])
        top1, top2 = sb("top1", [P, 2, 8]), sb("top2", [P, 2, 8])
        lowest = sb("lowest", [P, 2])
        chosen = sb("chosen", [P, 2, EXPERTS])
        expd = sb("expd", [P, 2, EXPERTS])
        gated = sb("gated", [P, 2, EXPERTS])
        total, inverse = sb("total", [P, 2]), sb("inverse", [P, 2])
        gates = sb("gates", [P, 2, EXPERTS])
        ranks = sb("ranks", [P, 2, KR])
        ranksT = pair("ranksT", [P, 2, KC, P])

        ps_score = ctx.enter_context(nc.psum_tensor("moe_ps_score", [P, 512], F32))
        ps_rank = ctx.enter_context(nc.psum_tensor("moe_ps_rank", [P, 2, 2, 512], F32))
        ps_turn = ctx.enter_context(nc.psum_tensor("moe_ps_turn", [P, 2, 512], F32))
        ps_out = ctx.enter_context(nc.psum_tensor("moe_ps_out", [P, 512], F32))

        router_in, down_in, up_in = sem("router_in"), [sem(f"down_in{i}") for i in range(DC)], [sem(f"up_in{i}") for i in range(2)]
        weights_hi, weights_split = sem("weights_hi"), sem("weights_split")
        scoresT_made, scoresT_copied = sem("scoresT_made"), sem("scoresT_copied")
        score_made, ranks_made, turned, out_made = sem("score_made"), sem("ranks_made"), sem("turned"), sem("out_made")
        picked, exp_done, gates_made = sem("picked"), sem("exp_done"), sem("gates_made")
        ranks_gated, turned_hi, turned_split, added, stored = sem("ranks_gated"), sem("turned_hi"), sem("turned_split"), sem("added"), sem("stored")
        up_hi, up_split, zeros_set = sem("up_hi"), sem("up_split"), sem("zeros_set")
        norm = LayerNorm(nc, m, ctx, 3, [ranks[:, k // 2, k % 2 * D:(k % 2 + 1) * D] for k in range(4)],
                         [ps_turn[:, 0, :], ps_turn[:, 1, :], ps_rank[:, 0, 0, :], ps_rank[:, 0, 1, :]])
        block = ctx.enter_context(nc.Block())
        pieces = [(router_raw[:], router, slice(None), router_in)]
        pieces += [(down_raw[:, c, :], down, c, down_in[c]) for c in range(DC)]

        @block.gpsimd
        def _(pool):
            nc.gpsimd.memset(zeros[:], 0.0).then_inc(zeros_set, 1)
            pool.wait_ge(zeros_set, 1)
            for k in range(KC):
                if k % 4 == 0:
                    pool.wait_ge(up_in[k // 4], 16)
                nc.gpsimd.tensor_tensor(up[0][:, k, :], up_raw[:, k, :], zeros[:], ALU.add).then_inc(up_hi, 1)
                pool.wait_ge(up_hi, k + 1)
                nc.gpsimd.tensor_tensor(up[1][:, k, :], up_raw[:, k, :], up[0][:, k, :].bitcast(F32), ALU.subtract).then_inc(up_split, 1)

        @block.sync
        def _(sp):
            sp.dma_start(router_raw[:], dram["router"]).then_inc(router_in, 16)
            for c in range(DC):
                sp.dma_start(down_raw[:, c, :], dram["down1"][:, c, :]).then_inc(down_in[c], 16)
            for i in range(2):
                sp.dma_start(up_raw[:, 4 * i:4 * i + 4, :], dram["up1"][:, 4 * i:4 * i + 4, :]).then_inc(up_in[i], 16)
            for t in range(NT):
                sp.wait_ge(added, t + 1)
                sp.dma_start(out[t * P:(t + 1) * P, :], m.x[:, t, :]).then_inc(stored, 16)
            sp.wait_ge(stored, 16 * NT)

        @block.tensor
        def _(pe):
            def make_scores():
                pe.wait_ge(weights_split, 1)
                for half in range(2):
                    at = slice(half * 512, (half + 1) * 512)
                    for c in range(DC):
                        last = product(nc, ps_rank[0:EXPERTS, 1, half, :], [x[:, c, :] for x in router],
                                       (m.xT_hi[:, c, at], m.xT_lo[:, c, at]), c == 0, c == DC - 1)
                    last.then_inc(scoresT_made, 1)

            def turn_scores():
                pe.wait_ge(scoresT_copied, 2)
                for t in range(NT):
                    last = nc.tensor.transpose(ps_score[:, t * EXPERTS:(t + 1) * EXPERTS], scoresT[:, t * P:(t + 1) * P],
                                               m.ident[0:EXPERTS, 0:EXPERTS])
                last.then_inc(score_made, 1)

            def rank(t):
                at = slice(t * P, (t + 1) * P)
                if t >= 2:
                    pe.wait_ge(ranks_gated, 2 * (t - 1))
                for c in range(DC):
                    if t == 0:
                        pe.wait_ge(weights_split, 2 + c)
                    for half in range(2):
                        last = product(nc, ps_rank[:, t % 2, half, :], (m.xT_hi[:, c, at], m.xT_lo[:, c, at]),
                                       [x[:, c, half * 512:(half + 1) * 512] for x in down], c == 0, c == DC - 1)
                last.then_inc(ranks_made, 1)

            def turn(t):
                for half in range(2):
                    pe.wait_ge(ranks_gated, 2 * t + half + 1)
                    wait(pe, turned_split, 2 * t + half - 1)
                    for k in range(4):
                        at = (4 * half + k) * P
                        last = nc.tensor.transpose(ps_turn[:, half, k * P:(k + 1) * P], ranks[:, t % 2, at:at + P], m.ident[:])
                    last.then_inc(turned, 1)

            def make_out(t):
                if t >= 1:
                    pe.wait_ge(added, t)
                for k in range(KC):
                    if k % 4 == 0:
                        pe.wait_ge(turned_split, 2 * t + k // 4 + 1)
                        if t == 0:
                            pe.wait_ge(up_split, k + 4)
                    last = product(nc, ps_out[:], [x[:, t % 2, k, :] for x in ranksT], [x[:, k, :] for x in up], k == 0, k == KC - 1)
                last.then_inc(out_made, 1)

            norm.tensor(pe)
            make_scores()
            rank(0)
            turn_scores()
            for t in range(NT):
                turn(t)
                if t + 1 < NT:
                    rank(t + 1)
                make_out(t)

        @block.vector
        def _(dve):
            def split_lo(i):
                src, (hi, lo), at, _ = pieces[i]
                dve.wait_ge(weights_hi, i + 1)
                nc.vector.tensor_tensor(lo[:, at], src, hi[:, at].bitcast(F32), ALU.subtract).then_inc(weights_split, 1)

            def pick(t):
                k = t % 2
                dve.wait_ge(score_made, 1)
                nc.vector.tensor_copy(scores[:, k, :], ps_score[:, t * EXPERTS:(t + 1) * EXPERTS]).then_inc(picked, 1)
                dve.wait_ge(picked, 5 * t + 1)
                nc.vector.max(top1[:, k, :], scores[:, k, :]).then_inc(picked, 1)
                dve.wait_ge(picked, 5 * t + 2)
                nc.vector.tensor_scalar(lowest[:, k:k + 1], top1[:, k, 0:1], -1.0, None, ALU.mult)
                nc.vector.match_replace(left1[:, k, :], top1[:, k, :], scores[:, k, :], LOWEST).then_inc(picked, 1)
                dve.wait_ge(picked, 5 * t + 3)
                nc.vector.max(top2[:, k, :], left1[:, k, :]).then_inc(picked, 1)
                dve.wait_ge(picked, 5 * t + 4)
                nc.vector.match_replace(left2[:, k, :], top2[:, k, :], left1[:, k, :], LOWEST).then_inc(picked, 1)
                dve.wait_ge(picked, 5 * t + 5)
                nc.vector.tensor_scalar(chosen[:, k, :], left2[:, k, :], LOWEST, None, ALU.is_equal).then_inc(gates_made, 1)
                dve.wait_ge(gates_made, 4 * t + 1)
                dve.wait_ge(exp_done, t + 1)
                nc.vector.tensor_tensor_reduce(out=gated[:, k, :], in0=expd[:, k, :], in1=chosen[:, k, :], scale=1.0, scalar=0.0,
                                               op0=ALU.mult, op1=ALU.add, accum_out=total[:, k:k + 1]).then_inc(gates_made, 1)
                dve.wait_ge(gates_made, 4 * t + 2)
                nc.vector.reciprocal(inverse[:, k:k + 1], total[:, k:k + 1]).then_inc(gates_made, 1)
                dve.wait_ge(gates_made, 4 * t + 3)
                nc.vector.tensor_scalar(gates[:, k, :], gated[:, k, :], inverse[:, k:k + 1], 2.0, ALU.mult, ALU.mult).then_inc(gates_made, 1)

            def gate_ranks(t):
                dve.wait_ge(gates_made, 4 * t + 4)
                dve.wait_ge(ranks_made, t + 1)
                if t >= 2:
                    dve.wait_ge(turned, 2 * (t - 1))
                for half in range(2):
                    n = EXPERTS // 2
                    nc.vector.tensor_tensor(
                        ranks[:, t % 2, half * 512:(half + 1) * 512].rearrange("p (k r) -> p k r", r=RANK),
                        ps_rank[:, t % 2, half, :].rearrange("p (k r) -> p k r", r=RANK),
                        gates[:, t % 2, half * n:(half + 1) * n].unsqueeze(2).to_broadcast((P, n, RANK)),
                        ALU.mult).then_inc(ranks_gated, 1)

            norm.vector(dve)
            for i in range(5):
                split_lo(i)
            pick(0)
            gate_ranks(0)
            for t in range(NT):
                if t + 1 < NT:
                    pick(t + 1)
                for half in range(2):
                    dve.wait_ge(turned_hi, 2 * t + half + 1)
                    nc.vector.tensor_tensor(ranksT[1][:, t % 2, 4 * half:4 * half + 4, :],
                                            ps_turn[:, half, :].rearrange("p (k n) -> p k n", k=4),
                                            ranksT[0][:, t % 2, 4 * half:4 * half + 4, :].bitcast(F32),
                                            ALU.subtract).then_inc(turned_split, 1)
                if t + 1 < NT:
                    gate_ranks(t + 1)
                dve.wait_ge(out_made, t + 1)
                nc.vector.tensor_tensor(m.x[:, t, :], ps_out[:], m.x[:, t, :], ALU.add).then_inc(added, 1)

        @block.scalar
        def _(act):
            def split_hi(i):
                src, (hi, _), at, landed = pieces[i]
                act.wait_ge(landed, 16)
                nc.scalar.copy(hi[:, at], src).then_inc(weights_hi, 1)

            def exponent(t):
                act.wait_ge(picked, 5 * t + 3)
                if t >= 2:
                    act.wait_ge(gates_made, 4 * (t - 1))
                nc.scalar.activation(expd[:, t % 2, :], scores[:, t % 2, :], ACT.Exp, bias=lowest[:, t % 2:t % 2 + 1]).then_inc(exp_done, 1)

            norm.scalar(act)
            for i in range(3):
                split_hi(i)
            for half in range(2):
                act.wait_ge(scoresT_made, half + 1)
                nc.scalar.copy(scoresT[:, half * 512:(half + 1) * 512], ps_rank[0:EXPERTS, 1, half, :]).then_inc(scoresT_copied, 1)
            for i in range(3, 5):
                split_hi(i)
            exponent(0)
            for t in range(NT):
                if t + 1 < NT:
                    exponent(t + 1)
                for half in range(2):
                    act.wait_ge(turned, 2 * t + half + 1)
                    if t >= 2:
                        act.wait_ge(out_made, t - 1)
                    nc.scalar.copy(ranksT[0][:, t % 2, 4 * half:4 * half + 4, :],
                                   ps_turn[:, half, :].rearrange("p (k n) -> p k n", k=4)).then_inc(turned_hi, 1)


def program(nc, dram, out):
    with ExitStack() as ctx:
        def sb(what, shape, dt=F32):
            return ctx.enter_context(nc.sbuf_tensor(what, shape, dt))

        m = Model(dram=dram, x=sb("x", [P, NT, D]), ident=sb("ident", [P, P]),
                  xT_hi=sb("xT_hi", [P, DC, TOK], F32R), xT_lo=sb("xT_lo", [P, DC, TOK], F32R),
                  ident_in=ctx.enter_context(nc.semaphore("ident_in")),
                  ln_loaded=[ctx.enter_context(nc.semaphore(f"ln_loaded{t}")) for t in range(NT)],
                  ln_semaphores=[ctx.enter_context(nc.semaphore(f"ln_{what}")) for what in LN_SEMAPHORES],
                  stats=sb("stats", [P, NT, 6]), moments=sb("moments", [P, NT, 2]))
        attention0_phase(nc, m)
        ffn0_phase(nc, m)
        attention1_phase(nc, m)
        moe_phase(nc, m, out)



def shape_constants():
    f = np.float32
    pos = np.arange(SEQ, dtype=f)
    inv_freq = (f(1.0) / f(10000.0) ** (np.arange(0, HD0, 2, dtype=f) / f(HD0))).astype(f)
    angle = np.concatenate([(pos[:, None] * inv_freq[None, :]).astype(f)] * 2, axis=1).T
    cos, sin = np.cos(angle).astype(f), np.sin(angle).astype(f)
    sin[HD0 // 2:] *= f(-1.0)
    scale = np.where(pos < SYS_LEN, f(0.5), np.where(pos < SYS_LEN + IMG_LEN, f(1.5), f(1.0))).astype(f)
    unscale = np.ones((P, P), f)
    unscale[:SYS_LEN + IMG_LEN] = (f(1.0) / scale[:P])[None, :]
    row, col = np.arange(P)[:, None], np.arange(P)[None, :]
    causal = np.zeros((P, SEQ), f)
    causal[:, SEQ - P:] = np.where(row >= col, f(0.0), f(MASKED))
    slopes = f(1.0) / f(2.0) ** (np.arange(1, HEADS1 + 1, dtype=f) * f(8.0 / HEADS1))
    slope = (slopes[:, None] * (pos - f(SEQ - 1))[None, :]).astype(f) * f(HD1 ** 0.5)
    slope_hi = (slope.view(np.uint32) + np.uint32(0x800) & np.uint32(0xFFFFF000)).view(f)
    slopes = np.zeros((CHUNKS1, 32, PAIRS, SEQ), f)
    pick = np.zeros((32, BATCH, PAIRS, 2, SEQ), f)
    for head in range(2):
        of_head = slope.reshape(CHUNKS1, PAIRS, 2, SEQ)[:, :, head], slope_hi.reshape(CHUNKS1, PAIRS, 2, SEQ)[:, :, head]
        slopes[:, 2 * head], slopes[:, 2 * head + 1] = of_head[1], of_head[0] - of_head[1]
        pick[2 * head:2 * head + 2, :, :, head] = f(1.0)
    return {"cos_q": cos, "sin_q": sin, "cos_k": cos * scale, "sin_k": sin * scale, "unscale": unscale,
            "causal": causal, "ident": np.eye(P, dtype=f), "slope": slopes.reshape(CHUNKS1, 32, PAIRS * SEQ),
            "pick": pick.reshape(32, BATCH * PAIRS * 2 * SEQ)}


def columns(w, n):
    return w.reshape(-1, n, DC, P).transpose(0, 3, 2, 1).reshape(-1, P, DC * n)


def lay_out(i):
    i = {k: np.asarray(v) for k, v in i.items()}
    w_qkv = columns(i["L1_attn_w_qkv"], P)
    return {
        "x": i["L0_attn_hidden_states"].reshape(TOK, D),
        "wq": columns(i["L0_attn_wq"], HD0).reshape(KV0, PER_KV, P, DC * HD0),
        "wk": columns(i["L0_attn_wk"], HD0),
        "wv": columns(i["L0_attn_wv"], HD0),
        "wo": i["L0_attn_wo"].T.reshape(KV0, PER_KV, HD0, D),
        "gate": columns(i["L0_ffn_gate_t"], P),
        "up": columns(i["L0_ffn_up_t"], P),
        "down": i["L0_ffn_down_t"].T.reshape(FC, P, D),
        "gate_s": i["L0_ffn_gate_s"].reshape(FC, P).T,
        "up_s": i["L0_ffn_up_s"].reshape(FC, P).T,
        "down_s": i["L0_ffn_down_s"].reshape(1, D),
        "wq1": w_qkv[0:4], "wk1": w_qkv[4:8], "wv1": w_qkv[8:12],
        "bias1": i["L1_attn_b_qkv"].reshape(3, CHUNKS1, P).transpose(2, 0, 1),
        "wo1": i["L1_attn_w_out"].T.reshape(CHUNKS1, P, D),
        "out_bias": i["L1_attn_b_out"].reshape(1, D),
        "router": i["L1_ffn_Wr"].T.reshape(DC, P, EXPERTS).transpose(1, 0, 2),
        "down1": i["L1_ffn_A"].reshape(KR, D).T.reshape(DC, P, KR).transpose(1, 0, 2),
        "up1": i["L1_ffn_B"].transpose(0, 2, 1).reshape(KR // P, P, D).transpose(1, 0, 2),
    }


def kernel(**inputs):
    import concourse.bacc as bacc
    from concourse.bass_utils import run_bass_kernel_spmd

    nc = bacc.Bacc("TRN2", target_bir_lowering=False, num_devices=1)
    arrays, dram = {}, {}
    for name, a in {**lay_out(inputs), **shape_constants()}.items():
        arrays[f"in_{name}"] = np.ascontiguousarray(a)
        dram[name] = nc.dram_tensor(f"in_{name}", a.shape, mybir.dt.from_np(a.dtype), kind="ExternalInput").ap()
    out = nc.dram_tensor("out", (TOK, D), F32, kind="ExternalOutput").ap()
    program(nc, dram, out)
    result = run_bass_kernel_spmd(nc, [arrays], core_ids=[0])
    return result.results[0]["out"].reshape(BATCH, SEQ, D)
```
